# Optimizing a Trainium2 kernel written in Bass

```python
import numpy as np
import jax
import jax.numpy as jnp

def _softmax(x, axis=-1):
    return jax.nn.softmax(x, axis=axis)

def _gelu(x):
    return jax.nn.gelu(x, approximate=True)

def _silu(x):
    return jax.nn.silu(x)

def _sigmoid(x):
    return jax.nn.sigmoid(x)

def _layernorm(x, axis=-1, eps=1e-05):
    m = jnp.mean(x, axis=axis, keepdims=True)
    v = jnp.var(x, axis=axis, keepdims=True)
    return (x - m) / jnp.sqrt(v + eps)

def _scatter_add(tgt, idx, src, axis=0):
    return tgt.at[idx].add(src)

def _segment_sum(src, seg, n):
    return jax.ops.segment_sum(src, seg, n)
kernel_name = 'mk_decoder_postln_d1_seqx_r4_57877d'

def setup_inputs(seed: int=0):
    np.random.seed(seed)
    _w = jnp.asarray

    def _rec_inputs():
        import jax
        import jax.numpy as jnp
        _rk = jax.random.key(seed)
        x = 4.136e-05 + 0.9999 * jax.random.normal(jax.random.fold_in(_rk, 1), (4, 1024, 256), jnp.float32)
        _lenS = 1024 - jax.random.randint(jax.random.fold_in(_rk, 7), (4,), 0, max(1, 1024 // 4) + 1, jnp.int32)
        _lenS2 = 77 - jax.random.randint(jax.random.fold_in(_rk, 8), (4,), 0, max(1, 77 // 4) + 1, jnp.int32)
        _ctx_2048P = jax.random.normal(jax.random.fold_in(_rk, 11), (4, 16, 512), jnp.float32)
        _ctx_2048c = jax.random.dirichlet(jax.random.fold_in(_rk, 511), 0.3 * jnp.ones((16,), jnp.float32), (4, 77))
        _ctx_2048t = jnp.einsum('bsk,bkd->bsd', _ctx_2048c, _ctx_2048P)
        _ctx_2048t = _ctx_2048t * jax.lax.rsqrt(jnp.mean(jnp.square(_ctx_2048t)) + 1e-12) * 0.953939
        ctx_2048 = -0.000392918 + 0.999932 * (_ctx_2048t + 0.3 * jax.random.normal(jax.random.fold_in(_rk, 611), (4, 77, 512), jnp.float32))
        _validS = jnp.arange(1024)[None, :] < _lenS[:, None]
        _validS2 = jnp.arange(77)[None, :] < _lenS2[:, None]
        _causal = jnp.tril(jnp.ones((1024, 1024), dtype=bool))
        mask_BxS2_ik0 = jnp.where(jnp.broadcast_to(_validS2[:, :], (4, 77)), 0, 1).astype(jnp.int32)
        return (x, ctx_2048, mask_BxS2_ik0)
    x, ctx_2048, mask_BxS2_ik0 = _rec_inputs()

    def _L0_attn_setup():
        import jax, jax.numpy as jnp
        import numpy as np
        B, N, C, H = (4, 2048, 256, 16)
        D = C // H
        EPS = 1e-05
        key = jax.random.key(seed)
        ks = jax.random.split(key, 10)
        s = 1.0 / np.sqrt(C)
        return {'x': jax.random.normal(ks[0], (B, N, C), jnp.float32), 'Wq': jax.random.uniform(ks[1], (C, C), jnp.float32, -s, s), 'bq': jax.random.uniform(ks[2], (C,), jnp.float32, -s, s), 'Wk': jax.random.uniform(ks[3], (C, C), jnp.float32, -s, s), 'bk': jax.random.uniform(ks[4], (C,), jnp.float32, -s, s), 'Wv': jax.random.uniform(ks[5], (C, C), jnp.float32, -s, s), 'bv': jax.random.uniform(ks[6], (C,), jnp.float32, -s, s), 'Wo': jax.random.uniform(ks[7], (C, C), jnp.float32, -s, s), 'bo': jax.random.uniform(ks[8], (C,), jnp.float32, -s, s), 'ln_g': jnp.ones((C,), jnp.float32), 'ln_b': jnp.zeros((C,), jnp.float32)}
    _L0_attn_all = _L0_attn_setup()
    _L0_attn_in = {k: v for k, v in _L0_attn_all.items() if k in ('Wq', 'bq', 'Wk', 'bk', 'Wv', 'bv', 'Wo', 'bo', 'ln_g', 'ln_b')}
    del _L0_attn_all

    def _L0_xattn_setup():
        import jax, jax.numpy as jnp
        import numpy as np
        UNITS = 256
        NUM_HEADS = 8

        def _split_heads(x, n):
            B, S, D = x.shape
            return x.reshape(B, S, n, D // n).transpose(0, 2, 1, 3)
        key = jax.random.key(seed)
        k1, k2, k3 = jax.random.split(key, 3)
        B, S = (8, 256)
        memory = jax.random.normal(k1, (B, S, 2 * UNITS), dtype=jnp.float32)
        query = jax.random.normal(k2, (B, S, UNITS), dtype=jnp.float32)
        seq_mask = jax.random.randint(k3, (B, S), 0, 2, dtype=jnp.int32)
        b = jnp.zeros((1,), dtype=jnp.float32)
        return {'memory': memory, 'query': query, 'seq_mask': seq_mask, 'b': b}
    _L0_xattn_all = _L0_xattn_setup()
    _L0_xattn_in = {k: v for k, v in _L0_xattn_all.items() if k in ('b',)}
    del _L0_xattn_all

    def _L0_ffn_setup():
        import jax, jax.numpy as jnp
        import numpy as np
        B, S, D = (2, 1024, 256)
        H = 1024
        E = 8
        K = 4
        key = jax.random.key(seed)
        kx, kr, ku, kd = jax.random.split(key, 4)
        x = jax.random.normal(kx, (B, S, D), dtype=jnp.float32)
        router_w = jax.random.normal(kr, (D, E), dtype=jnp.float32) / np.sqrt(D)
        up_w = jax.random.normal(ku, (E, D, H), dtype=jnp.float32) / np.sqrt(D)
        down_w = jax.random.normal(kd, (E, H, D), dtype=jnp.float32) / np.sqrt(H)
        return {'x': x, 'router_w': router_w, 'up_w': up_w, 'down_w': down_w}
    _L0_ffn_all = _L0_ffn_setup()
    _L0_ffn_in = {k: v for k, v in _L0_ffn_all.items() if k in ('router_w', 'up_w', 'down_w')}
    del _L0_ffn_all
    return {'x': x, 'ctx_2048': ctx_2048, 'mask_BxS2_ik0': mask_BxS2_ik0, 'L0_attn_Wq': _L0_attn_in['Wq'], 'L0_attn_bq': _L0_attn_in['bq'], 'L0_attn_Wk': _L0_attn_in['Wk'], 'L0_attn_bk': _L0_attn_in['bk'], 'L0_attn_Wv': _L0_attn_in['Wv'], 'L0_attn_bv': _L0_attn_in['bv'], 'L0_attn_Wo': _L0_attn_in['Wo'], 'L0_attn_bo': _L0_attn_in['bo'], 'L0_attn_ln_g': _L0_attn_in['ln_g'], 'L0_attn_ln_b': _L0_attn_in['ln_b'], 'L0_xattn_b': _L0_xattn_in['b'], 'L0_ffn_router_w': _L0_ffn_in['router_w'], 'L0_ffn_up_w': _L0_ffn_in['up_w'], 'L0_ffn_down_w': _L0_ffn_in['down_w']}

def reference(x, ctx_2048, mask_BxS2_ik0, L0_attn_Wq, L0_attn_bq, L0_attn_Wk, L0_attn_bk, L0_attn_Wv, L0_attn_bv, L0_attn_Wo, L0_attn_bo, L0_attn_ln_g, L0_attn_ln_b, L0_xattn_b, L0_ffn_router_w, L0_ffn_up_w, L0_ffn_down_w):
    import jax
    import jax.numpy as jnp

    def _L0_attn_ref(x, Wq, bq, Wk, bk, Wv, bv, Wo, bo, ln_g, ln_b):
        import jax, jax.numpy as jnp
        import numpy as np
        B, N, C, H = (4, 2048, 256, 16)
        D = C // H
        EPS = 1e-05
        b, n, c = x.shape
        q = x @ Wq.T + bq
        k = x @ Wk.T + bk
        v = x @ Wv.T + bv
        split = lambda z: z.reshape(b, n, H, D).transpose(0, 2, 1, 3)
        q, k, v = (split(q), split(k), split(v))
        q = jax.nn.softmax(q, axis=-1)
        k = jax.nn.softmax(k, axis=-2)
        state = jnp.einsum('bhnd,bhne->bhde', k, v)
        out = jnp.einsum('bhnd,bhde->bhne', q, state)
        out = out.transpose(0, 2, 1, 3).reshape(b, n, c)
        mu = out.mean(-1, keepdims=True)
        var = out.var(-1, keepdims=True)
        out = (out - mu) * jax.lax.rsqrt(var + EPS) * ln_g + ln_b
        return out @ Wo.T + bo

    def _L0_xattn_ref(memory, query, seq_mask, b):
        import jax, jax.numpy as jnp
        import numpy as np
        UNITS = 256
        NUM_HEADS = 8

        def _split_heads(x, n):
            B, S, D = x.shape
            return x.reshape(B, S, n, D // n).transpose(0, 2, 1, 3)
        H = NUM_HEADS
        depth = UNITS // H
        Q = _split_heads(query, H) * depth ** (-0.5)
        k_mem, v_mem = jnp.split(memory, 2, axis=2)
        K = _split_heads(k_mem, H)
        V = _split_heads(v_mem, H)
        logits = jnp.einsum('bhqd,bhkd->bhqk', Q, K) + b[0]
        mask = seq_mask.astype(jnp.float32)[:, None, None, :]
        logits = logits + -1e+30 * (1.0 - mask)
        weights = jax.nn.softmax(logits, axis=-1)
        out = jnp.einsum('bhqk,bhkd->bhqd', weights, V)
        B, _, S, _ = out.shape
        return out.transpose(0, 2, 1, 3).reshape(B, S, UNITS)

    def _L0_ffn_ref(x, router_w, up_w, down_w):
        import jax, jax.numpy as jnp
        import numpy as np
        B, S, D = (2, 1024, 256)
        H = 1024
        E = 8
        K = 4
        router_logits = jnp.einsum('bsd,de->bse', x, router_w)
        routing_weights = jax.nn.softmax(router_logits, axis=-1)
        topk_weights, topk_indices = jax.lax.top_k(routing_weights, K)
        topk_weights = topk_weights / jnp.sum(topk_weights, axis=-1, keepdims=True)
        h = jnp.einsum('bsd,edh->bseh', x, up_w)
        h = jax.nn.gelu(h)
        expert_outputs = jnp.einsum('bseh,ehd->bsed', h, down_w)
        gathered = jnp.take_along_axis(expert_outputs, topk_indices[:, :, :, None], axis=2)
        output = jnp.sum(topk_weights[:, :, :, None] * gathered, axis=2)
        return output
    x = _layernorm(x + _L0_attn_ref(x, L0_attn_Wq, L0_attn_bq, L0_attn_Wk, L0_attn_bk, L0_attn_Wv, L0_attn_bv, L0_attn_Wo, L0_attn_bo, L0_attn_ln_g, L0_attn_ln_b), axis=-1)
    x = _layernorm(x + _L0_xattn_ref(ctx_2048, x, mask_BxS2_ik0, L0_xattn_b), axis=-1)
    x = _layernorm(x + _L0_ffn_ref(x, L0_ffn_router_w, L0_ffn_up_w, L0_ffn_down_w), axis=-1)
    return x

_drawn_inputs = setup_inputs


def setup_inputs(seed=0):
    import zlib

    import numpy as np

    out = dict(_drawn_inputs(seed))
    spreads = {'L0_attn_ln_g': (1.0, 0.2), 'L0_attn_ln_b': (0.0, 0.1)}
    factors = {'L0_attn_bq': 8.0, 'L0_attn_bk': 8.0}
    for name, (base, spread) in spreads.items():
        noise = np.random.default_rng([zlib.crc32(name.encode()), seed]).standard_normal(out[name].shape)
        drawn = base * np.exp(spread * noise) if base else spread * noise
        out[name] = jnp.asarray(drawn.astype(out[name].dtype))
    for name, factor in factors.items():
        out[name] = (out[name] * factor).astype(out[name].dtype)
    return out
```

```python
from contextlib import ExitStack

import concourse.bass as bass
from concourse import mybir

F32 = mybir.dt.float32
F16 = mybir.dt.float16
BF16 = mybir.dt.bfloat16
I32 = mybir.dt.int32
ALU = mybir.AluOpType
ACT = mybir.ActivationFunctionType
AX_X = mybir.AxisListType.X
ABSMAX = bass.bass_isa.ReduceOp.absmax

P = 128
B, N, C = 4, 1024, 256
CC = C // P
TB = N // P
NT = B * TB
LH, LD = 16, 16
HPC = P // LD
XH, XD = 8, 32
XPC = P // XD
KEYS = 77
CTX = 2 * C
EXP, TOPK, HID = 8, 4, 1024
HC = HID // P
SLOTS = 256
SB = SLOTS // P
ETILES = (TOPK * B * N + EXP * (SLOTS - 1)) // SLOTS
EBLOCKS = ETILES * SB
PAIRS = HC // 2
TRASH = SB * P
ROWS = B * N + TRASH
ROW = 2 * C + 2 * EXP
LN_EPS = 1e-5
MASKED = -1e30
XSCALE = 64.0
WTARGET = 64.0
LOGIT0 = 1024 - 512 - XPC * KEYS
CONST_STEPS = 17
PIECES = 4
EXPONENT = 0x7F800000

TRANS_SETUP = 4 * CC
TRANS_BATCH = 5 * TB
SMALL_SETUP = CC
SMALL_BATCH = CC + 2 + CC + 4 * TB


def layer_kernel(nc, x, ctx, mask, Wq, bq, Wk, bk, Wv, bv, Wo, bo, ln_g, ln_b, xb, router, up, down, out):
    rows = nc.dram_tensor("token_rows", [ROWS, ROW // 2], F32, kind="Internal").ap()
    acc = nc.dram_tensor("token_sums", [ROWS, C], F32, kind="Internal").ap()
    with ExitStack() as all_:
        def keep(name, shape, dt):
            return all_.enter_context(nc.sbuf_tensor(name, shape, dt))

        k = {
            "wu": keep("w_up", [P, EXP, 2, CC, HID], F16),
            "wd": keep("w_down", [P, EXP, 2, HC, C], F16),
            "wpow": keep("w_pow", [P, 2 * EXP], F32),
            "rank": keep("rank", [P, EXP, NT], F32),
            "ident": keep("ident", [P, P], F32),
            "ones": keep("ones", [P, P], F32),
            "nhalf": keep("nhalf", [P, TB], F32),
        }
        attention(nc, k, rows, acc, x, ctx, mask, Wq, bq, Wk, bk, Wv, bv, Wo, bo, ln_g, ln_b, xb, router, up, down)
        with ExitStack() as plan:
            def tab(name, shape, dt):
                return plan.enter_context(nc.sbuf_tensor(name, shape, dt))

            k["slot_row"] = tab("slot_row", [P, EBLOCKS], I32)
            k["tile_expert"] = tab("tile_expert", [P, ETILES], I32)
            k["pick"] = tab("pick", [P, ETILES, EXP], F32)
            k["up_scale"] = tab("up_scale", [P, ETILES], F32)
            k["h_scale"] = tab("h_scale", [P, ETILES], F32)
            k["ident16"] = tab("ident16", [P, P], F16)
            routing(nc, k)
            experts(nc, k, rows, acc)
        last_norm(nc, k, acc, out)


def attention(nc, k, rows, acc, x, ctx, mask, Wq, bq, Wk, bk, Wv, bv, Wo, bo, ln_g, ln_b, xb, router, up, down):
    st = ExitStack()
    with st:
        def sb(name, shape, dt=F32):
            return st.enter_context(nc.sbuf_tensor(name, shape, dt))

        def ps(name, shape, dt=F32):
            return st.enter_context(nc.psum_tensor(name, shape, dt))

        def sem(name):
            return st.enter_context(nc.semaphore(name))

        ident, ones, nhalf = k["ident"], k["ones"], k["nhalf"]
        X = sb("X", [P, TB, C])
        Q = sb("Q", [P, TB, C])
        KZ = sb("KZ", [P, TB * (ROW // 2)])
        V = sb("V", [P, TB, CC, P + 1])
        K = KZ[:, 0:TB * C].rearrange("p (t c) -> p t c", c=C)
        XR = KZ[:, :].bitcast(F16).rearrange("p (t r) -> p t r", r=ROW)
        W8 = sb("W8", [P, 2048])
        wqkv = sb("wqkv", [P, CC, 3 * C])
        woT = sb("woT", [P, CC, C])
        bias = sb("bias", [P, 3 * C])
        cvec = sb("cvec", [P, C])
        tT = sb("tT", [P, 2, CC, P])
        kbd = sb("kbd", [P, CC, XPC, KEYS])
        hsel = sb("hsel", [P, XPC])
        bsel = sb("bsel", [P, HPC])
        state = sb("state", [P, CC, P + HPC])
        ctx_sb = sb("ctx_sb", [KEYS, CTX])
        vx = sb("vx", [KEYS, XH, XD + 1])
        mint = sb("mint", [1, KEYS], I32)
        mrow = sb("mrow", [1, KEYS])
        mbf = sb("mbf", [1, XPC, KEYS], BF16)
        one16 = sb("one16", [1, P], BF16)
        pr = sb("pr", [P, 2, XH, KEYS])
        pT = sb("pT", [P, 2, XH, P])
        rw = sb("rw", [P, CC, EXP])
        gb = sb("gb", [P, 2, CC])
        bcol = sb("bcol", [P, 1])
        kmx = pT[:, 1, 0:CC, :].rearrange("p c t -> p (c t)")
        kdiag = pT[:, 0, 0:CC, :]
        km2 = sb("km2", [P, CC])
        qm = sb("qm", [P, 2, LH])
        rden = sb("rden", [P, 2, LH])
        rst = sb("rst", [P, CC])
        stat = sb("stat", [P, 2, 6])
        mv = sb("mv", [P, 3, TB, 2])
        ve = sb("ve", [P, 3, TB])
        rstd = sb("rstd", [P, 3, TB])
        xm = sb("xm", [P, 2, XH])
        xmb = sb("xmb", [P, 2, XH])
        xr8 = sb("xr8", [P, 2, XH])
        L = sb("L", [P, TB, EXP])
        lm = sb("lm", [P, TB])
        le = sb("le", [P, TB, EXP])
        both = pr[:, :, :, :].rearrange("p r h k -> p (r h k)")[:, 0:2 * TB * EXP * EXP].rearrange(
            "p (r t e j) -> p r t e j", r=2, t=TB, e=EXP)
        cmpa, cmpb = both[:, 0], both[:, 1]
        lower = sb("lower", [P, EXP, EXP])
        rk = sb("rk", [P, TB, EXP])
        gsum = sb("gsum", [P, 2, TB])
        wmx = sb("wmx", [P, 1])
        wall = sb("wall", [P, 1])
        wcl = sb("wcl", [P, 1])
        wrp = sb("wrp", [P, 1])
        wsc = sb("wsc", [P, 1])

        trans = [ps(f"trans{i}", [P, CC, P]) for i in range(2)]
        small = [ps(f"small{i}", [P, 512]) for i in range(2)]
        big = [ps(f"big{i}", [P, 1024]) for i in range(2)]

        w_nat = X[:, :, :].rearrange("p (w o) c -> p w o c", w=4)
        zero16 = KZ[:, 0:ROW // 2]
        zero32 = K[:, 2, :]

        setup_loaded, setup_loaded2 = sem("setup_loaded"), sem("setup_loaded2")
        consts, zeros_ready = sem("consts"), sem("zeros_ready")
        x_loaded, ctx_loaded, mask_loaded, w_loaded = sem("x_loaded"), sem("ctx_loaded"), sem("mask_loaded"), sem("w_loaded")
        rows_stored, acc_stored = sem("rows_stored"), sem("acc_stored")
        trans_ready, trans_copied = sem("trans_ready"), sem("trans_copied")
        small_ready, small_free = sem("small_ready"), sem("small_free")
        lnbb_ready, woT_ready = sem("lnbb_ready"), sem("woT_ready")
        vx_ready, mask_ready, pool_step = sem("vx_ready"), sem("mask_ready"), sem("pool_step")
        qkv_ready, qk_ready, v_ready = sem("qkv_ready"), sem("qk_ready"), sem("v_ready")
        qm_ready, qs_ready, qe_ready, kmx_ready = sem("qm_ready"), sem("qs_ready"), sem("qe_ready"), sem("kmx_ready")
        km2_ready, kdiag_ready, ks_ready, ke_ready = sem("km2_ready"), sem("kdiag_ready"), sem("ks_ready"), sem("ke_ready")
        rst_ready = sem("rst_ready")
        rden_ready, o_ready = sem("rden_ready"), sem("o_ready")
        xc_ready = sem("xc_ready")
        stat_ready, mv_ready, ve_ready, rstd_ready = sem("stat_ready"), sem("mv_ready"), sem("ve_ready"), sem("rstd_ready")
        z_ready, x1_ready = sem("z_ready"), sem("x1_ready")
        lg_ready, xm_ready, xmb_ready, s_ready, p_ready = sem("lg_ready"), sem("xm_ready"), sem("xmb_ready"), sem("s_ready"), sem("p_ready")
        pT_ready, pT_copied = sem("pT_ready"), sem("pT_copied")
        xr8_ready, r2_ready, x2_ready = sem("xr8_ready"), sem("r2_ready"), sem("x2_ready")
        hi_ready, lo_ready = sem("hi_ready"), sem("lo_ready")
        L_ready, route_step, le_shift, le_ready, gates_ready = sem("L_ready"), sem("route_step"), sem("le_shift"), sem("le_ready"), sem("gates_ready")
        wmx_ready, wall_ready, wstep, wsc_ready, whi_ready, w_split = (
            sem("wmx_ready"), sem("wall_ready"), sem("wstep"), sem("wsc_ready"), sem("whi_ready"), sem("w_split"))

        passed = {e: sem(f"passed_{i}") for i, e in enumerate((nc.gpsimd, nc.scalar, nc.vector))}

        x_in = x.rearrange("b (t p) c -> b p t c", p=P)
        rows_out = rows[0:B * N, :].rearrange("(b t p) r -> b p t r", p=P, t=TB)
        acc_out = acc[0:B * N, :].rearrange("(b t p) c -> b p t c", p=P, t=TB)
        up_in = up.rearrange("e (c p) h -> e p c h", p=P)
        down_in = down.rearrange("e (c p) d -> e p c d", p=P)

        def lone(eng):
            eng.sem_inc(passed[eng], 1)

        def one(ap, b):
            a = ap[bass.ds(b, 1)]
            return a.squeeze(0)

        block = st.enter_context(nc.Block())

        @block.sync
        def _(sp):
            for w, mat in enumerate((Wq, Wk, Wv, Wo)):
                sp.dma_start(w_nat[:, w, :, :], mat.rearrange("(o p) c -> p o c", p=P)).then_inc(setup_loaded, 16)
            for w, vec in enumerate((bq, bk, bv)):
                sp.dma_start(bias[:, w * C:(w + 1) * C], vec.partition_broadcast(P)).then_inc(setup_loaded2, 16)
            sp.dma_start(cvec[:, :], bo.partition_broadcast(P)).then_inc(setup_loaded2, 16)
            sp.dma_start(bcol[:, :], xb.partition_broadcast(P)).then_inc(setup_loaded2, 16)
            sp.dma_start(gb[:, 0, :], ln_g.rearrange("(c p) -> p c", p=P), allow_slow_non_contiguous=True).then_inc(setup_loaded2, 16)
            sp.dma_start(gb[:, 1, :], ln_b.rearrange("(c p) -> p c", p=P), allow_slow_non_contiguous=True).then_inc(setup_loaded2, 16)
            sp.dma_start(rw[:, :, :], router.rearrange("(c p) e -> p c e", p=P)).then_inc(setup_loaded2, 16)
            sp.dma_start(ctx_sb[:, :], ctx[0]).then_inc(ctx_loaded, 16)
            sp.dma_start(mint[:, :], mask[0:1, :]).then_inc(mask_loaded, 16)
            sp.dma_start(W8[:, :].rearrange("p (c h) -> p c h", c=CC), up_in[0]).then_inc(w_loaded, 16)
            sp.wait_ge(zeros_ready, 2)
            for j in range(SB):
                sp.dma_start(rows[B * N + j * P:B * N + (j + 1) * P, :], zero16).then_inc(rows_stored, 16)
                sp.dma_start(acc[B * N + j * P:B * N + (j + 1) * P, :], zero32).then_inc(acc_stored, 16)
            sp.wait_ge(trans_ready, TRANS_SETUP)
            sp.dma_start(X[:, :, :], x_in[0]).then_inc(x_loaded, 16)

            def next_piece(b, q):
                sp.wait_ge(w_split, PIECES * b + (q + 1))
                e, src = 2 * b + (q + 1) // 2, (up_in, down_in)[(q + 1) % 2]
                piece = one(src, e) if not isinstance(e, int) else src[e]
                sp.dma_start(W8[:, :].rearrange("p (c h) -> p c h", c=piece.shape[1]), piece).then_inc(w_loaded, 16)

            def store(b):
                sp.wait_ge(x2_ready, TB * b + TB)
                sp.dma_start(acc_out[b] if isinstance(b, int) else one(acc_out, b), Q[:, :, :]).then_inc(acc_stored, 16)
                sp.wait_ge(hi_ready, TB * b + TB)
                sp.wait_ge(lo_ready, TB * b + TB)
                sp.wait_ge(gates_ready, b + 1)
                sp.dma_start(rows_out[b] if isinstance(b, int) else one(rows_out, b),
                             KZ[:, :].rearrange("p (t r) -> p t r", t=TB)).then_inc(rows_stored, 16)

            with sp.Fori(0, B - 1) as b:
                for q in range(PIECES):
                    next_piece(b, q)
                sp.wait_ge(small_free, SMALL_SETUP + SMALL_BATCH * b + 2 * CC + 2 + 2 * TB)
                sp.dma_start(X[:, :, :], one(x_in, b + 1)).then_inc(x_loaded, 16)
                sp.wait_ge(vx_ready, b + 1)
                sp.dma_start(ctx_sb[:, :], one(ctx, b + 1)).then_inc(ctx_loaded, 16)
                sp.wait_ge(mask_ready, b + 1)
                sp.dma_start(mint[:, :], mask[bass.ds(b + 1, 1), :]).then_inc(mask_loaded, 16)
                store(b)
            for q in range(PIECES - 1):
                next_piece(B - 1, q)
            store(B - 1)
            sp.wait_ge(acc_stored, 16 * (SB + B))
            sp.wait_ge(rows_stored, 16 * (SB + B))

        @block.gpsimd
        def _(pool):
            steps = [0]

            def done(ins):
                steps[0] += 1
                ins.then_inc(consts, 1)
                pool.wait_ge(consts, steps[0])

            done(pool.memset(ident[:, :], 0.0))
            done(pool.affine_select(out=ident[:, :], in_=ident[:, :], compare_op=ALU.not_equal, fill=1.0,
                                    base=0, pattern=[[-1, P]], channel_multiplier=1))
            done(pool.memset(ones[:, :], 1.0))
            pool.memset(zero16, 0.0).then_inc(zeros_ready, 1)
            pool.memset(zero32, 0.0).then_inc(zeros_ready, 1)
            done(pool.memset(nhalf[:, :], -0.5))
            done(pool.memset(one16[:, :], 1.0))
            done(pool.memset(V[:, :, :, P:P + 1], 1.0))
            done(pool.memset(vx[:, :, XD:XD + 1], 1.0))
            for tile, heads, d in ((hsel, XPC, XD), (bsel, HPC, LD)):
                done(pool.memset(tile[:, :], 1.0))
                done(pool.affine_select(out=tile[:, :], in_=tile[:, :], compare_op=ALU.is_ge, fill=0.0,
                                        base=0, pattern=[[-d, heads]], channel_multiplier=1))
                done(pool.affine_select(out=tile[:, :], in_=tile[:, :], compare_op=ALU.is_ge, fill=0.0,
                                        base=d - 1, pattern=[[d, heads]], channel_multiplier=-1))
            for c in range(CC):
                done(pool.tensor_copy(state[:, c, P:P + HPC], bsel[:, :]))
            done(pool.memset(lower[:, :, :], 1.0))
            done(pool.affine_select(out=lower[:, :, :], in_=lower[:, :, :], compare_op=ALU.is_gt, fill=0.0,
                                    base=0, pattern=[[1, EXP], [-1, EXP]], channel_multiplier=0))

            assert steps[0] == CONST_STEPS

            def all_max(b, q):
                pool.wait_ge(wmx_ready, PIECES * b + (q + 1))
                lone(pool)
                pool.partition_all_reduce(wall[:, :], wmx[:, :], P, ABSMAX).then_inc(wall_ready, 1)

            def inverse_deviation(b, kind, i):
                n = 3 * TB * b + TB * kind + i + 1
                pool.wait_ge(mv_ready, n)
                lone(pool)
                pool.tensor_scalar(ve[:, kind, i:i + 1], mv[:, kind, i, 1:2], LN_EPS, None, ALU.add).then_inc(ve_ready, 1)
                pool.wait_ge(ve_ready, n)
                pool.tensor_tensor(rstd[:, kind, i:i + 1], ve[:, kind, i:i + 1], nhalf[:, 0:1], ALU.pow).then_inc(rstd_ready, 1)

            with pool.Fori(0, B) as b:
                pool.wait_ge(ctx_loaded, 16 * b + 16)
                lone(pool)
                pool.tensor_copy(vx[:, :, 0:XD], ctx_sb[:, C:CTX].rearrange("k (h d) -> k h d", h=XH)).then_inc(vx_ready, 1)
                pool.wait_ge(mask_loaded, 16 * b + 16)
                lone(pool)
                pool.tensor_scalar(mrow[:, :], mint[:, :], -1.0, 1.0, ALU.mult, ALU.add).then_inc(pool_step, 1)
                pool.wait_ge(pool_step, 1 + b)
                lone(pool)
                for h in range(XPC):
                    ins = pool.tensor_scalar(mbf[:, h, :], mrow[:, :], MASKED, None, ALU.mult)
                ins.then_inc(mask_ready, 1)
                for i in range(TB):
                    if i == 0:
                        pool.wait_ge(small_free, SMALL_SETUP)
                    pool.wait_ge(trans_ready, TRANS_SETUP + TRANS_BATCH * b + i + 1)
                    pool.tensor_tensor(X[:, i, :], X[:, i, :], cvec[:, :], ALU.add).then_inc(xc_ready, 1)
                    if i in (0, 6):
                        all_max(b, i // 6)
                for kind in (0, 1):
                    for i in range(TB):
                        if kind == 1 and i == 0:
                            all_max(b, 2)
                        inverse_deviation(b, kind, i)
                all_max(b, 3)
                for i in range(TB + 1):
                    if i < TB:
                        pool.wait_ge(small_free, SMALL_SETUP + SMALL_BATCH * b + 2 * CC + 2 + 2 * TB + i + 1)
                        pool.tensor_tensor(Q[:, i, :].rearrange("p (c d) -> p c d", c=CC), Q[:, i, :].rearrange("p (c d) -> p c d", c=CC),
                                           V[:, i, :, 0:P], ALU.add).then_inc(r2_ready, 1)
                    if i >= 1:
                        inverse_deviation(b, 2, i - 1)

        @block.scalar
        def _(act):
            for w in range(4):
                for o in range(CC):
                    use = w * CC + o
                    act.wait_ge(trans_ready, use + 1)
                    dst = wqkv[:, :, w * C + o * P:w * C + (o + 1) * P] if w < 3 else woT[:, :, o * P:(o + 1) * P]
                    act.activation(dst, trans[use % 2][:, :, :], ACT.Copy).then_inc(trans_copied, 1)

            def copy_stage(b, stage, i, scale=1.0):
                s = stage * TB + i
                use = TRANS_SETUP + TRANS_BATCH * b + s
                act.wait_ge(trans_ready, use + 1)
                act.activation(tT[:, s % 2, :, :], trans[s % 2][:, :, :], ACT.Copy, scale=scale).then_inc(trans_copied, 1)

            def split_high(b, q):
                act.wait_ge(wsc_ready, PIECES * b + (q + 1))
                wt = (k["wu"], k["wd"])[q % 2]
                dst = wt[:, bass.ds(2 * b + q // 2, 1), 0, :, :].rearrange("p e c h -> p (e c h)")
                lone(act)
                act.activation(dst, W8[:, :], ACT.Copy, scale=wsc[:, 0:1]).then_inc(whi_ready, 1)

            with act.Fori(0, B) as b:
                for i in range(TB + 2):
                    if i < TB:
                        copy_stage(b, 0, i)
                    if i >= 2:
                        act.wait_ge(qs_ready, TB * b + i - 1)
                        act.activation(Q[:, i - 2, :], Q[:, i - 2, :], ACT.Exp).then_inc(qe_ready, 1)
                    if i == 3:
                        split_high(b, 0)
                for g in range(2):
                    if g == 0:
                        act.wait_ge(ks_ready, b + 1)
                    else:
                        act.wait_ge(small_free, SMALL_SETUP + SMALL_BATCH * b + CC + 2)
                    act.activation(K[:, g * 4:g * 4 + 4, :], K[:, g * 4:g * 4 + 4, :], ACT.Exp).then_inc(ke_ready, 1)
                split_high(b, 1)
                for i in range(TB):
                    copy_stage(b, 1, i)
                for i in range(TB):
                    copy_stage(b, 2, i)
                    if i == 4:
                        split_high(b, 2)
                for i in range(TB + 4):
                    if i < TB:
                        copy_stage(b, 3, i, XD ** -0.5)
                    if i == 5:
                        split_high(b, 3)
                    if 2 <= i < TB + 2:
                        act.wait_ge(s_ready, TB * b + i - 1)
                        act.activation(pr[:, (i - 2) % 2, :, :], pr[:, (i - 2) % 2, :, :], ACT.Exp).then_inc(p_ready, 1)
                    j = i - 4
                    if j >= 0:
                        act.wait_ge(pT_ready, TB * b + j + 1)
                        act.activation(pT[0:KEYS, j % 2, :, :].rearrange("k h t -> k (h t)"), big[1][0:KEYS, :], ACT.Copy).then_inc(pT_copied, 1)
                for i in range(TB):
                    copy_stage(b, 4, i)
                    act.activation(XR[:, i, 0:C], Q[:, i, :], ACT.Copy, scale=XSCALE).then_inc(hi_ready, 1)
                act.wait_ge(le_shift, b + 1)
                act.activation(le[:, :, :], le[:, :, :], ACT.Exp).then_inc(le_ready, 1)

        @block.vector
        def _(dve):
            def small_wait(b, s):
                dve.wait_ge(small_ready, SMALL_SETUP + SMALL_BATCH * b + s + 1)
                return small[(SMALL_SETUP + s) % 2]

            dve.wait_ge(setup_loaded2, 16 * 8)
            dve.wait_ge(consts, CONST_STEPS)
            for c in range(CC):
                dve.tensor_scalar(kdiag[:, c, :], ones[:, :], gb[:, 1, c:c + 1], None, ALU.mult).then_inc(lnbb_ready, 1)
            for c in range(CC):
                dve.wait_ge(small_ready, c + 1)
                dve.tensor_tensor(cvec[:, c * P:(c + 1) * P], small[c][:, 0:P], cvec[:, c * P:(c + 1) * P], ALU.add).then_inc(small_free, 1)
            for c in range(CC):
                dve.tensor_scalar(woT[:, c, :], woT[:, c, :], gb[:, 0, c:c + 1], None, ALU.mult).then_inc(woT_ready, 1)

            def abs_max(b, q):
                dve.wait_ge(w_loaded, 16 * (PIECES * b + q + 1))
                dve.tensor_reduce(wmx[:, :], W8[:, :], AX_X, ALU.max, apply_absolute_value=True).then_inc(wmx_ready, 1)

            def scale(b, q):
                n = PIECES * b + q
                at = k["wpow"][:, bass.ds(n, 1)]
                dve.wait_ge(wall_ready, n + 1)
                dve.tensor_scalar(wcl[:, :], wall[:, :], 1e-30, None, ALU.max).then_inc(wstep, 1)
                dve.wait_ge(wstep, 3 * n + 1)
                dve.tensor_scalar(wcl[:, :].bitcast(I32), wcl[:, :].bitcast(I32), EXPONENT, None, ALU.bitwise_and).then_inc(wstep, 1)
                dve.wait_ge(wstep, 3 * n + 2)
                dve.tensor_copy(at, wcl[:, :])
                dve.reciprocal(wrp[:, :], wcl[:, :]).then_inc(wstep, 1)
                dve.wait_ge(wstep, 3 * n + 3)
                dve.tensor_scalar(wsc[:, :], wrp[:, :], WTARGET, None, ALU.mult).then_inc(wsc_ready, 1)

            def split_low(b, q):
                wt = (k["wu"], k["wd"])[q % 2]
                at = wt[:, bass.ds(2 * b + q // 2, 1), :, :, :].rearrange("p e s c h -> p s (e c h)")
                dve.wait_ge(whi_ready, PIECES * b + q + 1)
                dve.scalar_tensor_tensor(out=at[:, 1, :], in0=W8[:, :], scalar=wsc[:, 0:1], in1=at[:, 0, :],
                                         op0=ALU.mult, op1=ALU.subtract).then_inc(w_split, 1)

            def stats(b, kind, i, src):
                n = 3 * TB * b + TB * kind + i
                dve.bn_stats(stat[:, i % 2, :], src).then_inc(stat_ready, 1)
                dve.wait_ge(stat_ready, n + 1)
                lone(dve)
                dve.bn_aggr(mv[:, kind, i, :], stat[:, i % 2, :]).then_inc(mv_ready, 1)

            def norm(b, kind, i, tile, ready):
                dve.wait_ge(rstd_ready, 3 * TB * b + TB * kind + i + 1)
                dve.tensor_scalar(tile, tile, mv[:, kind, i, 0:1], rstd[:, kind, i:i + 1], ALU.subtract, ALU.mult).then_inc(ready, 1)

            with dve.Fori(0, B) as b:
                for c in range(CC):
                    kt = small_wait(b, c)
                    dve.tensor_tensor(kbd[:, c, :, :], kt[:, 0:KEYS].unsqueeze(1).to_broadcast([P, XPC, KEYS]),
                                      hsel[:, :].unsqueeze(2).to_broadcast([P, XPC, KEYS]), ALU.mult).then_inc(small_free, 1)
                dve.wait_ge(rows_stored, 16 * (SB + b))
                dve.wait_ge(acc_stored, 16 * (SB + b))
                for i in range(TB):
                    n = TB * b + i
                    if i in (0, 6):
                        abs_max(b, i // 6)
                    if i == 3:
                        split_low(b, 0)
                    src = big[i % 2]
                    dve.wait_ge(qkv_ready, n + 1)
                    dve.tensor_tensor(Q[:, i, :], src[:, 0:C], bias[:, 0:C], ALU.add).then_inc(qk_ready, 1)
                    dve.tensor_tensor(K[:, i, :], src[:, C:2 * C], bias[:, C:2 * C], ALU.add).then_inc(qk_ready, 1)
                    dve.tensor_tensor(V[:, i, :, 0:P], src[:, 2 * C:3 * C].rearrange("p (c d) -> p c d", c=CC),
                                      bias[:, 2 * C:3 * C].rearrange("p (c d) -> p c d", c=CC), ALU.add).then_inc(v_ready, 1)
                    q3 = Q[:, i, :].rearrange("p (h d) -> p h d", h=LH)
                    dve.wait_ge(qk_ready, 2 * n + 2)
                    dve.tensor_reduce(qm[:, i % 2, :], q3, AX_X, ALU.max).then_inc(qm_ready, 1)
                    if i == 0:
                        dve.tensor_copy(kmx[:, :], K[:, 0, :]).then_inc(kmx_ready, 1)
                    else:
                        dve.wait_ge(kmx_ready, n)
                        dve.tensor_tensor(kmx[:, :], kmx[:, :], K[:, i, :], ALU.max).then_inc(kmx_ready, 1)
                    dve.wait_ge(qm_ready, n + 1)
                    dve.tensor_tensor(q3, q3, qm[:, i % 2, :].unsqueeze(2).to_broadcast([P, LH, LD]), ALU.subtract).then_inc(qs_ready, 1)
                    if i in (1, 7):
                        scale(b, i // 6)
                km = small_wait(b, CC)
                dve.tensor_reduce(km2[:, :], km[:, 0:C].rearrange("p (c t) -> p c t", c=CC), AX_X, ALU.max).then_inc(small_free, 1)
                dve.wait_ge(small_free, SMALL_SETUP + SMALL_BATCH * b + CC + 1)
                for c in range(CC):
                    dve.tensor_scalar(kdiag[:, c, :], ident[:, :], km2[:, c:c + 1], None, ALU.mult).then_inc(kdiag_ready, 1)
                kb = small_wait(b, CC + 1)
                for g in range(2):
                    dve.tensor_tensor(K[:, 4 * g:4 * g + 4, :], K[:, 4 * g:4 * g + 4, :],
                                      kb[:, 0:C].unsqueeze(1).to_broadcast([P, 4, C]), ALU.subtract
                                      ).then_inc((ks_ready, small_free)[g], 1)
                split_low(b, 1)
                for c in range(CC):
                    sp_ = small_wait(b, CC + 2 + c)
                    dve.reciprocal(rst[:, c:c + 1], sp_[:, P:P + 1]).then_inc(rst_ready, 1)
                    dve.wait_ge(rst_ready, CC * b + c + 1)
                    dve.scalar_tensor_tensor(out=state[:, c, 0:P].rearrange("p (h d) -> p h d", h=HPC),
                                             in0=sp_[:, 0:P].rearrange("p (h d) -> p h d", h=HPC), scalar=rst[:, c:c + 1],
                                             in1=bsel[:, :].unsqueeze(2).to_broadcast([P, HPC, LD]),
                                             op0=ALU.mult, op1=ALU.mult).then_inc(small_free, 1)
                for i in range(TB + 1):
                    if i < TB:
                        n = TB * b + i
                        s = 2 * CC + 2 + i
                        o = small_wait(b, s)[:, 0:CC * (P + HPC)].rearrange("p (c m) -> p c m", c=CC)
                        rd = rden[:, i % 2, :].rearrange("p (c h) -> p c h", c=CC)
                        dve.reciprocal(rd, o[:, :, P:P + HPC]).then_inc(rden_ready, 1)
                        dve.wait_ge(rden_ready, n + 1)
                        dve.tensor_tensor(K[:, i, :].rearrange("p (c h d) -> p c h d", c=CC, h=HPC),
                                          o[:, :, 0:P].rearrange("p c (h d) -> p c h d", h=HPC),
                                          rd.unsqueeze(3).to_broadcast([P, CC, HPC, LD]), ALU.mult).then_inc(small_free, 1)
                        dve.wait_ge(small_free, SMALL_SETUP + SMALL_BATCH * b + s + 1)
                        stats(b, 0, i, K[:, i, :])
                    if i >= 1:
                        norm(b, 0, i - 1, K[:, i - 1, :], z_ready)
                for i in range(TB + 1):
                    if i == 0:
                        abs_max(b, 2)
                    if i == 2:
                        scale(b, 2)
                    if i == 5:
                        split_low(b, 2)
                    if i < TB:
                        n = TB * b + i
                        y = small_wait(b, 2 * CC + 2 + TB + i)
                        dve.wait_ge(xc_ready, n + 1)
                        dve.tensor_tensor(V[:, i, :, 0:P], y[:, 0:C].rearrange("p (c d) -> p c d", c=CC),
                                          X[:, i, :].rearrange("p (c d) -> p c d", c=CC), ALU.add).then_inc(small_free, 1)
                        dve.wait_ge(small_free, SMALL_SETUP + SMALL_BATCH * b + 2 * CC + 2 + TB + i + 1)
                        stats_src = V[:, i, :, 0:P]
                        dve.bn_stats(stat[:, i % 2, :], stats_src).then_inc(stat_ready, 1)
                        dve.wait_ge(stat_ready, 3 * TB * b + TB + i + 1)
                        lone(dve)
                        dve.bn_aggr(mv[:, 1, i, :], stat[:, i % 2, :]).then_inc(mv_ready, 1)
                    if i >= 1:
                        norm(b, 1, i - 1, V[:, i - 1, :, 0:P], x1_ready)
                for i in range(TB + 3):
                    if i == 1:
                        abs_max(b, 3)
                    if i == 3:
                        scale(b, 3)
                    if i == 6:
                        split_low(b, 3)
                    if i < TB:
                        n = TB * b + i
                        lg = big[0][:, LOGIT0:LOGIT0 + XH * KEYS].rearrange("p (h k) -> p h k", h=XH)
                        dve.wait_ge(lg_ready, n + 1)
                        dve.tensor_reduce(xm[:, i % 2, :], lg, AX_X, ALU.max).then_inc(xm_ready, 1)
                        dve.wait_ge(xm_ready, n + 1)
                        dve.tensor_scalar(xmb[:, i % 2, :], xm[:, i % 2, :], bcol[:, 0:1], None, ALU.add).then_inc(xmb_ready, 1)
                        dve.wait_ge(xmb_ready, n + 1)
                        dve.scalar_tensor_tensor(out=pr[:, i % 2, :, :], in0=lg, scalar=bcol[:, 0:1],
                                                 in1=xmb[:, i % 2, :].unsqueeze(2).to_broadcast([P, XH, KEYS]),
                                                 op0=ALU.add, op1=ALU.subtract).then_inc(s_ready, 1)
                    j = i - 3
                    if j >= 0:
                        n = TB * b + j
                        s = 2 * CC + 2 + 2 * TB + j
                        o = small_wait(b, s)[:, 0:XH * (XD + 1)].rearrange("p (h m) -> p h m", h=XH)
                        dve.reciprocal(xr8[:, j % 2, :].unsqueeze(2), o[:, :, XD:XD + 1]).then_inc(xr8_ready, 1)
                        dve.wait_ge(xr8_ready, n + 1)
                        dve.tensor_tensor(Q[:, j, :].rearrange("p (h d) -> p h d", h=XH), o[:, :, 0:XD],
                                          xr8[:, j % 2, :].unsqueeze(2).to_broadcast([P, XH, XD]), ALU.mult).then_inc(small_free, 1)
                    if j >= 1:
                        dve.wait_ge(r2_ready, TB * b + j)
                        stats(b, 2, j - 1, Q[:, j - 1, :])
                    if j >= 2:
                        norm(b, 2, j - 2, Q[:, j - 2, :], x2_ready)
                dve.wait_ge(r2_ready, TB * b + TB)
                stats(b, 2, TB - 1, Q[:, TB - 1, :])
                norm(b, 2, TB - 2, Q[:, TB - 2, :], x2_ready)
                norm(b, 2, TB - 1, Q[:, TB - 1, :], x2_ready)
                for i in range(TB):
                    n = TB * b + i
                    dve.wait_ge(hi_ready, n + 1)
                    dve.scalar_tensor_tensor(out=XR[:, i, C:2 * C], in0=Q[:, i, :], scalar=XSCALE, in1=XR[:, i, 0:C],
                                             op0=ALU.mult, op1=ALU.subtract).then_inc(lo_ready, 1)
                    s = 2 * CC + 2 + 3 * TB + i
                    lg8 = small_wait(b, s)
                    dve.tensor_copy(L[:, i, :], lg8[:, 0:EXP]).then_inc(small_free, 1)
                dve.wait_ge(small_free, SMALL_SETUP + SMALL_BATCH * b + SMALL_BATCH)
                lj = L[:, :, :].unsqueeze(2).to_broadcast([P, TB, EXP, EXP])
                le_ = L[:, :, :].unsqueeze(3).to_broadcast([P, TB, EXP, EXP])
                r0 = 9 * b
                dve.tensor_reduce(lm[:, :], L[:, :, :], AX_X, ALU.max).then_inc(route_step, 1)
                dve.tensor_tensor(cmpa[:, :, :, :], lj, le_, ALU.is_gt).then_inc(route_step, 1)
                dve.tensor_tensor(cmpb[:, :, :, :], lj, le_, ALU.is_equal).then_inc(route_step, 1)
                dve.wait_ge(route_step, r0 + 1)
                dve.tensor_tensor(le[:, :, :], L[:, :, :], lm[:, :].unsqueeze(2).to_broadcast([P, TB, EXP]), ALU.subtract).then_inc(le_shift, 1)
                dve.wait_ge(route_step, r0 + 3)
                dve.tensor_tensor(cmpb[:, :, :, :], cmpb[:, :, :, :], lower[:, :, :].unsqueeze(1).to_broadcast([P, TB, EXP, EXP]), ALU.mult).then_inc(route_step, 1)
                dve.wait_ge(route_step, r0 + 4)
                dve.tensor_tensor(cmpa[:, :, :, :], cmpa[:, :, :, :], cmpb[:, :, :, :], ALU.add).then_inc(route_step, 1)
                dve.wait_ge(route_step, r0 + 5)
                dve.tensor_reduce(rk[:, :, :], cmpa[:, :, :, :], AX_X, ALU.add).then_inc(route_step, 1)
                dve.wait_ge(route_step, r0 + 6)
                dve.tensor_copy(k["rank"][:, :, bass.ds(TB * b, TB)].rearrange("p e t -> p t e"), rk[:, :, :])
                dve.wait_ge(le_ready, b + 1)
                dve.scalar_tensor_tensor(out=le[:, :, :], in0=rk[:, :, :], scalar=float(TOPK), in1=le[:, :, :],
                                         op0=ALU.is_lt, op1=ALU.mult).then_inc(route_step, 1)
                dve.wait_ge(route_step, r0 + 7)
                dve.tensor_reduce(gsum[:, 0, :], le[:, :, :], AX_X, ALU.add).then_inc(route_step, 1)
                dve.wait_ge(route_step, r0 + 8)
                dve.reciprocal(gsum[:, 1, :], gsum[:, 0, :]).then_inc(route_step, 1)
                dve.wait_ge(route_step, r0 + 9)
                dve.tensor_tensor(XR[:, :, 2 * C:ROW].bitcast(F32), le[:, :, :],
                                  gsum[:, 1, :].unsqueeze(2).to_broadcast([P, TB, EXP]), ALU.mult).then_inc(gates_ready, 1)

        @block.tensor
        def _(pe):
            pe.wait_ge(consts, CONST_STEPS)
            pe.wait_ge(setup_loaded, 16 * 4)
            for w in range(4):
                for o in range(CC):
                    use = w * CC + o
                    if use >= 2:
                        pe.wait_ge(trans_copied, use - 1)
                    for c in range(CC):
                        ins = pe.transpose(trans[use % 2][:, c, :], w_nat[:, w, o, c * P:(c + 1) * P], ident[:, :])
                    ins.then_inc(trans_ready, 1)
            pe.wait_ge(trans_copied, TRANS_SETUP)
            pe.wait_ge(lnbb_ready, CC)
            for half in range(CC):
                for c in range(CC):
                    ins = pe.matmul(small[half][:, 0:P], kdiag[:, c, :], woT[:, c, half * P:(half + 1) * P],
                                    start=(c == 0), stop=(c == CC - 1))
                ins.then_inc(small_ready, 1)

            with pe.Fori(0, B) as b:
                def trans_stage(stage, i, src):
                    s = stage * TB + i
                    use = TRANS_SETUP + TRANS_BATCH * b + s
                    pe.wait_ge(trans_copied, use - 1)
                    for c in range(CC):
                        ins = pe.transpose(trans[s % 2][:, c, :], src(c), ident[:, :])
                    ins.then_inc(trans_ready, 1)

                def copied(stage, i):
                    s = stage * TB + i
                    pe.wait_ge(trans_copied, TRANS_SETUP + TRANS_BATCH * b + s + 1)
                    return tT[:, s % 2, :, :]

                def small_slot(s):
                    pe.wait_ge(small_free, SMALL_SETUP + SMALL_BATCH * b + s - 1)
                    return small[(SMALL_SETUP + s) % 2]

                pe.wait_ge(ctx_loaded, 16 * b + 16)
                for c in range(CC):
                    pe.transpose(small_slot(c)[:, 0:KEYS], ctx_sb[:, c * P:(c + 1) * P], ident[0:KEYS, 0:KEYS]).then_inc(small_ready, 1)
                pe.wait_ge(x_loaded, 16 * b + 16)
                for i in range(TB + 1):
                    if i < TB:
                        trans_stage(0, i, lambda c: X[:, i, c * P:(c + 1) * P])
                    if i >= 1:
                        j = i - 1
                        xT = copied(0, j)
                        if j >= 2:
                            pe.wait_ge(v_ready, TB * b + j - 1)
                        for c in range(CC):
                            pe.matmul(big[j % 2][:, 0:2 * C], xT[:, c, :], wqkv[:, c, 0:2 * C], start=(c == 0), stop=(c == CC - 1))
                        for c in range(CC):
                            ins = pe.matmul(big[j % 2][:, 2 * C:3 * C], xT[:, c, :], wqkv[:, c, 2 * C:3 * C], start=(c == 0), stop=(c == CC - 1))
                        ins.then_inc(qkv_ready, 1)
                pe.wait_ge(kmx_ready, TB * b + TB)
                km = small_slot(CC)
                for c in range(CC):
                    ins = pe.transpose(km[:, c * P:(c + 1) * P], kmx[:, c * P:(c + 1) * P], ident[:, :])
                ins.then_inc(small_ready, 1)
                pe.wait_ge(kdiag_ready, CC * b + CC)
                pe.matmul(small_slot(CC + 1)[:, 0:C], ones[:, :], kdiag[:, :, :].rearrange("p c t -> p (c t)"),
                          start=True, stop=True).then_inc(small_ready, 1)
                pe.wait_ge(v_ready, TB * b + TB)
                for c in range(CC):
                    dst = small_slot(CC + 2 + c)
                    for i in range(TB):
                        if c == 0 and i % 4 == 0:
                            pe.wait_ge(ke_ready, 2 * b + i // 4 + 1)
                        ins = pe.matmul(dst[:, 0:P + 1], K[:, i, c * P:(c + 1) * P], V[:, i, c, :], start=(i == 0), stop=(i == TB - 1))
                    ins.then_inc(small_ready, 1)
                for i in range(TB + 1):
                    if i < TB:
                        pe.wait_ge(qe_ready, TB * b + i + 1)
                        trans_stage(1, i, lambda c: Q[:, i, c * P:(c + 1) * P])
                    if i >= 1:
                        j = i - 1
                        qT = copied(1, j)
                        if j == 0:
                            pe.wait_ge(small_free, SMALL_SETUP + SMALL_BATCH * b + 2 * CC + 2)
                        dst = small_slot(2 * CC + 2 + j)
                        for c in range(CC):
                            ins = pe.matmul(dst[:, c * (P + HPC):(c + 1) * (P + HPC)], qT[:, c, :], state[:, c, :], start=True, stop=True)
                        ins.then_inc(small_ready, 1)
                for i in range(TB + 1):
                    if i < TB:
                        pe.wait_ge(z_ready, TB * b + i + 1)
                        trans_stage(2, i, lambda c: K[:, i, c * P:(c + 1) * P])
                    if i >= 1:
                        j = i - 1
                        zT = copied(2, j)
                        if j == 0:
                            pe.wait_ge(woT_ready, CC)
                        dst = small_slot(2 * CC + 2 + TB + j)
                        for c in range(CC):
                            ins = pe.matmul(dst[:, 0:C], zT[:, c, :], woT[:, c, :], start=(c == 0), stop=(c == CC - 1))
                        ins.then_inc(small_ready, 1)
                pe.wait_ge(small_free, SMALL_SETUP + SMALL_BATCH * b + CC)
                pe.wait_ge(mask_ready, b + 1)
                pe.wait_ge(vx_ready, b + 1)
                for i in range(TB + 4):
                    if i < TB:
                        pe.wait_ge(x1_ready, TB * b + i + 1)
                        trans_stage(3, i, lambda c: V[:, i, c, 0:P])
                    j = i - 3
                    if 0 <= j < TB:
                        pe.wait_ge(p_ready, TB * b + j + 1)
                        if j >= 1:
                            pe.wait_ge(pT_copied, TB * b + j)
                        for h in range(XH):
                            ins = pe.transpose(big[1][0:KEYS, h * P:(h + 1) * P], pr[:, j % 2, h, :], ident[:, :])
                        ins.then_inc(pT_ready, 1)
                    j = i - 1
                    if 0 <= j < TB:
                        x1T = copied(3, j)
                        if j >= 1:
                            pe.wait_ge(s_ready, TB * b + j)
                        for c in range(CC):
                            dst = big[0][:, LOGIT0 + c * XPC * KEYS:LOGIT0 + (c + 1) * XPC * KEYS]
                            pe.matmul(dst, x1T[:, c, :], kbd[:, c, :, :].rearrange("p h k -> p (h k)"), start=True, stop=False)
                            ins = pe.matmul(dst, one16[:, :], mbf[:, :, :].rearrange("p h k -> p (h k)"), start=False, stop=True)
                        ins.then_inc(lg_ready, 1)
                    j = i - 4
                    if 0 <= j < TB:
                        pe.wait_ge(pT_copied, TB * b + j + 1)
                        dst = small_slot(2 * CC + 2 + 2 * TB + j)
                        for h in range(XH):
                            ins = pe.matmul(dst[:, h * (XD + 1):(h + 1) * (XD + 1)], pT[0:KEYS, j % 2, h, :], vx[:, h, :], start=True, stop=True)
                        ins.then_inc(small_ready, 1)
                for i in range(TB + 1):
                    if i < TB:
                        pe.wait_ge(x2_ready, TB * b + i + 1)
                        trans_stage(4, i, lambda c: Q[:, i, c * P:(c + 1) * P])
                    if i >= 1:
                        j = i - 1
                        x2T = copied(4, j)
                        dst = small_slot(2 * CC + 2 + 3 * TB + j)
                        for c in range(CC):
                            ins = pe.matmul(dst[:, 0:EXP], x2T[:, c, :], rw[:, c, :], start=(c == 0), stop=(c == CC - 1))
                        ins.then_inc(small_ready, 1)


def routing(nc, k):
    st = ExitStack()
    with st:
        def sb(name, shape, dt=F32):
            return st.enter_context(nc.sbuf_tensor(name, shape, dt))

        def sem(name):
            return st.enter_context(nc.semaphore(name))

        PER = N * B // SLOTS
        HALF = NT // 2
        rank, ones, ident = k["rank"], k["ones"], k["ident"]
        chosen = sb("chosen", [P, EXP, NT])
        before = sb("before", [P, P])
        reset = sb("reset", [P, EXP, NT])
        incl = sb("incl", [P, EXP, NT])
        pos = sb("pos", [P, EXP, NT])
        picked = sb("picked", [P, NT, EXP])
        steps256 = sb("steps256", [P, PER])
        cmpt = sb("cmpt", [P, EXP, PER])
        tiles = sb("tiles", [P, EXP])
        endt = sb("endt", [P, EXP])
        start = sb("start", [P, EXP])
        posk = sb("posk", [P, TOPK, NT])
        posi = sb("posi", [P, TOPK, NT], I32)
        hii = sb("hii", [P, TOPK, NT], I32)
        loi = sb("loi", [P, TOPK, NT], I32)
        hif = sb("hif", [P, TOPK, NT])
        lof = sb("lof", [P, TOPK, NT])
        io = sb("io", [P, EBLOCKS], I32)
        iof = sb("iof", [P, EBLOCKS])
        io16 = sb("io16", [P, EBLOCKS], F16)
        vali = sb("vali", [P, HALF], I32)
        val = sb("val", [P, HALF])
        padi = sb("padi", [P, EBLOCKS], I32)
        pad = sb("pad", [P, EBLOCKS])
        RING = 4
        lo_hot = sb("lo_hot", [P, RING, P], F16)
        hi_hot = sb("hi_hot", [P, RING, EBLOCKS], F16)
        late = sb("late", [P, EBLOCKS])
        token = sb("token", [P, EBLOCKS])
        empty = sb("empty", [P, EBLOCKS])
        te = sb("te", [P, ETILES])
        cmpe = sb("cmpe", [P, ETILES, EXP])
        hot = sb("hot", [P, ETILES, EXP])
        eio = sb("eio", [P, EXP], I32)
        eiof = sb("eiof", [P, EXP])
        inv = sb("inv", [P, 2 * EXP])
        fac = sb("fac", [P, 3, EXP])
        tmp = sb("tmp", [P, ETILES, EXP])
        counts = st.enter_context(nc.psum_tensor("counts", [P, 512], F32))
        table = [st.enter_context(nc.psum_tensor(f"table{i}", [P, 512], F32)) for i in range(2)]

        made, dve_step, chosen_ready, counts_ready = sem("made"), sem("dve_step"), sem("chosen_ready"), sem("counts_ready")
        hot_ready, table_step = sem("hot_ready"), sem("table_step")
        block = st.enter_context(nc.Block())
        MADE = 12

        @block.gpsimd
        def _(pool):
            n = [0]

            def done(ins):
                n[0] += 1
                ins.then_inc(made, 1)
                pool.wait_ge(made, n[0])

            done(pool.memset(before[:, :], 1.0))
            done(pool.affine_select(out=before[:, :], in_=before[:, :], compare_op=ALU.is_gt, fill=0.0,
                                    base=0, pattern=[[1, P]], channel_multiplier=-1))
            done(pool.memset(reset[:, :, :], 1.0))
            done(pool.memset(reset[:, :, 0:1], 0.0))
            done(pool.iota(io[:, :], pattern=[[1, EBLOCKS]], base=0, channel_multiplier=0))
            done(pool.iota(eio[:, :], pattern=[[1, EXP]], base=0, channel_multiplier=0))
            done(pool.iota(vali[:, :], pattern=[[P, HALF]], base=1, channel_multiplier=1))
            done(pool.iota(padi[:, :].rearrange("p (t j) -> p t j", j=SB), pattern=[[0, ETILES], [P, SB]],
                           base=B * N + 1, channel_multiplier=1))
            done(pool.tensor_copy(iof[:, :], io[:, :]))
            done(pool.tensor_copy(eiof[:, :], eio[:, :]))
            done(pool.tensor_copy(val[:, :], vali[:, :]))
            done(pool.tensor_copy(pad[:, :], padi[:, :]))
            assert n[0] == MADE

        @block.vector
        def _(dve):
            n = [0]

            def done(ins):
                n[0] += 1
                ins.then_inc(dve_step, 1)
                dve.wait_ge(dve_step, n[0])

            dve.tensor_scalar(chosen[:, :, :], rank[:, :, :], float(TOPK), None, ALU.is_lt).then_inc(chosen_ready, 1)
            dve.wait_ge(made, MADE)
            done(dve.tensor_copy(io16[:, :], iof[:, :]))
            done(dve.tensor_copy(k["ident16"][:, :], ident[:, :]))
            done(dve.tensor_scalar(steps256[:, :], iof[:, 0:PER], float(SLOTS), None, ALU.mult))
            dve.wait_ge(counts_ready, 1)
            prefix = counts[:, 0:EXP * NT]
            total = counts[:, EXP * NT:2 * EXP * NT]
            flat = lambda t: t[:, :, :].rearrange("p e t -> p (e t)")
            done(dve.tensor_tensor_scan(flat(incl), flat(reset), total, 0.0, ALU.mult, ALU.add))
            done(dve.tensor_tensor(cmpt[:, :, :], incl[:, :, NT - 1:NT].to_broadcast([P, EXP, PER]),
                                   steps256[:, :].unsqueeze(1).to_broadcast([P, EXP, PER]), ALU.is_gt))
            done(dve.tensor_reduce(tiles[:, :], cmpt[:, :, :], AX_X, ALU.add))
            done(dve.tensor_tensor_scan(endt[:, :], ones[:, 0:EXP], tiles[:, :], 0.0, ALU.mult, ALU.add))
            done(dve.tensor_tensor(start[:, :], endt[:, :], tiles[:, :], ALU.subtract))
            done(dve.tensor_tensor(flat(pos), flat(incl), total, ALU.subtract))
            done(dve.tensor_tensor(flat(pos), flat(pos), prefix, ALU.add))
            done(dve.tensor_scalar(start[:, :], start[:, :], float(SLOTS), None, ALU.mult))
            done(dve.tensor_tensor(pos[:, :, :], pos[:, :, :], start[:, :].unsqueeze(2).to_broadcast([P, EXP, NT]), ALU.add))
            for j in range(TOPK):
                done(dve.scalar_tensor_tensor(out=picked[:, :, :].rearrange("p t e -> p e t"), in0=rank[:, :, :], scalar=float(j),
                                              in1=pos[:, :, :], op0=ALU.is_equal, op1=ALU.mult))
                done(dve.tensor_reduce(posk[:, j, :], picked[:, :, :], AX_X, ALU.add))
            done(dve.tensor_copy(posi[:, :, :], posk[:, :, :]))
            done(dve.tensor_scalar(hii[:, :, :], posi[:, :, :], 7, None, ALU.logical_shift_right))
            done(dve.tensor_scalar(loi[:, :, :], posi[:, :, :], P - 1, None, ALU.bitwise_and))
            done(dve.tensor_copy(hif[:, :, :], hii[:, :, :]))
            done(dve.tensor_copy(lof[:, :, :], loi[:, :, :]))
            q = 0
            for h in range(2):
                for j in range(TOPK):
                    for t in range(HALF):
                        T = h * HALF + t
                        if q >= RING:
                            dve.wait_ge(table_step, q - RING + 1)
                        dve.tensor_scalar(lo_hot[:, q % RING, :], io16[:, 0:P], lof[:, j, T:T + 1], None, ALU.is_equal).then_inc(hot_ready, 1)
                        dve.tensor_scalar(hi_hot[:, q % RING, :], io16[:, :], hif[:, j, T:T + 1], val[:, t:t + 1],
                                          ALU.is_equal, ALU.mult).then_inc(hot_ready, 1)
                        q += 1
            done(dve.tensor_tensor(cmpe[:, :, :], iof[:, 0:ETILES].unsqueeze(2).to_broadcast([P, ETILES, EXP]),
                                   endt[:, :].unsqueeze(1).to_broadcast([P, ETILES, EXP]), ALU.is_ge))
            done(dve.tensor_reduce(te[:, :], cmpe[:, :, :], AX_X, ALU.add))
            done(dve.tensor_scalar(te[:, :], te[:, :], float(EXP - 1), None, ALU.min))
            done(dve.tensor_copy(k["tile_expert"][:, :], te[:, :]))
            done(dve.tensor_tensor(hot[:, :, :], te[:, :].unsqueeze(2).to_broadcast([P, ETILES, EXP]),
                                   eiof[:, :].unsqueeze(1).to_broadcast([P, ETILES, EXP]), ALU.is_equal))
            done(dve.reciprocal(inv[:, :], k["wpow"][:, :]))
            wp = k["wpow"][:, :].rearrange("p (e m) -> p e m", m=2)
            iv = inv[:, :].rearrange("p (e m) -> p e m", m=2)
            done(dve.tensor_scalar(fac[:, 0, :], wp[:, :, 0], 1.0 / (XSCALE * WTARGET), None, ALU.mult))
            done(dve.tensor_scalar(fac[:, 1, :], iv[:, :, 0], WTARGET, None, ALU.mult))
            done(dve.scalar_tensor_tensor(out=fac[:, 2, :], in0=wp[:, :, 0], scalar=1.0 / (WTARGET * WTARGET),
                                          in1=wp[:, :, 1], op0=ALU.mult, op1=ALU.mult))
            for f, dst in ((0, k["up_scale"]), (1, k["h_scale"])):
                done(dve.tensor_tensor(tmp[:, :, :], hot[:, :, :], fac[:, f, :].unsqueeze(1).to_broadcast([P, ETILES, EXP]), ALU.mult))
                done(dve.tensor_reduce(dst[:, :], tmp[:, :, :], AX_X, ALU.add))
            done(dve.tensor_tensor(k["pick"][:, :, :], hot[:, :, :], fac[:, 2, :].unsqueeze(1).to_broadcast([P, ETILES, EXP]), ALU.mult))
            dve.wait_ge(table_step, TOPK * NT)
            done(dve.tensor_scalar(late[:, :], table[1][:, 0:EBLOCKS], 0.0, float(HALF * P), ALU.is_gt, ALU.mult))
            done(dve.tensor_tensor(late[:, :], table[1][:, 0:EBLOCKS], late[:, :], ALU.add))
            done(dve.tensor_tensor(token[:, :], table[0][:, 0:EBLOCKS], late[:, :], ALU.add))
            done(dve.scalar_tensor_tensor(out=empty[:, :], in0=token[:, :], scalar=0.0, in1=pad[:, :], op0=ALU.is_equal, op1=ALU.mult))
            done(dve.scalar_tensor_tensor(out=k["slot_row"][:, :], in0=token[:, :], scalar=-1.0, in1=empty[:, :], op0=ALU.add, op1=ALU.add))

        @block.tensor
        def _(pe):
            pe.wait_ge(made, MADE)
            pe.wait_ge(chosen_ready, 1)
            flat = chosen[:, :, :].rearrange("p e t -> p (e t)")
            pe.matmul(counts[:, 0:EXP * NT], before[:, :], flat, start=True, stop=True)
            pe.matmul(counts[:, EXP * NT:2 * EXP * NT], ones[:, :], flat, start=True, stop=True).then_inc(counts_ready, 1)
            for q in range(TOPK * NT):
                half, at = divmod(q, TOPK * HALF)
                pe.wait_ge(hot_ready, 2 * q + 2)
                pe.matmul(table[half][:, 0:EBLOCKS], lo_hot[:, q % RING, :], hi_hot[:, q % RING, :],
                          start=(at == 0), stop=(at == TOPK * HALF - 1)).then_inc(table_step, 1)


def experts(nc, k, rows, acc):
    st = ExitStack()
    with st:
        def sb(name, shape, dt=F32):
            return st.enter_context(nc.sbuf_tensor(name, shape, dt))

        def ps(name, shape, dt=F32):
            return st.enter_context(nc.psum_tensor(name, shape, dt))

        def sem(name):
            return st.enter_context(nc.semaphore(name))

        xg = sb("xg", [P, 2, SB, ROW // 2])
        xT = sb("xT", [P, 2, 2 * CC, SLOTS], F16)
        h = sb("h", [P, PAIRS, 2 * SLOTS])
        hh = sb("hh", [P, 2, HC, SLOTS], F16)
        hl = sb("hl", [P, 2, HC, SLOTS], F16)
        y = sb("y", [P, 2, SB, C])
        gp = sb("gp", [P, 2, SB, EXP])
        gate = sb("gate", [P, 2, SB])
        psx = [ps(f"psx{i}", [P, 2 * CC, SLOTS], F16) for i in range(2)]
        psu = [ps(f"psu{i}", [P, 512]) for i in range(PAIRS)]
        psy = [ps(f"psy{i}", [P, SB, C]) for i in range(2)]
        warm = sb("warm", [P, 1])
        gather_rows = sb("gather_rows", [P, 2, SB], I32)
        add_rows = sb("add_rows", [P, 2, SB], I32)

        xg_loaded = [sem(f"xg_loaded{i}") for i in range(2)]
        y_added = [sem(f"y_added{i}") for i in range(2)]
        xt_ready, xt_copied, up_ready, gelu_ready = sem("xt_ready"), sem("xt_copied"), sem("up_ready"), sem("gelu_ready")
        hh_ready, hl_ready, down_ready, y_ready = sem("hh_ready"), sem("hl_ready"), sem("down_ready"), sem("y_ready")
        gather_rows_ready, add_rows_ready = sem("gather_rows_ready"), sem("add_rows_ready")
        gp_ready, gate_ready, table_loaded = sem("gp_ready"), sem("gate_ready"), sem("warm_ready")
        passed = {e: sem(f"tiles_passed_{i}") for i, e in enumerate((nc.gpsimd, nc.scalar))}
        block = st.enter_context(nc.Block())

        def lone(eng):
            eng.sem_inc(passed[eng], 1)

        @block.gpsimd
        def _(pool):
            def slot_rows(dst, t, ready):
                at = t * SB
                src = k["slot_row"][:, bass.ds(at, SB)] if not isinstance(at, int) else k["slot_row"][:, at:at + SB]
                lone(pool)
                pool.tensor_copy(dst, src).then_inc(ready, 1)
                pool.wait_ge(ready, t + 1)
                lone(pool)

            def gather(t, par, half):
                slot_rows(gather_rows[:, par, :], t, gather_rows_ready)
                for j in range(SB):
                    pool.indirect_dma_start(xg[:, par, j, :], None, rows,
                                            bass.IndirectOffsetOnAxis(ap=gather_rows[:, par, j:j + 1], axis=0)
                                            ).then_inc(xg_loaded[par], 16)

            def add(t, par, half):
                for j in range(SB):
                    pool.indirect_dma_start(acc, bass.IndirectOffsetOnAxis(ap=add_rows[:, par, j:j + 1], axis=0),
                                            y[:, par, j, :], None, compute_op=ALU.add).then_inc(y_added[par], 16)

            def step(t, par, half, prior):
                if prior:
                    pool.wait_ge(xt_ready, t - 1)
                    pool.wait_ge(gate_ready, t - 1)
                gather(t, par, half)

            def result(t, par, half, prior):
                pool.wait_ge(y_ready, SB * (t + 1))
                slot_rows(add_rows[:, par, :], t, add_rows_ready)
                if prior:
                    pool.wait_ge(y_added[1 - par], 16 * SB * (half + par))
                lone(pool)
                add(t, par, half)

            gather(0, 0, 0)
            gather(1, 1, 0)
            step(2, 0, 1, True)
            result(0, 0, 0, False)
            step(3, 1, 1, True)
            result(1, 1, 0, True)
            with pool.Fori(2, ETILES // 2) as u:
                for par in range(2):
                    step(2 * u + par, par, u, True)
                    result(2 * u + par - 2, par, u - 1, True)
            for t in range(ETILES - ETILES % 2, ETILES):
                step(t, t % 2, t // 2, True)
            for t in range(2 * (ETILES // 2) - 2, ETILES):
                result(t, t % 2, t // 2, True)
            pool.wait_ge(y_added[0], 16 * SB * ((ETILES + 1) // 2))
            pool.wait_ge(y_added[1], 16 * SB * (ETILES // 2))

        @block.tensor
        def _(pe):
            def row_transposes(t, par, half, prior=True):
                pe.wait_ge(xg_loaded[par], 16 * SB * (half + 1))
                if prior:
                    pe.wait_ge(xt_copied, t - 1)
                for q in range(2 * CC):
                    for j in range(SB):
                        ins = pe.transpose(psx[par][:, q, j * P:(j + 1) * P], xg[:, par, j, q * P // 2:(q + 1) * P // 2].bitcast(F16), k["ident16"][:, :])
                ins.then_inc(xt_ready, 1)

            def up_products(t, par, half, e, prior=True):
                pe.wait_ge(xt_copied, t + 1)
                w = k["wu"][:, bass.ds(e, 1), :, :, :].rearrange("p e s c h -> p (e s) c h")
                for p in range(PAIRS):
                    if prior:
                        pe.wait_ge(gelu_ready, PAIRS * (t - 1) + (p + 1))
                    for i in range(2):
                        m = (2 * p + i) * P
                        n = 0
                        for c in range(CC):
                            for ws, xs in ((0, 0), (0, 1), (1, 0)):
                                ins = pe.matmul(psu[p][:, i * SLOTS:(i + 1) * SLOTS], w[:, ws, c, m:m + P], xT[:, par, xs * CC + c, :],
                                                start=(n == 0), stop=(n == 3 * CC - 1))
                                n += 1
                    ins.then_inc(up_ready, 1)

            def down_products(t, par, half, e, prior=True):
                pe.wait_ge(hl_ready, PAIRS * (t + 1))
                w = k["wd"][:, bass.ds(e, 1), :, :, :].rearrange("p e s c d -> p (e s) c d")
                for j in range(SB):
                    if prior and j == 0:
                        pe.wait_ge(y_ready, SB * (t - 1))
                    n = 0
                    for c in range(HC):
                        for hs, ws in ((0, 0), (0, 1), (1, 0)):
                            ins = pe.matmul(psy[par][:, j, :], (hh, hl)[hs][:, par, c, j * P:(j + 1) * P], w[:, ws, c, :],
                                            start=(n == 0), stop=(n == 3 * HC - 1))
                            n += 1
                    ins.then_inc(down_ready, 1)

            def expert_of(t):
                at = k["tile_expert"][0:1, bass.ds(t, 1)] if not isinstance(t, int) else k["tile_expert"][0:1, t:t + 1]
                return pe.value_load(at, min_val=0, max_val=EXP - 1)

            def turn(t, par, half, more=True, prior=(True, True)):
                up_products(t, par, half, expert_of(t))
                if more:
                    row_transposes(t + 1, 1 - par, half + par)
                down_products(t - 1, 1 - par, half, expert_of(t - 1), prior[0])

            row_transposes(0, 0, 0, False)
            up_products(0, 0, 0, expert_of(0), False)
            row_transposes(1, 1, 0, False)
            turn(1, 1, 0, prior=(False, True))
            turn(2, 0, 1, prior=(False, True))
            turn(3, 1, 1)
            with pe.Fori(2, (ETILES - 1) // 2) as u:
                for par in range(2):
                    turn(2 * u + par, par, u)
            last = ETILES - 1
            for t in range(2 * (last // 2), ETILES):
                turn(t, t % 2, t // 2, more=t + 1 < ETILES)
            down_products(last, last % 2, last // 2, expert_of(last))

        @block.scalar
        def _(act):
            act.activation(warm[:, :], k["nhalf"][:, 0:1], ACT.Gelu_apprx_tanh).then_inc(table_loaded, 1)

            def gelus(t, par, half, prior=True):
                sc = k["up_scale"][:, bass.ds(t, 1)] if not isinstance(t, int) else k["up_scale"][:, t:t + 1]
                for p in range(PAIRS):
                    act.wait_ge(up_ready, PAIRS * t + (p + 1))
                    if prior:
                        act.wait_ge(hl_ready, PAIRS * (t - 1) + (p + 1))
                    lone(act)
                    act.activation(h[:, p, :], psu[p][:, :], ACT.Gelu_apprx_tanh, scale=sc).then_inc(gelu_ready, 1)

            def results(t, par, half, prior=True):
                act.wait_ge(gate_ready, t + 1)
                if prior:
                    act.wait_ge(y_added[par], 16 * SB * half)
                act.wait_ge(down_ready, SB * (t + 1))
                for j in range(SB):
                    act.activation(y[:, par, j, :], psy[par][:, j, :], ACT.Copy, scale=gate[:, par, j:j + 1]).then_inc(y_ready, 1)

            gelus(0, 0, 0, False)
            gelus(1, 1, 0)
            results(0, 0, 0, False)
            gelus(2, 0, 1)
            results(1, 1, 0, False)
            gelus(3, 1, 1)
            results(2, 0, 1)
            with act.Fori(2, ETILES // 2) as u:
                for par in range(2):
                    gelus(2 * u + par, par, u)
                    results(2 * u + par - 1, 1 - par, u - 1 + par)
            for t in range(2 * (ETILES // 2), ETILES):
                gelus(t, t % 2, t // 2)
                results(t - 1, 1 - t % 2, (t - 1) // 2)
            results(ETILES - 1, (ETILES - 1) % 2, (ETILES - 1) // 2)

        @block.vector
        def _(dve):
            def take_rows(t, par, half, prior=True):
                dve.wait_ge(xt_ready, t + 1)
                if prior:
                    dve.wait_ge(up_ready, PAIRS * (t - 1))
                dve.tensor_copy(xT[:, par, :, :], psx[par][:, :, :]).then_inc(xt_copied, 1)
                pick = k["pick"][:, bass.ds(t, 1), :] if not isinstance(t, int) else k["pick"][:, t:t + 1, :]
                if prior:
                    dve.wait_ge(y_ready, SB * (t - 1))
                dve.tensor_tensor(gp[:, par, :, :], xg[:, par, :, C:ROW // 2], pick.to_broadcast([P, SB, EXP]),
                                  ALU.mult).then_inc(gp_ready, 1)
                dve.wait_ge(gp_ready, t + 1)
                dve.tensor_reduce(gate[:, par, :], gp[:, par, :, :], AX_X, ALU.add).then_inc(gate_ready, 1)

            def halves(t, par, half, prior=True):
                sc = k["h_scale"][:, bass.ds(t, 1)] if not isinstance(t, int) else k["h_scale"][:, t:t + 1]
                if prior:
                    dve.wait_ge(down_ready, SB * (t - 1))
                for p in range(PAIRS):
                    hi = hh[:, par, 2 * p:2 * p + 2, :].rearrange("p c s -> p (c s)")
                    lo = hl[:, par, 2 * p:2 * p + 2, :].rearrange("p c s -> p (c s)")
                    dve.wait_ge(gelu_ready, PAIRS * t + (p + 1))
                    dve.tensor_scalar(hi, h[:, p, :], sc, None, ALU.mult).then_inc(hh_ready, 1)
                    dve.wait_ge(hh_ready, PAIRS * t + (p + 1))
                    dve.scalar_tensor_tensor(out=lo, in0=h[:, p, :], scalar=sc, in1=hi, op0=ALU.mult, op1=ALU.subtract).then_inc(hl_ready, 1)

            take_rows(0, 0, 0, False)
            halves(0, 0, 0, False)
            take_rows(1, 1, 0, False)
            halves(1, 1, 0, False)
            take_rows(2, 0, 1)
            with dve.Fori(1, (ETILES - 1) // 2) as u:
                for par in range(2):
                    halves(2 * u + par, par, u)
                    take_rows(2 * u + par + 1, 1 - par, u + par)
            for t in range(2 * ((ETILES - 1) // 2), ETILES):
                halves(t, t % 2, t // 2)
                if t + 1 < ETILES:
                    take_rows(t + 1, 1 - t % 2, (t + 1) // 2)


def last_norm(nc, k, acc, out):
    st = ExitStack()
    with st:
        def sem(name):
            return st.enter_context(nc.semaphore(name))

        GROUPS = B
        G = NT // GROUPS
        s = st.enter_context(nc.sbuf_tensor("sums", [P, NT, C], F32))
        stat = st.enter_context(nc.sbuf_tensor("fstat", [P, 2, 6], F32))
        mv = st.enter_context(nc.sbuf_tensor("fmv", [P, NT, 2], F32))
        var = st.enter_context(nc.sbuf_tensor("fvar", [P, NT], F32))
        rstd = st.enter_context(nc.sbuf_tensor("frstd", [P, NT], F32))
        loaded = [sem(f"loaded{g}") for g in range(GROUPS)]
        stats_ready, mv_ready, var_ready, rstd_ready, normed, stored = (
            sem("fstats_ready"), sem("fmv_ready"), sem("fvar_ready"), sem("frstd_ready"), sem("normed"), sem("stored"))
        a = acc[0:B * N, :].rearrange("(t p) c -> p t c", p=P)
        o = out.rearrange("b (t p) c -> b p t c", p=P)
        block = st.enter_context(nc.Block())

        @block.sync
        def _(sp):
            for g in range(GROUPS):
                sp.dma_start(s[:, g * G:(g + 1) * G, :], a[:, g * G:(g + 1) * G, :]).then_inc(loaded[g], 16)
            for g in range(GROUPS):
                sp.wait_ge(normed, (g + 1) * G)
                sp.dma_start(o[g], s[:, g * G:(g + 1) * G, :]).then_inc(stored, 16)
            sp.wait_ge(stored, 16 * GROUPS)

        @block.vector
        def _(dve):
            for t in range(NT + 3):
                if t < NT:
                    if t % G == 0:
                        dve.wait_ge(loaded[t // G], 16)
                    dve.bn_stats(stat[:, t % 2, :], s[:, t, :]).then_inc(stats_ready, 1)
                    dve.wait_ge(stats_ready, t + 1)
                    dve.bn_aggr(mv[:, t, :], stat[:, t % 2, :]).then_inc(mv_ready, 1)
                if t >= 3:
                    i = t - 3
                    dve.wait_ge(rstd_ready, i + 1)
                    dve.tensor_scalar(s[:, i, :], s[:, i, :], mv[:, i, 0:1], rstd[:, i:i + 1], ALU.subtract, ALU.mult).then_inc(normed, 1)

        @block.gpsimd
        def _(pool):
            for t in range(NT):
                pool.wait_ge(mv_ready, t + 1)
                pool.tensor_scalar(var[:, t:t + 1], mv[:, t, 1:2], LN_EPS, None, ALU.add).then_inc(var_ready, 1)
                pool.wait_ge(var_ready, t + 1)
                pool.tensor_tensor(rstd[:, t:t + 1], var[:, t:t + 1], k["nhalf"][:, 0:1], ALU.pow).then_inc(rstd_ready, 1)


_INS = ["x", "ctx_2048", "mask_BxS2_ik0", "L0_attn_Wq", "L0_attn_bq", "L0_attn_Wk", "L0_attn_bk", "L0_attn_Wv",
        "L0_attn_bv", "L0_attn_Wo", "L0_attn_bo", "L0_attn_ln_g", "L0_attn_ln_b", "L0_xattn_b", "L0_ffn_router_w",
        "L0_ffn_up_w", "L0_ffn_down_w"]
_OUTS = [((B, N, C), "float32")]


def kernel(**inputs):
    import numpy as _np
    import concourse.bacc as _bacc
    from concourse import mybir as _mybir
    from concourse.bass_utils import run_bass_kernel_spmd as _run

    nc = _bacc.Bacc("TRN2", target_bir_lowering=False, num_devices=1)
    arrays, args = {}, []
    for name in _INS:
        a = _np.ascontiguousarray(inputs[name])
        arrays[f"in_{name}_dram"] = a
        args.append(nc.dram_tensor(f"in_{name}_dram", a.shape, _mybir.dt.from_np(a.dtype), kind="ExternalInput").ap())
    for i, (shape, dtype) in enumerate(_OUTS):
        dt = _mybir.dt.from_np(_np.dtype(dtype))
        args.append(nc.dram_tensor(f"out_{i}_dram", shape, dt, kind="ExternalOutput").ap())
    layer_kernel(nc, *args)
    r = _run(nc, [arrays], core_ids=[0])
    return r.results[0]["out_0_dram"]
```

```python
from contextlib import ExitStack

import concourse.bass as bass
from concourse import mybir

F32 = mybir.dt.float32
F16 = mybir.dt.float16
BF16 = mybir.dt.bfloat16
I32 = mybir.dt.int32
ALU = mybir.AluOpType
ACT = mybir.ActivationFunctionType
AX_X = mybir.AxisListType.X
ABSMAX = bass.bass_isa.ReduceOp.absmax

P = 128
B, N, C = 4, 1024, 256
CC = C // P
TB = N // P
NT = B * TB
LH, LD = 16, 16
HPC = P // LD
XH, XD = 8, 32
XPC = P // XD
KEYS = 77
CTX = 2 * C
EXP, TOPK, HID = 8, 4, 1024
HC = HID // P
SLOTS = 256
SB = SLOTS // P
ETILES = (TOPK * B * N + EXP * (SLOTS - 1)) // SLOTS
EBLOCKS = ETILES * SB
PAIRS = HC // 2
TRASH = SB * P
ROWS = B * N + TRASH
FLAT = XH * KEYS
FCH = -(-FLAT // P)
ROW = 2 * C + 2 * EXP
LN_EPS = 1e-5
MASKED = -1e30
XSCALE = 64.0
WTARGET = 64.0
LOGIT0 = 1024 - 512 - XPC * KEYS
CONST_STEPS = 17 + 3 * FCH
PIECES = 4
EXPONENT = 0x7F800000

TRANS_SETUP = 4 * CC
TRANS_BATCH = 7 * TB
SMALL_SETUP = CC
SMALL_BATCH = CC + 2 + CC + 4 * TB


SPAN = [(c * P // KEYS, -(-min((c + 1) * P, FLAT) // KEYS)) for c in range(FCH)]
SPAN_MAX = max(b - a for a, b in SPAN)
SEGMENTS = [(c, max(c * P, h * KEYS) - c * P, h, max(c * P, h * KEYS) - h * KEYS,
             min((c + 1) * P, (h + 1) * KEYS) - max(c * P, h * KEYS))
            for c in range(FCH) for h in range(*SPAN[c])]


def cross_uses():
    order = []
    for i in range(TB + 4):
        if i < TB:
            order.append(("x1", i))
        if 0 <= i - 3 < TB:
            order += [("pa", i - 3), ("pb", i - 3)]
    return {what: n for n, what in enumerate(order)}


CROSS = cross_uses()


def layer_kernel(nc, x, ctx, mask, Wq, bq, Wk, bk, Wv, bv, Wo, bo, ln_g, ln_b, xb, router, up, down, out):
    rows = nc.dram_tensor("token_rows", [ROWS, ROW // 2], F32, kind="Internal").ap()
    acc = nc.dram_tensor("token_sums", [ROWS, C], F32, kind="Internal").ap()
    with ExitStack() as all_:
        def keep(name, shape, dt):
            return all_.enter_context(nc.sbuf_tensor(name, shape, dt))

        k = {
            "wu": keep("w_up", [P, EXP, 2, CC, HID], F16),
            "wd": keep("w_down", [P, EXP, 2, HC, C], F16),
            "wpow": keep("w_pow", [P, 2 * EXP], F32),
            "rank": keep("rank", [P, EXP, NT], F32),
            "ident": keep("ident", [P, P], F32),
            "ones": keep("ones", [P, P], F32),
            "nhalf": keep("nhalf", [P, TB], F32),
        }
        attention(nc, k, rows, acc, x, ctx, mask, Wq, bq, Wk, bk, Wv, bv, Wo, bo, ln_g, ln_b, xb, router, up, down)
        with ExitStack() as plan:
            def tab(name, shape, dt):
                return plan.enter_context(nc.sbuf_tensor(name, shape, dt))

            k["slot_row"] = tab("slot_row", [P, EBLOCKS], I32)
            k["tile_expert"] = tab("tile_expert", [P, ETILES], I32)
            k["pick"] = tab("pick", [P, ETILES, EXP], F32)
            k["up_scale"] = tab("up_scale", [P, ETILES], F32)
            k["h_scale"] = tab("h_scale", [P, ETILES], F32)
            k["ident16"] = tab("ident16", [P, P], F16)
            routing(nc, k)
            experts(nc, k, rows, acc)
        last_norm(nc, k, acc, out)


def attention(nc, k, rows, acc, x, ctx, mask, Wq, bq, Wk, bk, Wv, bv, Wo, bo, ln_g, ln_b, xb, router, up, down):
    st = ExitStack()
    with st:
        def sb(name, shape, dt=F32):
            return st.enter_context(nc.sbuf_tensor(name, shape, dt))

        def ps(name, shape, dt=F32):
            return st.enter_context(nc.psum_tensor(name, shape, dt))

        def sem(name):
            return st.enter_context(nc.semaphore(name))

        ident, ones, nhalf = k["ident"], k["ones"], k["nhalf"]
        X = sb("X", [P, TB, C])
        Q = sb("Q", [P, TB, C])
        KZ = sb("KZ", [P, TB * (ROW // 2)])
        V = sb("V", [P, TB, CC, P + 1])
        K = KZ[:, 0:TB * C].rearrange("p (t c) -> p t c", c=C)
        XR = KZ[:, :].bitcast(F16).rearrange("p (t r) -> p t r", r=ROW)
        W8 = sb("W8", [P, 2048])
        wqkv = sb("wqkv", [P, CC, 3 * C])
        woT = sb("woT", [P, CC, C])
        bias = sb("bias", [P, 3 * C])
        cvec = sb("cvec", [P, C])
        tT = sb("tT", [P, 2, CC, P])
        kbd = sb("kbd", [P, CC, XPC, KEYS])
        hsel = sb("hsel", [P, XPC])
        bsel = sb("bsel", [P, HPC])
        state = sb("state", [P, CC, P + HPC])
        ctx_sb = sb("ctx_sb", [KEYS, C])
        vx = sb("vx", [P, FCH, SPAN_MAX, XD + 1])
        mint = sb("mint", [1, KEYS], I32)
        mrow = sb("mrow", [1, KEYS])
        mbf = sb("mbf", [1, XPC, KEYS], BF16)
        one16 = sb("one16", [1, P], BF16)
        pr = sb("pr", [P, 2, XH, KEYS])
        pT = sb("pT", [P, 2, FCH, P])
        rw = sb("rw", [P, CC, EXP])
        gb = sb("gb", [P, 2, CC])
        bcol = sb("bcol", [P, 1])
        kmx = pT[:, 1, 0:CC, :].rearrange("p c t -> p (c t)")
        kdiag = pT[:, 0, 0:CC, :]
        km2 = sb("km2", [P, CC])
        qm = sb("qm", [P, 2, LH])
        rden = sb("rden", [P, 2, LH])
        rst = sb("rst", [P, CC])
        stat = sb("stat", [P, 2, 6])
        mv = sb("mv", [P, 3, TB, 2])
        ve = sb("ve", [P, 3, TB])
        rstd = sb("rstd", [P, 3, TB])
        xm = sb("xm", [P, 2, XH])
        xmb = sb("xmb", [P, 2, XH])
        xr8 = sb("xr8", [P, 2, XH])
        L = sb("L", [P, TB, EXP])
        lm = sb("lm", [P, TB])
        le = sb("le", [P, TB, EXP])
        both = pr[:, :, :, :].rearrange("p r h k -> p (r h k)")[:, 0:2 * TB * EXP * EXP].rearrange(
            "p (r t e j) -> p r t e j", r=2, t=TB, e=EXP)
        cmpa, cmpb = both[:, 0], both[:, 1]
        lower = sb("lower", [P, EXP, EXP])
        rk = sb("rk", [P, TB, EXP])
        gsum = sb("gsum", [P, 2, TB])
        wmx = sb("wmx", [P, 1])
        wall = sb("wall", [P, 1])
        wcl = sb("wcl", [P, 1])
        wrp = sb("wrp", [P, 1])
        wsc = sb("wsc", [P, 1])

        trans = [ps(f"trans{i}", [P, 4, P]) for i in range(2)]
        small = [ps(f"small{i}", [P, 512]) for i in range(2)]
        big = [ps(f"big{i}", [P, 1024]) for i in range(2)]

        w_nat = X[:, :, :].rearrange("p (w o) c -> p w o c", w=4)
        zero16 = KZ[:, 0:ROW // 2]
        zero32 = K[:, 2, :]

        setup_loaded, setup_loaded2 = sem("setup_loaded"), sem("setup_loaded2")
        consts, zeros_ready = sem("consts"), sem("zeros_ready")
        x_loaded, ctx_loaded, mask_loaded, w_loaded = sem("x_loaded"), sem("ctx_loaded"), sem("mask_loaded"), sem("w_loaded")
        rows_stored, acc_stored = sem("rows_stored"), sem("acc_stored")
        trans_ready, trans_copied = sem("trans_ready"), sem("trans_copied")
        small_ready, small_free = sem("small_ready"), sem("small_free")
        lnbb_ready, woT_ready = sem("lnbb_ready"), sem("woT_ready")
        vx_loaded, mask_ready, pool_step = sem("vx_loaded"), sem("mask_ready"), sem("pool_step")
        qkv_ready, qk_ready, v_ready = sem("qkv_ready"), sem("qk_ready"), sem("v_ready")
        qm_ready, qs_ready, qe_ready, kmx_ready = sem("qm_ready"), sem("qs_ready"), sem("qe_ready"), sem("kmx_ready")
        km2_ready, kdiag_ready, ks_ready, ke_ready = sem("km2_ready"), sem("kdiag_ready"), sem("ks_ready"), sem("ke_ready")
        rst_ready = sem("rst_ready")
        rden_ready, o_ready = sem("rden_ready"), sem("o_ready")
        xc_ready = sem("xc_ready")
        stat_ready, mv_ready, ve_ready, rstd_ready = sem("stat_ready"), sem("mv_ready"), sem("ve_ready"), sem("rstd_ready")
        z_ready, x1_ready = sem("z_ready"), sem("x1_ready")
        lg_ready, xm_ready, xmb_ready, s_ready, p_ready = sem("lg_ready"), sem("xm_ready"), sem("xmb_ready"), sem("s_ready"), sem("p_ready")
        xr8_ready, r2_ready, x2_ready = sem("xr8_ready"), sem("r2_ready"), sem("x2_ready")
        hi_ready, lo_ready = sem("hi_ready"), sem("lo_ready")
        L_ready, route_step, le_shift, le_ready, gates_ready = sem("L_ready"), sem("route_step"), sem("le_shift"), sem("le_ready"), sem("gates_ready")
        wmx_ready, wall_ready, wstep, wsc_ready, whi_ready, w_split = (
            sem("wmx_ready"), sem("wall_ready"), sem("wstep"), sem("wsc_ready"), sem("whi_ready"), sem("w_split"))

        passed = {e: sem(f"passed_{i}") for i, e in enumerate((nc.gpsimd, nc.scalar, nc.vector))}

        x_in = x.rearrange("b (t p) c -> b p t c", p=P)
        rows_out = rows[0:B * N, :].rearrange("(b t p) r -> b p t r", p=P, t=TB)
        acc_out = acc[0:B * N, :].rearrange("(b t p) c -> b p t c", p=P, t=TB)
        up_in = up.rearrange("e (c p) h -> e p c h", p=P)
        down_in = down.rearrange("e (c p) d -> e p c d", p=P)

        def lone(eng):
            eng.sem_inc(passed[eng], 1)

        def one(ap, b):
            a = ap[bass.ds(b, 1)]
            return a.squeeze(0)

        def trans_use(stage, i):
            return stage * TB + i if stage < 3 else 3 * TB + CROSS["x1", i] if stage == 3 else 6 * TB + i

        block = st.enter_context(nc.Block())

        @block.sync
        def _(sp):
            for w, mat in enumerate((Wq, Wk, Wv, Wo)):
                sp.dma_start(w_nat[:, w, :, :], mat.rearrange("(o p) c -> p o c", p=P)).then_inc(setup_loaded, 16)
            for w, vec in enumerate((bq, bk, bv)):
                sp.dma_start(bias[:, w * C:(w + 1) * C], vec.partition_broadcast(P)).then_inc(setup_loaded2, 16)
            sp.dma_start(cvec[:, :], bo.partition_broadcast(P)).then_inc(setup_loaded2, 16)
            sp.dma_start(bcol[:, :], xb.partition_broadcast(P)).then_inc(setup_loaded2, 16)
            sp.dma_start(gb[:, 0, :], ln_g.rearrange("(c p) -> p c", p=P), allow_slow_non_contiguous=True).then_inc(setup_loaded2, 16)
            sp.dma_start(gb[:, 1, :], ln_b.rearrange("(c p) -> p c", p=P), allow_slow_non_contiguous=True).then_inc(setup_loaded2, 16)
            sp.dma_start(rw[:, :, :], router.rearrange("(c p) e -> p c e", p=P)).then_inc(setup_loaded2, 16)
            sp.dma_start(ctx_sb[:, :], ctx[0, :, 0:C]).then_inc(ctx_loaded, 16)
            sp.dma_start(mint[:, :], mask[0:1, :]).then_inc(mask_loaded, 16)
            sp.dma_start(W8[:, :].rearrange("p (c h) -> p c h", c=CC), up_in[0]).then_inc(w_loaded, 16)
            def load_values(of_batch):
                for c, p, h, key, n in SEGMENTS:
                    sp.dma_start(vx[p:p + n, c, h - SPAN[c][0], 0:XD], of_batch[key:key + n, C + h * XD:C + (h + 1) * XD]).then_inc(vx_loaded, 16)

            sp.wait_ge(consts, CONST_STEPS)
            load_values(ctx[0])
            sp.wait_ge(zeros_ready, 2)
            for j in range(SB):
                sp.dma_start(rows[B * N + j * P:B * N + (j + 1) * P, :], zero16).then_inc(rows_stored, 16)
                sp.dma_start(acc[B * N + j * P:B * N + (j + 1) * P, :], zero32).then_inc(acc_stored, 16)
            sp.wait_ge(trans_ready, TRANS_SETUP)
            sp.dma_start(X[:, :, :], x_in[0]).then_inc(x_loaded, 16)

            def next_piece(b, q):
                sp.wait_ge(w_split, PIECES * b + (q + 1))
                e, src = 2 * b + (q + 1) // 2, (up_in, down_in)[(q + 1) % 2]
                piece = one(src, e) if not isinstance(e, int) else src[e]
                sp.dma_start(W8[:, :].rearrange("p (c h) -> p c h", c=piece.shape[1]), piece).then_inc(w_loaded, 16)

            def store(b):
                sp.wait_ge(x2_ready, TB * b + TB)
                sp.dma_start(acc_out[b] if isinstance(b, int) else one(acc_out, b), Q[:, :, :]).then_inc(acc_stored, 16)
                sp.wait_ge(hi_ready, TB * b + TB)
                sp.wait_ge(lo_ready, TB * b + TB)
                sp.wait_ge(gates_ready, b + 1)
                sp.dma_start(rows_out[b] if isinstance(b, int) else one(rows_out, b),
                             KZ[:, :].rearrange("p (t r) -> p t r", t=TB)).then_inc(rows_stored, 16)

            with sp.Fori(0, B - 1) as b:
                for q in range(PIECES):
                    next_piece(b, q)
                sp.wait_ge(small_free, SMALL_SETUP + SMALL_BATCH * b + 2 * CC + 2 + 2 * TB)
                sp.dma_start(X[:, :, :], one(x_in, b + 1)).then_inc(x_loaded, 16)
                sp.dma_start(ctx_sb[:, :], one(ctx, b + 1)[:, 0:C]).then_inc(ctx_loaded, 16)
                sp.wait_ge(mask_ready, b + 1)
                sp.dma_start(mint[:, :], mask[bass.ds(b + 1, 1), :]).then_inc(mask_loaded, 16)
                store(b)
                load_values(one(ctx, b + 1))
            for q in range(PIECES - 1):
                next_piece(B - 1, q)
            store(B - 1)
            sp.wait_ge(acc_stored, 16 * (SB + B))
            sp.wait_ge(rows_stored, 16 * (SB + B))

        @block.gpsimd
        def _(pool):
            steps = [0]

            def done(ins):
                steps[0] += 1
                ins.then_inc(consts, 1)
                pool.wait_ge(consts, steps[0])

            done(pool.memset(ident[:, :], 0.0))
            done(pool.affine_select(out=ident[:, :], in_=ident[:, :], compare_op=ALU.not_equal, fill=1.0,
                                    base=0, pattern=[[-1, P]], channel_multiplier=1))
            done(pool.memset(ones[:, :], 1.0))
            pool.memset(zero16, 0.0).then_inc(zeros_ready, 1)
            pool.memset(zero32, 0.0).then_inc(zeros_ready, 1)
            done(pool.memset(nhalf[:, :], -0.5))
            done(pool.memset(one16[:, :], 1.0))
            done(pool.memset(V[:, :, :, P:P + 1], 1.0))
            done(pool.memset(vx[:, :, :, :], 0.0))
            for c, (h0, h1) in enumerate(SPAN):
                col = vx[:, c, 0:h1 - h0, XD]
                done(pool.memset(col, 1.0))
                done(pool.affine_select(out=col, in_=col, compare_op=ALU.is_ge, fill=0.0, base=c * P - h0 * KEYS,
                                        pattern=[[-KEYS, h1 - h0]], channel_multiplier=1))
                done(pool.affine_select(out=col, in_=col, compare_op=ALU.is_ge, fill=0.0, base=h0 * KEYS + KEYS - 1 - c * P,
                                        pattern=[[KEYS, h1 - h0]], channel_multiplier=-1))
            for tile, heads, d in ((hsel, XPC, XD), (bsel, HPC, LD)):
                done(pool.memset(tile[:, :], 1.0))
                done(pool.affine_select(out=tile[:, :], in_=tile[:, :], compare_op=ALU.is_ge, fill=0.0,
                                        base=0, pattern=[[-d, heads]], channel_multiplier=1))
                done(pool.affine_select(out=tile[:, :], in_=tile[:, :], compare_op=ALU.is_ge, fill=0.0,
                                        base=d - 1, pattern=[[d, heads]], channel_multiplier=-1))
            for c in range(CC):
                done(pool.tensor_copy(state[:, c, P:P + HPC], bsel[:, :]))
            done(pool.memset(lower[:, :, :], 1.0))
            done(pool.affine_select(out=lower[:, :, :], in_=lower[:, :, :], compare_op=ALU.is_gt, fill=0.0,
                                    base=0, pattern=[[1, EXP], [-1, EXP]], channel_multiplier=0))

            assert steps[0] == CONST_STEPS

            def all_max(b, q):
                pool.wait_ge(wmx_ready, PIECES * b + (q + 1))
                lone(pool)
                pool.partition_all_reduce(wall[:, :], wmx[:, :], P, ABSMAX).then_inc(wall_ready, 1)

            def inverse_deviation(b, kind, i):
                n = 3 * TB * b + TB * kind + i + 1
                pool.wait_ge(mv_ready, n)
                lone(pool)
                pool.tensor_scalar(ve[:, kind, i:i + 1], mv[:, kind, i, 1:2], LN_EPS, None, ALU.add).then_inc(ve_ready, 1)
                pool.wait_ge(ve_ready, n)
                pool.tensor_tensor(rstd[:, kind, i:i + 1], ve[:, kind, i:i + 1], nhalf[:, 0:1], ALU.pow).then_inc(rstd_ready, 1)

            with pool.Fori(0, B) as b:
                pool.wait_ge(mask_loaded, 16 * b + 16)
                lone(pool)
                pool.tensor_scalar(mrow[:, :], mint[:, :], -1.0, 1.0, ALU.mult, ALU.add).then_inc(pool_step, 1)
                pool.wait_ge(pool_step, 1 + b)
                lone(pool)
                for h in range(XPC):
                    ins = pool.tensor_scalar(mbf[:, h, :], mrow[:, :], MASKED, None, ALU.mult)
                ins.then_inc(mask_ready, 1)
                for i in range(TB):
                    if i == 0:
                        pool.wait_ge(small_free, SMALL_SETUP)
                    pool.wait_ge(trans_ready, TRANS_SETUP + TRANS_BATCH * b + i + 1)
                    pool.tensor_tensor(X[:, i, :], X[:, i, :], cvec[:, :], ALU.add).then_inc(xc_ready, 1)
                    if i in (0, 6):
                        all_max(b, i // 6)
                for kind in (0, 1):
                    for i in range(TB):
                        if kind == 1 and i == 0:
                            all_max(b, 2)
                        inverse_deviation(b, kind, i)
                all_max(b, 3)
                for i in range(TB + 1):
                    if i < TB:
                        pool.wait_ge(small_free, SMALL_SETUP + SMALL_BATCH * b + 2 * CC + 2 + 2 * TB + i + 1)
                        pool.tensor_tensor(Q[:, i, :].rearrange("p (c d) -> p c d", c=CC), Q[:, i, :].rearrange("p (c d) -> p c d", c=CC),
                                           V[:, i, :, 0:P], ALU.add).then_inc(r2_ready, 1)
                    if i >= 1:
                        inverse_deviation(b, 2, i - 1)

        @block.scalar
        def _(act):
            for w in range(4):
                for o in range(CC):
                    use = w * CC + o
                    act.wait_ge(trans_ready, use + 1)
                    dst = wqkv[:, :, w * C + o * P:w * C + (o + 1) * P] if w < 3 else woT[:, :, o * P:(o + 1) * P]
                    act.activation(dst, trans[use % 2][:, 0:CC, :], ACT.Copy).then_inc(trans_copied, 1)

            def copy_stage(b, stage, i, scale=1.0):
                s = trans_use(stage, i)
                act.wait_ge(trans_ready, TRANS_SETUP + TRANS_BATCH * b + s + 1)
                act.activation(tT[:, i % 2, :, :], trans[s % 2][:, 0:CC, :], ACT.Copy, scale=scale).then_inc(trans_copied, 1)

            def copy_probs(b, part, j):
                s = 3 * TB + CROSS[part, j]
                act.wait_ge(trans_ready, TRANS_SETUP + TRANS_BATCH * b + s + 1)
                rows_, at, n = (P, 0, 4) if part == "pa" else (FLAT - 4 * P, 4, 1)
                act.activation(pT[0:rows_, j % 2, at:at + n, :], trans[s % 2][0:rows_, 0:n, :], ACT.Copy).then_inc(trans_copied, 1)

            def split_high(b, q):
                act.wait_ge(wsc_ready, PIECES * b + (q + 1))
                wt = (k["wu"], k["wd"])[q % 2]
                dst = wt[:, bass.ds(2 * b + q // 2, 1), 0, :, :].rearrange("p e c h -> p (e c h)")
                lone(act)
                act.activation(dst, W8[:, :], ACT.Copy, scale=wsc[:, 0:1]).then_inc(whi_ready, 1)

            with act.Fori(0, B) as b:
                for i in range(TB + 2):
                    if i < TB:
                        copy_stage(b, 0, i)
                    if i >= 2:
                        act.wait_ge(qs_ready, TB * b + i - 1)
                        act.activation(Q[:, i - 2, :], Q[:, i - 2, :], ACT.Exp).then_inc(qe_ready, 1)
                    if i == 3:
                        split_high(b, 0)
                for g in range(2):
                    if g == 0:
                        act.wait_ge(ks_ready, b + 1)
                    else:
                        act.wait_ge(small_free, SMALL_SETUP + SMALL_BATCH * b + CC + 2)
                    act.activation(K[:, g * 4:g * 4 + 4, :], K[:, g * 4:g * 4 + 4, :], ACT.Exp).then_inc(ke_ready, 1)
                split_high(b, 1)
                for i in range(TB):
                    copy_stage(b, 1, i)
                for i in range(TB):
                    copy_stage(b, 2, i)
                    if i == 4:
                        split_high(b, 2)
                for i in range(TB + 4):
                    if i < TB:
                        copy_stage(b, 3, i, XD ** -0.5)
                    if i == 5:
                        split_high(b, 3)
                    if 0 <= i - 3 < TB:
                        copy_probs(b, "pa", i - 3)
                        copy_probs(b, "pb", i - 3)
                    if 2 <= i < TB + 2:
                        act.wait_ge(s_ready, TB * b + i - 1)
                        act.activation(pr[:, (i - 2) % 2, :, :], pr[:, (i - 2) % 2, :, :], ACT.Exp).then_inc(p_ready, 1)
                for i in range(TB):
                    copy_stage(b, 4, i)
                    act.activation(XR[:, i, 0:C], Q[:, i, :], ACT.Copy, scale=XSCALE).then_inc(hi_ready, 1)
                act.wait_ge(le_shift, b + 1)
                act.activation(le[:, :, :], le[:, :, :], ACT.Exp).then_inc(le_ready, 1)

        @block.vector
        def _(dve):
            def small_wait(b, s):
                dve.wait_ge(small_ready, SMALL_SETUP + SMALL_BATCH * b + s + 1)
                return small[(SMALL_SETUP + s) % 2]

            dve.wait_ge(setup_loaded2, 16 * 8)
            dve.wait_ge(consts, CONST_STEPS)
            for c in range(CC):
                dve.tensor_scalar(kdiag[:, c, :], ones[:, :], gb[:, 1, c:c + 1], None, ALU.mult).then_inc(lnbb_ready, 1)
            for c in range(CC):
                dve.wait_ge(small_ready, c + 1)
                dve.tensor_tensor(cvec[:, c * P:(c + 1) * P], small[c][:, 0:P], cvec[:, c * P:(c + 1) * P], ALU.add).then_inc(small_free, 1)
            for c in range(CC):
                dve.tensor_scalar(woT[:, c, :], woT[:, c, :], gb[:, 0, c:c + 1], None, ALU.mult).then_inc(woT_ready, 1)

            def abs_max(b, q):
                dve.wait_ge(w_loaded, 16 * (PIECES * b + q + 1))
                dve.tensor_reduce(wmx[:, :], W8[:, :], AX_X, ALU.max, apply_absolute_value=True).then_inc(wmx_ready, 1)

            def scale(b, q):
                n = PIECES * b + q
                at = k["wpow"][:, bass.ds(n, 1)]
                dve.wait_ge(wall_ready, n + 1)
                dve.tensor_scalar(wcl[:, :], wall[:, :], 1e-30, None, ALU.max).then_inc(wstep, 1)
                dve.wait_ge(wstep, 3 * n + 1)
                dve.tensor_scalar(wcl[:, :].bitcast(I32), wcl[:, :].bitcast(I32), EXPONENT, None, ALU.bitwise_and).then_inc(wstep, 1)
                dve.wait_ge(wstep, 3 * n + 2)
                dve.tensor_copy(at, wcl[:, :])
                dve.reciprocal(wrp[:, :], wcl[:, :]).then_inc(wstep, 1)
                dve.wait_ge(wstep, 3 * n + 3)
                dve.tensor_scalar(wsc[:, :], wrp[:, :], WTARGET, None, ALU.mult).then_inc(wsc_ready, 1)

            def split_low(b, q):
                wt = (k["wu"], k["wd"])[q % 2]
                at = wt[:, bass.ds(2 * b + q // 2, 1), :, :, :].rearrange("p e s c h -> p s (e c h)")
                dve.wait_ge(whi_ready, PIECES * b + q + 1)
                dve.scalar_tensor_tensor(out=at[:, 1, :], in0=W8[:, :], scalar=wsc[:, 0:1], in1=at[:, 0, :],
                                         op0=ALU.mult, op1=ALU.subtract).then_inc(w_split, 1)

            def stats(b, kind, i, src):
                n = 3 * TB * b + TB * kind + i
                dve.bn_stats(stat[:, i % 2, :], src).then_inc(stat_ready, 1)
                dve.wait_ge(stat_ready, n + 1)
                lone(dve)
                dve.bn_aggr(mv[:, kind, i, :], stat[:, i % 2, :]).then_inc(mv_ready, 1)

            def norm(b, kind, i, tile, ready):
                dve.wait_ge(rstd_ready, 3 * TB * b + TB * kind + i + 1)
                dve.tensor_scalar(tile, tile, mv[:, kind, i, 0:1], rstd[:, kind, i:i + 1], ALU.subtract, ALU.mult).then_inc(ready, 1)

            with dve.Fori(0, B) as b:
                for c in range(CC):
                    kt = small_wait(b, c)
                    dve.tensor_tensor(kbd[:, c, :, :], kt[:, 0:KEYS].unsqueeze(1).to_broadcast([P, XPC, KEYS]),
                                      hsel[:, :].unsqueeze(2).to_broadcast([P, XPC, KEYS]), ALU.mult).then_inc(small_free, 1)
                dve.wait_ge(rows_stored, 16 * (SB + b))
                dve.wait_ge(acc_stored, 16 * (SB + b))
                for i in range(TB):
                    n = TB * b + i
                    if i in (0, 6):
                        abs_max(b, i // 6)
                    if i == 3:
                        split_low(b, 0)
                    src = big[i % 2]
                    dve.wait_ge(qkv_ready, n + 1)
                    dve.tensor_tensor(Q[:, i, :], src[:, 0:C], bias[:, 0:C], ALU.add).then_inc(qk_ready, 1)
                    dve.tensor_tensor(K[:, i, :], src[:, C:2 * C], bias[:, C:2 * C], ALU.add).then_inc(qk_ready, 1)
                    dve.tensor_tensor(V[:, i, :, 0:P], src[:, 2 * C:3 * C].rearrange("p (c d) -> p c d", c=CC),
                                      bias[:, 2 * C:3 * C].rearrange("p (c d) -> p c d", c=CC), ALU.add).then_inc(v_ready, 1)
                    q3 = Q[:, i, :].rearrange("p (h d) -> p h d", h=LH)
                    dve.wait_ge(qk_ready, 2 * n + 2)
                    dve.tensor_reduce(qm[:, i % 2, :], q3, AX_X, ALU.max).then_inc(qm_ready, 1)
                    if i == 0:
                        dve.tensor_copy(kmx[:, :], K[:, 0, :]).then_inc(kmx_ready, 1)
                    else:
                        dve.wait_ge(kmx_ready, n)
                        dve.tensor_tensor(kmx[:, :], kmx[:, :], K[:, i, :], ALU.max).then_inc(kmx_ready, 1)
                    dve.wait_ge(qm_ready, n + 1)
                    dve.tensor_tensor(q3, q3, qm[:, i % 2, :].unsqueeze(2).to_broadcast([P, LH, LD]), ALU.subtract).then_inc(qs_ready, 1)
                    if i in (1, 7):
                        scale(b, i // 6)
                km = small_wait(b, CC)
                dve.tensor_reduce(km2[:, :], km[:, 0:C].rearrange("p (c t) -> p c t", c=CC), AX_X, ALU.max).then_inc(small_free, 1)
                dve.wait_ge(small_free, SMALL_SETUP + SMALL_BATCH * b + CC + 1)
                for c in range(CC):
                    dve.tensor_scalar(kdiag[:, c, :], ident[:, :], km2[:, c:c + 1], None, ALU.mult).then_inc(kdiag_ready, 1)
                kb = small_wait(b, CC + 1)
                for g in range(2):
                    dve.tensor_tensor(K[:, 4 * g:4 * g + 4, :], K[:, 4 * g:4 * g + 4, :],
                                      kb[:, 0:C].unsqueeze(1).to_broadcast([P, 4, C]), ALU.subtract
                                      ).then_inc((ks_ready, small_free)[g], 1)
                split_low(b, 1)
                for c in range(CC):
                    sp_ = small_wait(b, CC + 2 + c)
                    dve.reciprocal(rst[:, c:c + 1], sp_[:, P:P + 1]).then_inc(rst_ready, 1)
                    dve.wait_ge(rst_ready, CC * b + c + 1)
                    dve.scalar_tensor_tensor(out=state[:, c, 0:P].rearrange("p (h d) -> p h d", h=HPC),
                                             in0=sp_[:, 0:P].rearrange("p (h d) -> p h d", h=HPC), scalar=rst[:, c:c + 1],
                                             in1=bsel[:, :].unsqueeze(2).to_broadcast([P, HPC, LD]),
                                             op0=ALU.mult, op1=ALU.mult).then_inc(small_free, 1)
                for i in range(TB + 1):
                    if i < TB:
                        n = TB * b + i
                        s = 2 * CC + 2 + i
                        o = small_wait(b, s)[:, 0:CC * (P + HPC)].rearrange("p (c m) -> p c m", c=CC)
                        rd = rden[:, i % 2, :].rearrange("p (c h) -> p c h", c=CC)
                        dve.reciprocal(rd, o[:, :, P:P + HPC]).then_inc(rden_ready, 1)
                        dve.wait_ge(rden_ready, n + 1)
                        dve.tensor_tensor(K[:, i, :].rearrange("p (c h d) -> p c h d", c=CC, h=HPC),
                                          o[:, :, 0:P].rearrange("p c (h d) -> p c h d", h=HPC),
                                          rd.unsqueeze(3).to_broadcast([P, CC, HPC, LD]), ALU.mult).then_inc(small_free, 1)
                        dve.wait_ge(small_free, SMALL_SETUP + SMALL_BATCH * b + s + 1)
                        stats(b, 0, i, K[:, i, :])
                    if i >= 1:
                        norm(b, 0, i - 1, K[:, i - 1, :], z_ready)
                for i in range(TB + 1):
                    if i == 0:
                        abs_max(b, 2)
                    if i == 2:
                        scale(b, 2)
                    if i == 5:
                        split_low(b, 2)
                    if i < TB:
                        n = TB * b + i
                        y = small_wait(b, 2 * CC + 2 + TB + i)
                        dve.wait_ge(xc_ready, n + 1)
                        dve.tensor_tensor(V[:, i, :, 0:P], y[:, 0:C].rearrange("p (c d) -> p c d", c=CC),
                                          X[:, i, :].rearrange("p (c d) -> p c d", c=CC), ALU.add).then_inc(small_free, 1)
                        dve.wait_ge(small_free, SMALL_SETUP + SMALL_BATCH * b + 2 * CC + 2 + TB + i + 1)
                        stats_src = V[:, i, :, 0:P]
                        dve.bn_stats(stat[:, i % 2, :], stats_src).then_inc(stat_ready, 1)
                        dve.wait_ge(stat_ready, 3 * TB * b + TB + i + 1)
                        lone(dve)
                        dve.bn_aggr(mv[:, 1, i, :], stat[:, i % 2, :]).then_inc(mv_ready, 1)
                    if i >= 1:
                        norm(b, 1, i - 1, V[:, i - 1, :, 0:P], x1_ready)
                for i in range(TB + 3):
                    if i == 1:
                        abs_max(b, 3)
                    if i == 3:
                        scale(b, 3)
                    if i == 6:
                        split_low(b, 3)
                    if i < TB:
                        n = TB * b + i
                        lg = big[i % 2][:, LOGIT0:LOGIT0 + XH * KEYS].rearrange("p (h k) -> p h k", h=XH)
                        dve.wait_ge(lg_ready, n + 1)
                        dve.tensor_reduce(xm[:, i % 2, :], lg, AX_X, ALU.max).then_inc(xm_ready, 1)
                        dve.wait_ge(xm_ready, n + 1)
                        dve.tensor_scalar(xmb[:, i % 2, :], xm[:, i % 2, :], bcol[:, 0:1], None, ALU.add).then_inc(xmb_ready, 1)
                        dve.wait_ge(xmb_ready, n + 1)
                        dve.scalar_tensor_tensor(out=pr[:, i % 2, :, :], in0=lg, scalar=bcol[:, 0:1],
                                                 in1=xmb[:, i % 2, :].unsqueeze(2).to_broadcast([P, XH, KEYS]),
                                                 op0=ALU.add, op1=ALU.subtract).then_inc(s_ready, 1)
                    j = i - 3
                    if j >= 0:
                        n = TB * b + j
                        s = 2 * CC + 2 + 2 * TB + j
                        o = small_wait(b, s)[:, 0:XH * (XD + 1)].rearrange("p (h m) -> p h m", h=XH)
                        dve.reciprocal(xr8[:, j % 2, :].unsqueeze(2), o[:, :, XD:XD + 1]).then_inc(xr8_ready, 1)
                        dve.wait_ge(xr8_ready, n + 1)
                        dve.tensor_tensor(Q[:, j, :].rearrange("p (h d) -> p h d", h=XH), o[:, :, 0:XD],
                                          xr8[:, j % 2, :].unsqueeze(2).to_broadcast([P, XH, XD]), ALU.mult).then_inc(small_free, 1)
                    if j >= 1:
                        dve.wait_ge(r2_ready, TB * b + j)
                        stats(b, 2, j - 1, Q[:, j - 1, :])
                    if j >= 2:
                        norm(b, 2, j - 2, Q[:, j - 2, :], x2_ready)
                dve.wait_ge(r2_ready, TB * b + TB)
                stats(b, 2, TB - 1, Q[:, TB - 1, :])
                norm(b, 2, TB - 2, Q[:, TB - 2, :], x2_ready)
                norm(b, 2, TB - 1, Q[:, TB - 1, :], x2_ready)
                for i in range(TB):
                    n = TB * b + i
                    dve.wait_ge(hi_ready, n + 1)
                    dve.scalar_tensor_tensor(out=XR[:, i, C:2 * C], in0=Q[:, i, :], scalar=XSCALE, in1=XR[:, i, 0:C],
                                             op0=ALU.mult, op1=ALU.subtract).then_inc(lo_ready, 1)
                    s = 2 * CC + 2 + 3 * TB + i
                    lg8 = small_wait(b, s)
                    dve.tensor_copy(L[:, i, :], lg8[:, 0:EXP]).then_inc(small_free, 1)
                dve.wait_ge(small_free, SMALL_SETUP + SMALL_BATCH * b + SMALL_BATCH)
                lj = L[:, :, :].unsqueeze(2).to_broadcast([P, TB, EXP, EXP])
                le_ = L[:, :, :].unsqueeze(3).to_broadcast([P, TB, EXP, EXP])
                r0 = 9 * b
                dve.tensor_reduce(lm[:, :], L[:, :, :], AX_X, ALU.max).then_inc(route_step, 1)
                dve.tensor_tensor(cmpa[:, :, :, :], lj, le_, ALU.is_gt).then_inc(route_step, 1)
                dve.tensor_tensor(cmpb[:, :, :, :], lj, le_, ALU.is_equal).then_inc(route_step, 1)
                dve.wait_ge(route_step, r0 + 1)
                dve.tensor_tensor(le[:, :, :], L[:, :, :], lm[:, :].unsqueeze(2).to_broadcast([P, TB, EXP]), ALU.subtract).then_inc(le_shift, 1)
                dve.wait_ge(route_step, r0 + 3)
                dve.tensor_tensor(cmpb[:, :, :, :], cmpb[:, :, :, :], lower[:, :, :].unsqueeze(1).to_broadcast([P, TB, EXP, EXP]), ALU.mult).then_inc(route_step, 1)
                dve.wait_ge(route_step, r0 + 4)
                dve.tensor_tensor(cmpa[:, :, :, :], cmpa[:, :, :, :], cmpb[:, :, :, :], ALU.add).then_inc(route_step, 1)
                dve.wait_ge(route_step, r0 + 5)
                dve.tensor_reduce(rk[:, :, :], cmpa[:, :, :, :], AX_X, ALU.add).then_inc(route_step, 1)
                dve.wait_ge(route_step, r0 + 6)
                dve.tensor_copy(k["rank"][:, :, bass.ds(TB * b, TB)].rearrange("p e t -> p t e"), rk[:, :, :])
                dve.wait_ge(le_ready, b + 1)
                dve.scalar_tensor_tensor(out=le[:, :, :], in0=rk[:, :, :], scalar=float(TOPK), in1=le[:, :, :],
                                         op0=ALU.is_lt, op1=ALU.mult).then_inc(route_step, 1)
                dve.wait_ge(route_step, r0 + 7)
                dve.tensor_reduce(gsum[:, 0, :], le[:, :, :], AX_X, ALU.add).then_inc(route_step, 1)
                dve.wait_ge(route_step, r0 + 8)
                dve.reciprocal(gsum[:, 1, :], gsum[:, 0, :]).then_inc(route_step, 1)
                dve.wait_ge(route_step, r0 + 9)
                dve.tensor_tensor(XR[:, :, 2 * C:ROW].bitcast(F32), le[:, :, :],
                                  gsum[:, 1, :].unsqueeze(2).to_broadcast([P, TB, EXP]), ALU.mult).then_inc(gates_ready, 1)

        @block.tensor
        def _(pe):
            pe.wait_ge(consts, CONST_STEPS)
            pe.wait_ge(setup_loaded, 16 * 4)
            for w in range(4):
                for o in range(CC):
                    use = w * CC + o
                    if use >= 2:
                        pe.wait_ge(trans_copied, use - 1)
                    for c in range(CC):
                        ins = pe.transpose(trans[use % 2][:, c, :], w_nat[:, w, o, c * P:(c + 1) * P], ident[:, :])
                    ins.then_inc(trans_ready, 1)
            pe.wait_ge(trans_copied, TRANS_SETUP)
            pe.wait_ge(lnbb_ready, CC)
            for half in range(CC):
                for c in range(CC):
                    ins = pe.matmul(small[half][:, 0:P], kdiag[:, c, :], woT[:, c, half * P:(half + 1) * P],
                                    start=(c == 0), stop=(c == CC - 1))
                ins.then_inc(small_ready, 1)

            with pe.Fori(0, B) as b:
                def trans_stage(stage, i, src):
                    s = trans_use(stage, i)
                    pe.wait_ge(trans_copied, TRANS_SETUP + TRANS_BATCH * b + s - 1)
                    for c in range(CC):
                        ins = pe.transpose(trans[s % 2][:, c, :], src(c), ident[:, :])
                    ins.then_inc(trans_ready, 1)

                def copied(stage, i):
                    pe.wait_ge(trans_copied, TRANS_SETUP + TRANS_BATCH * b + trans_use(stage, i) + 1)
                    return tT[:, i % 2, :, :]

                def small_slot(s):
                    pe.wait_ge(small_free, SMALL_SETUP + SMALL_BATCH * b + s - 1)
                    return small[(SMALL_SETUP + s) % 2]

                pe.wait_ge(ctx_loaded, 16 * b + 16)
                for c in range(CC):
                    pe.transpose(small_slot(c)[:, 0:KEYS], ctx_sb[:, c * P:(c + 1) * P], ident[0:KEYS, 0:KEYS]).then_inc(small_ready, 1)
                pe.wait_ge(x_loaded, 16 * b + 16)
                for i in range(TB + 1):
                    if i < TB:
                        trans_stage(0, i, lambda c: X[:, i, c * P:(c + 1) * P])
                    if i >= 1:
                        j = i - 1
                        xT = copied(0, j)
                        if j >= 2:
                            pe.wait_ge(v_ready, TB * b + j - 1)
                        for c in range(CC):
                            pe.matmul(big[j % 2][:, 0:2 * C], xT[:, c, :], wqkv[:, c, 0:2 * C], start=(c == 0), stop=(c == CC - 1))
                        for c in range(CC):
                            ins = pe.matmul(big[j % 2][:, 2 * C:3 * C], xT[:, c, :], wqkv[:, c, 2 * C:3 * C], start=(c == 0), stop=(c == CC - 1))
                        ins.then_inc(qkv_ready, 1)
                pe.wait_ge(kmx_ready, TB * b + TB)
                km = small_slot(CC)
                for c in range(CC):
                    ins = pe.transpose(km[:, c * P:(c + 1) * P], kmx[:, c * P:(c + 1) * P], ident[:, :])
                ins.then_inc(small_ready, 1)
                pe.wait_ge(kdiag_ready, CC * b + CC)
                pe.matmul(small_slot(CC + 1)[:, 0:C], ones[:, :], kdiag[:, :, :].rearrange("p c t -> p (c t)"),
                          start=True, stop=True).then_inc(small_ready, 1)
                pe.wait_ge(v_ready, TB * b + TB)
                for c in range(CC):
                    dst = small_slot(CC + 2 + c)
                    for i in range(TB):
                        if c == 0 and i % 4 == 0:
                            pe.wait_ge(ke_ready, 2 * b + i // 4 + 1)
                        ins = pe.matmul(dst[:, 0:P + 1], K[:, i, c * P:(c + 1) * P], V[:, i, c, :], start=(i == 0), stop=(i == TB - 1))
                    ins.then_inc(small_ready, 1)
                for i in range(TB + 1):
                    if i < TB:
                        pe.wait_ge(qe_ready, TB * b + i + 1)
                        trans_stage(1, i, lambda c: Q[:, i, c * P:(c + 1) * P])
                    if i >= 1:
                        j = i - 1
                        qT = copied(1, j)
                        if j == 0:
                            pe.wait_ge(small_free, SMALL_SETUP + SMALL_BATCH * b + 2 * CC + 2)
                        dst = small_slot(2 * CC + 2 + j)
                        for c in range(CC):
                            ins = pe.matmul(dst[:, c * (P + HPC):(c + 1) * (P + HPC)], qT[:, c, :], state[:, c, :], start=True, stop=True)
                        ins.then_inc(small_ready, 1)
                for i in range(TB + 1):
                    if i < TB:
                        pe.wait_ge(z_ready, TB * b + i + 1)
                        trans_stage(2, i, lambda c: K[:, i, c * P:(c + 1) * P])
                    if i >= 1:
                        j = i - 1
                        zT = copied(2, j)
                        if j == 0:
                            pe.wait_ge(woT_ready, CC)
                        dst = small_slot(2 * CC + 2 + TB + j)
                        for c in range(CC):
                            ins = pe.matmul(dst[:, 0:C], zT[:, c, :], woT[:, c, :], start=(c == 0), stop=(c == CC - 1))
                        ins.then_inc(small_ready, 1)
                pe.wait_ge(small_free, SMALL_SETUP + SMALL_BATCH * b + CC)
                pe.wait_ge(mask_ready, b + 1)
                pe.wait_ge(vx_loaded, 16 * len(SEGMENTS) * (b + 1))
                for i in range(TB + 4):
                    if i < TB:
                        pe.wait_ge(x1_ready, TB * b + i + 1)
                        trans_stage(3, i, lambda c: V[:, i, c, 0:P])
                    j = i - 3
                    if 0 <= j < TB:
                        pe.wait_ge(p_ready, TB * b + j + 1)
                        flat = pr[:, j % 2, :, :].rearrange("p h k -> p (h k)")
                        for part, chunks in (("pa", range(4)), ("pb", range(4, FCH))):
                            s = 3 * TB + CROSS[part, j]
                            pe.wait_ge(trans_copied, TRANS_SETUP + TRANS_BATCH * b + s - 1)
                            for c in chunks:
                                n = min(P, FLAT - c * P)
                                ins = pe.transpose(trans[s % 2][0:n, c % 4, :], flat[:, c * P:c * P + n], ident[:, :])
                            ins.then_inc(trans_ready, 1)
                    j = i - 1
                    if 0 <= j < TB:
                        x1T = copied(3, j)
                        if j >= 2:
                            pe.wait_ge(s_ready, TB * b + j - 1)
                        for c in range(CC):
                            dst = big[j % 2][:, LOGIT0 + c * XPC * KEYS:LOGIT0 + (c + 1) * XPC * KEYS]
                            pe.matmul(dst, x1T[:, c, :], kbd[:, c, :, :].rearrange("p h k -> p (h k)"), start=True, stop=False)
                            ins = pe.matmul(dst, one16[:, :], mbf[:, :, :].rearrange("p h k -> p (h k)"), start=False, stop=True)
                        ins.then_inc(lg_ready, 1)
                    j = i - 4
                    if 0 <= j < TB:
                        pe.wait_ge(trans_copied, TRANS_SETUP + TRANS_BATCH * b + 3 * TB + CROSS["pb", j] + 1)
                        dst = small_slot(2 * CC + 2 + 2 * TB + j)
                        for c, (h0, h1) in enumerate(SPAN):
                            n = min(P, FLAT - c * P)
                            ins = pe.matmul(dst[:, h0 * (XD + 1):h1 * (XD + 1)], pT[0:n, j % 2, c, :],
                                            vx[0:n, c, 0:h1 - h0, :].rearrange("p h d -> p (h d)"),
                                            start=(c == 0), stop=(c == FCH - 1), skip_group_check=True)
                        ins.then_inc(small_ready, 1)
                for i in range(TB + 1):
                    if i < TB:
                        pe.wait_ge(x2_ready, TB * b + i + 1)
                        trans_stage(4, i, lambda c: Q[:, i, c * P:(c + 1) * P])
                    if i >= 1:
                        j = i - 1
                        x2T = copied(4, j)
                        dst = small_slot(2 * CC + 2 + 3 * TB + j)
                        for c in range(CC):
                            ins = pe.matmul(dst[:, 0:EXP], x2T[:, c, :], rw[:, c, :], start=(c == 0), stop=(c == CC - 1))
                        ins.then_inc(small_ready, 1)


def routing(nc, k):
    st = ExitStack()
    with st:
        def sb(name, shape, dt=F32):
            return st.enter_context(nc.sbuf_tensor(name, shape, dt))

        def sem(name):
            return st.enter_context(nc.semaphore(name))

        PER = N * B // SLOTS
        HALF = NT // 2
        rank, ones, ident = k["rank"], k["ones"], k["ident"]
        chosen = sb("chosen", [P, EXP, NT])
        before = sb("before", [P, P])
        reset = sb("reset", [P, EXP, NT])
        incl = sb("incl", [P, EXP, NT])
        pos = sb("pos", [P, EXP, NT])
        picked = sb("picked", [P, NT, EXP])
        steps256 = sb("steps256", [P, PER])
        cmpt = sb("cmpt", [P, EXP, PER])
        tiles = sb("tiles", [P, EXP])
        endt = sb("endt", [P, EXP])
        start = sb("start", [P, EXP])
        posk = sb("posk", [P, TOPK, NT])
        posi = sb("posi", [P, TOPK, NT], I32)
        hii = sb("hii", [P, TOPK, NT], I32)
        loi = sb("loi", [P, TOPK, NT], I32)
        hif = sb("hif", [P, TOPK, NT], F16)
        lof = sb("lof", [P, TOPK, NT], F16)
        io = sb("io", [P, EBLOCKS], I32)
        iof = sb("iof", [P, EBLOCKS])
        values = sb("values", [P, EBLOCKS, NT], F16)
        vali = sb("vali", [P, 2, HALF], I32)
        val = sb("val", [P, NT], F16)
        padi = sb("padi", [P, EBLOCKS], I32)
        pad = sb("pad", [P, EBLOCKS])
        lo_is = sb("lo_is", [P, P, NT], F16)
        lo_hot = sb("lo_hot", [P, 2, P, NT], F16)
        hi_hot = sb("hi_hot", [P, 2, EBLOCKS, NT], F16)
        late = sb("late", [P, EBLOCKS])
        token = sb("token", [P, EBLOCKS])
        empty = sb("empty", [P, EBLOCKS])
        te = sb("te", [P, ETILES])
        past = sb("past", [P, ETILES, EXP + 1])
        hot = sb("hot", [P, ETILES, EXP])
        inv = sb("inv", [P, 2 * EXP])
        fac = sb("fac", [P, 3, EXP])
        tmp = sb("tmp", [P, ETILES, EXP])
        sum4 = sb("sum4", [P, ETILES, EXP // 2])
        sum2 = sb("sum2", [P, ETILES, EXP // 4])
        counts = st.enter_context(nc.psum_tensor("counts", [P, 512], F32))
        table = [st.enter_context(nc.psum_tensor(f"table{i}", [P, 512], F32)) for i in range(2)]

        made, dve_step, chosen_ready, counts_ready = sem("made"), sem("dve_step"), sem("chosen_ready"), sem("counts_ready")
        is_ready, hot_ready, table_step = sem("is_ready"), sem("hot_ready"), sem("table_step")
        values_ready, past_ready, fac_ready, pool_step = sem("values_ready"), sem("past_ready"), sem("fac_ready"), sem("by_tile_step")
        block = st.enter_context(nc.Block())
        MADE_FIRST, MADE = 6, 12

        @block.gpsimd
        def _(pool):
            n = [0]

            def done(ins):
                n[0] += 1
                ins.then_inc(made, 1)
                pool.wait_ge(made, n[0])

            done(pool.memset(before[:, :], 1.0))
            done(pool.affine_select(out=before[:, :], in_=before[:, :], compare_op=ALU.is_gt, fill=0.0,
                                    base=0, pattern=[[1, P]], channel_multiplier=-1))
            done(pool.iota(io[:, :], pattern=[[1, EBLOCKS]], base=0, channel_multiplier=0))
            done(pool.tensor_copy(iof[:, :], io[:, :]))
            done(pool.memset(reset[:, :, :], 1.0))
            done(pool.memset(reset[:, :, 0:1], 0.0))
            assert n[0] == MADE_FIRST
            done(pool.iota(vali[:, :, :], pattern=[[0, 2], [P, HALF]], base=1, channel_multiplier=1))
            done(pool.tensor_copy(val[:, :], vali[:, :, :].rearrange("p h t -> p (h t)")))
            done(pool.memset(past[:, :, 0:1], 1.0))
            done(pool.memset(past[:, :, EXP:EXP + 1], 0.0))
            done(pool.iota(padi[:, :].rearrange("p (t j) -> p t j", j=SB), pattern=[[0, ETILES], [P, SB]],
                           base=B * N + 1, channel_multiplier=1))
            done(pool.tensor_copy(pad[:, :], padi[:, :]))
            assert n[0] == MADE

            m = [0]

            def then(ins):
                m[0] += 1
                ins.then_inc(pool_step, 1)
                pool.wait_ge(pool_step, m[0])

            def sum_experts(dst, of):
                then(pool.tensor_tensor(sum4[:, :, :], of[:, :, 0:4], of[:, :, 4:8], ALU.add))
                then(pool.tensor_tensor(sum2[:, :, :], sum4[:, :, 0:2], sum4[:, :, 2:4], ALU.add))
                then(pool.tensor_tensor(dst, sum2[:, :, 0], sum2[:, :, 1], ALU.add))

            pool.wait_ge(past_ready, 1)
            sum_experts(te[:, :], past[:, :, 1:EXP + 1])
            then(pool.tensor_copy(k["tile_expert"][:, :], te[:, :]))
            then(pool.tensor_tensor(hot[:, :, :], past[:, :, 0:EXP], past[:, :, 1:EXP + 1], ALU.subtract))
            pool.wait_ge(fac_ready, 1)
            for f, dst in ((0, k["up_scale"]), (1, k["h_scale"])):
                then(pool.tensor_tensor(tmp[:, :, :], hot[:, :, :], fac[:, f, :].unsqueeze(1).to_broadcast([P, ETILES, EXP]), ALU.mult))
                sum_experts(dst[:, :], tmp)
            then(pool.tensor_tensor(k["pick"][:, :, :], hot[:, :, :], fac[:, 2, :].unsqueeze(1).to_broadcast([P, ETILES, EXP]), ALU.mult))

        @block.scalar
        def _(act):
            act.wait_ge(made, MADE_FIRST)
            act.activation(values[:, :, :], iof[:, :].unsqueeze(2).to_broadcast([P, EBLOCKS, NT]), ACT.Copy).then_inc(values_ready, 1)

        @block.vector
        def _(dve):
            n = [0]

            def done(ins):
                n[0] += 1
                ins.then_inc(dve_step, 1)
                dve.wait_ge(dve_step, n[0])

            dve.tensor_scalar(chosen[:, :, :], rank[:, :, :], float(TOPK), None, ALU.is_lt).then_inc(chosen_ready, 1)
            dve.wait_ge(made, MADE_FIRST)
            dve.tensor_copy(k["ident16"][:, :], ident[:, :])
            done(dve.tensor_scalar(steps256[:, :], iof[:, 0:PER], float(SLOTS), None, ALU.mult))
            done(dve.reciprocal(inv[:, :], k["wpow"][:, :]))
            wp = k["wpow"][:, :].rearrange("p (e m) -> p e m", m=2)
            iv = inv[:, :].rearrange("p (e m) -> p e m", m=2)
            done(dve.tensor_scalar(fac[:, 0, :], wp[:, :, 0], 1.0 / (XSCALE * WTARGET), None, ALU.mult))
            done(dve.tensor_scalar(fac[:, 1, :], iv[:, :, 0], WTARGET, None, ALU.mult))
            dve.scalar_tensor_tensor(out=fac[:, 2, :], in0=wp[:, :, 0], scalar=1.0 / (WTARGET * WTARGET),
                                     in1=wp[:, :, 1], op0=ALU.mult, op1=ALU.mult).then_inc(fac_ready, 1)
            dve.wait_ge(counts_ready, 1)
            prefix = counts[:, 0:EXP * NT]
            total = counts[:, EXP * NT:2 * EXP * NT]
            flat = lambda t: t[:, :, :].rearrange("p e t -> p (e t)")
            done(dve.tensor_tensor_scan(flat(incl), flat(reset), total, 0.0, ALU.mult, ALU.add))
            done(dve.tensor_tensor(cmpt[:, :, :], incl[:, :, NT - 1:NT].to_broadcast([P, EXP, PER]),
                                   steps256[:, :].unsqueeze(1).to_broadcast([P, EXP, PER]), ALU.is_gt))
            done(dve.tensor_reduce(tiles[:, :], cmpt[:, :, :], AX_X, ALU.add))
            done(dve.tensor_tensor_scan(endt[:, :], ones[:, 0:EXP], tiles[:, :], 0.0, ALU.mult, ALU.add))
            dve.tensor_tensor(past[:, :, 1:EXP], iof[:, 0:ETILES].unsqueeze(2).to_broadcast([P, ETILES, EXP - 1]),
                              endt[:, 0:EXP - 1].unsqueeze(1).to_broadcast([P, ETILES, EXP - 1]), ALU.is_ge).then_inc(past_ready, 1)
            done(dve.tensor_tensor(start[:, :], endt[:, :], tiles[:, :], ALU.subtract))
            done(dve.tensor_tensor(flat(pos), flat(incl), total, ALU.subtract))
            done(dve.tensor_tensor(flat(pos), flat(pos), prefix, ALU.add))
            done(dve.tensor_scalar(start[:, :], start[:, :], float(SLOTS), None, ALU.mult))
            done(dve.tensor_tensor(pos[:, :, :], pos[:, :, :], start[:, :].unsqueeze(2).to_broadcast([P, EXP, NT]), ALU.add))
            for j in range(TOPK):
                done(dve.scalar_tensor_tensor(out=picked[:, :, :].rearrange("p t e -> p e t"), in0=rank[:, :, :], scalar=float(j),
                                              in1=pos[:, :, :], op0=ALU.is_equal, op1=ALU.mult))
                done(dve.tensor_reduce(posk[:, j, :], picked[:, :, :], AX_X, ALU.add))
            done(dve.tensor_copy(posi[:, :, :], posk[:, :, :]))
            done(dve.tensor_scalar(hii[:, :, :], posi[:, :, :], 7, None, ALU.logical_shift_right))
            done(dve.tensor_scalar(loi[:, :, :], posi[:, :, :], P - 1, None, ALU.bitwise_and))
            done(dve.tensor_copy(hif[:, :, :], hii[:, :, :]))
            done(dve.tensor_copy(lof[:, :, :], loi[:, :, :]))
            dve.wait_ge(values_ready, 1)
            dve.wait_ge(made, MADE)
            for j in range(TOPK):
                if j >= 1:
                    dve.wait_ge(hot_ready, 2 * j)
                if j >= 2:
                    dve.wait_ge(table_step, j - 1)
                dve.tensor_tensor(lo_is[:, :, :], values[:, 0:P, :], lof[:, j, :].unsqueeze(1).to_broadcast([P, P, NT]),
                                  ALU.is_equal).then_inc(is_ready, 1)
                dve.tensor_tensor(hi_hot[:, j % 2, :, :], values[:, :, :], hif[:, j, :].unsqueeze(1).to_broadcast([P, EBLOCKS, NT]),
                                  ALU.is_equal).then_inc(hot_ready, 1)
                dve.wait_ge(is_ready, j + 1)
                dve.tensor_tensor(lo_hot[:, j % 2, :, :], lo_is[:, :, :], val[:, :].unsqueeze(1).to_broadcast([P, P, NT]),
                                  ALU.mult).then_inc(hot_ready, 1)
            dve.wait_ge(table_step, TOPK)
            done(dve.tensor_scalar(late[:, :], table[1][:, 0:EBLOCKS], 0.0, float(HALF * P), ALU.is_gt, ALU.mult))
            done(dve.tensor_tensor(late[:, :], table[1][:, 0:EBLOCKS], late[:, :], ALU.add))
            done(dve.tensor_tensor(token[:, :], table[0][:, 0:EBLOCKS], late[:, :], ALU.add))
            done(dve.scalar_tensor_tensor(out=empty[:, :], in0=token[:, :], scalar=0.0, in1=pad[:, :], op0=ALU.is_equal, op1=ALU.mult))
            done(dve.scalar_tensor_tensor(out=k["slot_row"][:, :], in0=token[:, :], scalar=-1.0, in1=empty[:, :], op0=ALU.add, op1=ALU.add))

        @block.tensor
        def _(pe):
            pe.wait_ge(made, MADE_FIRST)
            pe.wait_ge(chosen_ready, 1)
            flat = chosen[:, :, :].rearrange("p e t -> p (e t)")
            pe.matmul(counts[:, 0:EXP * NT], before[:, :], flat, start=True, stop=True)
            pe.matmul(counts[:, EXP * NT:2 * EXP * NT], ones[:, :], flat, start=True, stop=True).then_inc(counts_ready, 1)
            for j in range(TOPK):
                pe.wait_ge(hot_ready, 2 * j + 2)
                for t in range(NT):
                    ins = pe.matmul(table[t // HALF][:, 0:EBLOCKS], lo_hot[:, j % 2, :, t], hi_hot[:, j % 2, :, t],
                                    start=(j == 0 and t % HALF == 0), stop=(j == TOPK - 1 and t % HALF == HALF - 1))
                ins.then_inc(table_step, 1)


def experts(nc, k, rows, acc):
    st = ExitStack()
    with st:
        def sb(name, shape, dt=F32):
            return st.enter_context(nc.sbuf_tensor(name, shape, dt))

        def ps(name, shape, dt=F32):
            return st.enter_context(nc.psum_tensor(name, shape, dt))

        def sem(name):
            return st.enter_context(nc.semaphore(name))

        xg = sb("xg", [P, 2, SB, ROW // 2])
        xT = sb("xT", [P, 2, 2 * CC, SLOTS], F16)
        h = sb("h", [P, PAIRS, 2 * SLOTS])
        hh = sb("hh", [P, 2, HC, SLOTS], F16)
        hl = sb("hl", [P, 2, HC, SLOTS], F16)
        y = sb("y", [P, 2, SB, C])
        gp = sb("gp", [P, 2, SB, EXP])
        gate = sb("gate", [P, ETILES * SB])
        psx = [ps(f"psx{i}", [P, 2 * CC, SLOTS], F16) for i in range(2)]
        psu = [ps(f"psu{i}", [P, 512]) for i in range(PAIRS)]
        psy = [ps(f"psy{i}", [P, SB, C]) for i in range(2)]
        warm = sb("warm", [P, 1])
        gather_rows = sb("gather_rows", [P, 2, SB], I32)
        add_rows = sb("add_rows", [P, 2, SB], I32)

        xg_loaded = [sem(f"xg_loaded{i}") for i in range(2)]
        y_added = [sem(f"y_added{i}") for i in range(2)]
        xt_ready, xt_copied, up_ready, gelu_ready = sem("xt_ready"), sem("xt_copied"), sem("up_ready"), sem("gelu_ready")
        hh_ready, hl_ready, down_ready, y_ready = sem("hh_ready"), sem("hl_ready"), sem("down_ready"), sem("y_ready")
        gather_rows_ready, add_rows_ready = sem("gather_rows_ready"), sem("add_rows_ready")
        gp_ready, gate_ready, table_loaded = sem("gp_ready"), sem("gate_ready"), sem("warm_ready")
        passed = {e: sem(f"tiles_passed_{i}") for i, e in enumerate((nc.gpsimd, nc.scalar))}
        block = st.enter_context(nc.Block())

        def lone(eng):
            eng.sem_inc(passed[eng], 1)

        @block.gpsimd
        def _(pool):
            def slot_rows(dst, t, ready):
                at = t * SB
                src = k["slot_row"][:, bass.ds(at, SB)] if not isinstance(at, int) else k["slot_row"][:, at:at + SB]
                lone(pool)
                pool.tensor_copy(dst, src).then_inc(ready, 1)
                pool.wait_ge(ready, t + 1)
                lone(pool)

            def gather(t, par, half):
                slot_rows(gather_rows[:, par, :], t, gather_rows_ready)
                for j in range(SB):
                    pool.indirect_dma_start(xg[:, par, j, :], None, rows,
                                            bass.IndirectOffsetOnAxis(ap=gather_rows[:, par, j:j + 1], axis=0)
                                            ).then_inc(xg_loaded[par], 16)

            def add(t, par, half):
                for j in range(SB):
                    pool.indirect_dma_start(acc, bass.IndirectOffsetOnAxis(ap=add_rows[:, par, j:j + 1], axis=0),
                                            y[:, par, j, :], None, compute_op=ALU.add).then_inc(y_added[par], 16)

            def step(t, par, half, prior):
                if prior:
                    pool.wait_ge(xt_ready, t - 1)
                    pool.wait_ge(gate_ready, t - 1)
                gather(t, par, half)

            def result(t, par, half, prior):
                pool.wait_ge(y_ready, SB * (t + 1))
                slot_rows(add_rows[:, par, :], t, add_rows_ready)
                if prior:
                    pool.wait_ge(y_added[1 - par], 16 * SB * (half + par))
                lone(pool)
                add(t, par, half)

            gather(0, 0, 0)
            gather(1, 1, 0)
            step(2, 0, 1, True)
            step(3, 1, 1, True)
            result(0, 0, 0, False)
            with pool.Fori(2, ETILES // 2) as u:
                for par in range(2):
                    step(2 * u + par, par, u, True)
                    result(2 * u + par - 3, 1 - par, u - 2 + par, True)
            for t in range(ETILES - ETILES % 2, ETILES):
                step(t, t % 2, t // 2, True)
            for t in range(2 * (ETILES // 2) - 3, ETILES):
                result(t, t % 2, t // 2, True)
            pool.wait_ge(y_added[0], 16 * SB * ((ETILES + 1) // 2))
            pool.wait_ge(y_added[1], 16 * SB * (ETILES // 2))

        @block.tensor
        def _(pe):
            def row_transposes(t, par, half, prior=True):
                pe.wait_ge(xg_loaded[par], 16 * SB * (half + 1))
                if prior:
                    pe.wait_ge(xt_copied, t - 1)
                for q in range(2 * CC):
                    for j in range(SB):
                        ins = pe.transpose(psx[par][:, q, j * P:(j + 1) * P], xg[:, par, j, q * P // 2:(q + 1) * P // 2].bitcast(F16), k["ident16"][:, :])
                ins.then_inc(xt_ready, 1)

            def up_products(t, par, half, e, prior=True):
                pe.wait_ge(xt_copied, t + 1)
                w = k["wu"][:, bass.ds(e, 1), :, :, :].rearrange("p e s c h -> p (e s) c h")
                for p in range(PAIRS):
                    if prior:
                        pe.wait_ge(gelu_ready, PAIRS * (t - 1) + (p + 1))
                    for i in range(2):
                        m = (2 * p + i) * P
                        n = 0
                        for c in range(CC):
                            for ws, xs in ((0, 0), (0, 1), (1, 0)):
                                ins = pe.matmul(psu[p][:, i * SLOTS:(i + 1) * SLOTS], w[:, ws, c, m:m + P], xT[:, par, xs * CC + c, :],
                                                start=(n == 0), stop=(n == 3 * CC - 1))
                                n += 1
                    ins.then_inc(up_ready, 1)

            def down_products(t, par, half, e, prior=True):
                pe.wait_ge(hl_ready, PAIRS * (t + 1))
                w = k["wd"][:, bass.ds(e, 1), :, :, :].rearrange("p e s c d -> p (e s) c d")
                for j in range(SB):
                    if prior and j == 0:
                        pe.wait_ge(y_ready, SB * (t - 1))
                    n = 0
                    for c in range(HC):
                        for hs, ws in ((0, 0), (0, 1), (1, 0)):
                            ins = pe.matmul(psy[par][:, j, :], (hh, hl)[hs][:, par, c, j * P:(j + 1) * P], w[:, ws, c, :],
                                            start=(n == 0), stop=(n == 3 * HC - 1))
                            n += 1
                    ins.then_inc(down_ready, 1)

            def expert_of(t):
                at = k["tile_expert"][0:1, bass.ds(t, 1)] if not isinstance(t, int) else k["tile_expert"][0:1, t:t + 1]
                return pe.value_load(at, min_val=0, max_val=EXP - 1)

            def turn(t, par, half, more=True, prior=(True, True)):
                up_products(t, par, half, expert_of(t))
                if more:
                    row_transposes(t + 1, 1 - par, half + par)
                down_products(t - 1, 1 - par, half, expert_of(t - 1), prior[0])

            row_transposes(0, 0, 0, False)
            up_products(0, 0, 0, expert_of(0), False)
            row_transposes(1, 1, 0, False)
            turn(1, 1, 0, prior=(False, True))
            turn(2, 0, 1, prior=(False, True))
            turn(3, 1, 1)
            with pe.Fori(2, (ETILES - 1) // 2) as u:
                for par in range(2):
                    turn(2 * u + par, par, u)
            last = ETILES - 1
            for t in range(2 * (last // 2), ETILES):
                turn(t, t % 2, t // 2, more=t + 1 < ETILES)
            down_products(last, last % 2, last // 2, expert_of(last))

        @block.scalar
        def _(act):
            act.activation(warm[:, :], k["nhalf"][:, 0:1], ACT.Gelu_apprx_tanh).then_inc(table_loaded, 1)

            def gelus(t, par, half, prior=True):
                sc = k["up_scale"][:, bass.ds(t, 1)] if not isinstance(t, int) else k["up_scale"][:, t:t + 1]
                for p in range(PAIRS):
                    act.wait_ge(up_ready, PAIRS * t + (p + 1))
                    if prior:
                        act.wait_ge(hl_ready, PAIRS * (t - 1) + (p + 1))
                    lone(act)
                    act.activation(h[:, p, :], psu[p][:, :], ACT.Gelu_apprx_tanh, scale=sc).then_inc(gelu_ready, 1)

            def results(t, par, half, prior=True):
                if prior:
                    act.wait_ge(y_added[par], 16 * SB * half)
                act.wait_ge(gate_ready, t + 1)
                act.wait_ge(down_ready, SB * (t + 1))
                lone(act)
                for j in range(SB):
                    g = t * SB + j
                    scale = gate[:, bass.ds(g, 1)] if not isinstance(g, int) else gate[:, g:g + 1]
                    act.activation(y[:, par, j, :], psy[par][:, j, :], ACT.Copy, scale=scale).then_inc(y_ready, 1)

            gelus(0, 0, 0, False)
            gelus(1, 1, 0)
            results(0, 0, 0, False)
            gelus(2, 0, 1)
            results(1, 1, 0, False)
            gelus(3, 1, 1)
            results(2, 0, 1)
            with act.Fori(2, ETILES // 2) as u:
                for par in range(2):
                    gelus(2 * u + par, par, u)
                    results(2 * u + par - 1, 1 - par, u - 1 + par)
            for t in range(2 * (ETILES // 2), ETILES):
                gelus(t, t % 2, t // 2)
                results(t - 1, 1 - t % 2, (t - 1) // 2)
            results(ETILES - 1, (ETILES - 1) % 2, (ETILES - 1) // 2)

        @block.vector
        def _(dve):
            def take_rows(t, par, half, prior=True):
                dve.wait_ge(xt_ready, t + 1)
                if prior:
                    dve.wait_ge(up_ready, PAIRS * (t - 1))
                dve.tensor_copy(xT[:, par, :, :], psx[par][:, :, :]).then_inc(xt_copied, 1)
                pick = k["pick"][:, bass.ds(t, 1), :] if not isinstance(t, int) else k["pick"][:, t:t + 1, :]
                dve.tensor_tensor(gp[:, par, :, :], xg[:, par, :, C:ROW // 2], pick.to_broadcast([P, SB, EXP]),
                                  ALU.mult).then_inc(gp_ready, 1)
                dve.wait_ge(gp_ready, t + 1)
                at = t * SB
                dst = gate[:, bass.ds(at, SB)] if not isinstance(at, int) else gate[:, at:at + SB]
                dve.tensor_reduce(dst, gp[:, par, :, :], AX_X, ALU.add).then_inc(gate_ready, 1)

            def halves(t, par, half, prior=True):
                sc = k["h_scale"][:, bass.ds(t, 1)] if not isinstance(t, int) else k["h_scale"][:, t:t + 1]
                if prior:
                    dve.wait_ge(down_ready, SB * (t - 1))
                for p in range(PAIRS):
                    hi = hh[:, par, 2 * p:2 * p + 2, :].rearrange("p c s -> p (c s)")
                    lo = hl[:, par, 2 * p:2 * p + 2, :].rearrange("p c s -> p (c s)")
                    dve.wait_ge(gelu_ready, PAIRS * t + (p + 1))
                    dve.tensor_scalar(hi, h[:, p, :], sc, None, ALU.mult).then_inc(hh_ready, 1)
                    dve.wait_ge(hh_ready, PAIRS * t + (p + 1))
                    dve.scalar_tensor_tensor(out=lo, in0=h[:, p, :], scalar=sc, in1=hi, op0=ALU.mult, op1=ALU.subtract).then_inc(hl_ready, 1)

            take_rows(0, 0, 0, False)
            halves(0, 0, 0, False)
            take_rows(1, 1, 0, False)
            halves(1, 1, 0, False)
            take_rows(2, 0, 1)
            with dve.Fori(1, (ETILES - 1) // 2) as u:
                for par in range(2):
                    halves(2 * u + par, par, u)
                    take_rows(2 * u + par + 1, 1 - par, u + par)
            for t in range(2 * ((ETILES - 1) // 2), ETILES):
                halves(t, t % 2, t // 2)
                if t + 1 < ETILES:
                    take_rows(t + 1, 1 - t % 2, (t + 1) // 2)


def last_norm(nc, k, acc, out):
    st = ExitStack()
    with st:
        def sem(name):
            return st.enter_context(nc.semaphore(name))

        GROUPS = B
        G = NT // GROUPS
        s = st.enter_context(nc.sbuf_tensor("sums", [P, NT, C], F32))
        stat = st.enter_context(nc.sbuf_tensor("fstat", [P, 2, 6], F32))
        mv = st.enter_context(nc.sbuf_tensor("fmv", [P, NT, 2], F32))
        var = st.enter_context(nc.sbuf_tensor("fvar", [P, NT], F32))
        rstd = st.enter_context(nc.sbuf_tensor("frstd", [P, NT], F32))
        loaded = [sem(f"loaded{g}") for g in range(GROUPS)]
        stats_ready, mv_ready, var_ready, rstd_ready, normed, stored = (
            sem("fstats_ready"), sem("fmv_ready"), sem("fvar_ready"), sem("frstd_ready"), sem("normed"), sem("stored"))
        a = acc[0:B * N, :].rearrange("(t p) c -> p t c", p=P)
        o = out.rearrange("b (t p) c -> b p t c", p=P)
        block = st.enter_context(nc.Block())

        @block.sync
        def _(sp):
            for g in range(GROUPS):
                sp.dma_start(s[:, g * G:(g + 1) * G, :], a[:, g * G:(g + 1) * G, :]).then_inc(loaded[g], 16)
            for g in range(GROUPS):
                sp.wait_ge(normed, (g + 1) * G)
                sp.dma_start(o[g], s[:, g * G:(g + 1) * G, :]).then_inc(stored, 16)
            sp.wait_ge(stored, 16 * GROUPS)

        @block.vector
        def _(dve):
            for t in range(NT + 3):
                if t < NT:
                    if t % G == 0:
                        dve.wait_ge(loaded[t // G], 16)
                    dve.bn_stats(stat[:, t % 2, :], s[:, t, :]).then_inc(stats_ready, 1)
                    dve.wait_ge(stats_ready, t + 1)
                    dve.bn_aggr(mv[:, t, :], stat[:, t % 2, :]).then_inc(mv_ready, 1)
                if t >= 3:
                    i = t - 3
                    dve.wait_ge(rstd_ready, i + 1)
                    dve.tensor_scalar(s[:, i, :], s[:, i, :], mv[:, i, 0:1], rstd[:, i:i + 1], ALU.subtract, ALU.mult).then_inc(normed, 1)

        @block.gpsimd
        def _(pool):
            for t in range(NT):
                pool.wait_ge(mv_ready, t + 1)
                pool.tensor_scalar(var[:, t:t + 1], mv[:, t, 1:2], LN_EPS, None, ALU.add).then_inc(var_ready, 1)
                pool.wait_ge(var_ready, t + 1)
                pool.tensor_tensor(rstd[:, t:t + 1], var[:, t:t + 1], k["nhalf"][:, 0:1], ALU.pow).then_inc(rstd_ready, 1)


_INS = ["x", "ctx_2048", "mask_BxS2_ik0", "L0_attn_Wq", "L0_attn_bq", "L0_attn_Wk", "L0_attn_bk", "L0_attn_Wv",
        "L0_attn_bv", "L0_attn_Wo", "L0_attn_bo", "L0_attn_ln_g", "L0_attn_ln_b", "L0_xattn_b", "L0_ffn_router_w",
        "L0_ffn_up_w", "L0_ffn_down_w"]
_OUTS = [((B, N, C), "float32")]


def kernel(**inputs):
    import numpy as _np
    import concourse.bacc as _bacc
    from concourse import mybir as _mybir
    from concourse.bass_utils import run_bass_kernel_spmd as _run

    nc = _bacc.Bacc("TRN2", target_bir_lowering=False, num_devices=1)
    arrays, args = {}, []
    for name in _INS:
        a = _np.ascontiguousarray(inputs[name])
        arrays[f"in_{name}_dram"] = a
        args.append(nc.dram_tensor(f"in_{name}_dram", a.shape, _mybir.dt.from_np(a.dtype), kind="ExternalInput").ap())
    for i, (shape, dtype) in enumerate(_OUTS):
        dt = _mybir.dt.from_np(_np.dtype(dtype))
        args.append(nc.dram_tensor(f"out_{i}_dram", shape, dt, kind="ExternalOutput").ap())
    layer_kernel(nc, *args)
    r = _run(nc, [arrays], core_ids=[0])
    return r.results[0]["out_0_dram"]
```

```python
from contextlib import ExitStack

import concourse.bass as bass
from concourse import mybir

F32 = mybir.dt.float32
F16 = mybir.dt.float16
BF16 = mybir.dt.bfloat16
I32 = mybir.dt.int32
ALU = mybir.AluOpType
ACT = mybir.ActivationFunctionType
AX_X = mybir.AxisListType.X
SUM = bass.bass_isa.ReduceOp.add

P = 128
B, N, C = 4, 1024, 256
CC = C // P
TB = N // P
NT = B * TB
LH, LD = 16, 16
HPC = P // LD
XH, XD = 8, 32
XPC = P // XD
KEYS = 77
CTX = 2 * C
EXP, TOPK, HID = 8, 4, 1024
HC = HID // P
SLOTS = 256
SB = SLOTS // P
ETILES = (TOPK * B * N + EXP * (SLOTS - 1)) // SLOTS
EBLOCKS = ETILES * SB
PAIRS = HC // 2
TRASH = SB * P
ROWS = B * N + TRASH
FLAT = XH * KEYS
FCH = -(-FLAT // P)
ROW = 2 * C + 2 * EXP
LN_EPS = 1e-5
MASKED = -1e30
XSCALE = 64.0
WTARGET = 2.0 ** 14
HTARGET = 2.0 ** 10
LOGIT0 = 1024 - 512 - XPC * KEYS
CONST_STEPS = 18 + 3 * FCH
IDENT_MADE, ONES_MADE = 2, 3
PIECES = 4
HALVES = 2
HT = TB // HALVES
KG = 4
EXPONENT = 0x7F800000

TRANS_SETUP = 4 * CC
TRANS_BATCH = 7 * TB
SMALL_SETUP = CC
SMALL_BATCH = CC + 2 + CC + 4 * TB


SPAN = [(c * P // KEYS, -(-min((c + 1) * P, FLAT) // KEYS)) for c in range(FCH)]
SPAN_MAX = max(b - a for a, b in SPAN)
SEGMENTS = [(c, max(c * P, h * KEYS) - c * P, h, max(c * P, h * KEYS) - h * KEYS,
             min((c + 1) * P, (h + 1) * KEYS) - max(c * P, h * KEYS))
            for c in range(FCH) for h in range(*SPAN[c])]


def cross_uses():
    order = []
    for i in range(TB + 4):
        if i < TB:
            order.append(("x1", i))
        if 0 <= i - 3 < TB:
            order += [("pa", i - 3), ("pb", i - 3)]
    return {what: n for n, what in enumerate(order)}


CROSS = cross_uses()


def layer_kernel(nc, x, ctx, mask, Wq, bq, Wk, bk, Wv, bv, Wo, bo, ln_g, ln_b, xb, router, up, down, out):
    rows = nc.dram_tensor("token_rows", [ROWS, ROW // 2], F32, kind="Internal").ap()
    acc = nc.dram_tensor("token_sums", [ROWS, C], F32, kind="Internal").ap()
    with ExitStack() as all_:
        def keep(name, shape, dt):
            return all_.enter_context(nc.sbuf_tensor(name, shape, dt))

        k = {
            "wu": keep("w_up", [P, EXP, 2, CC, HID], F16),
            "wd": keep("w_down", [P, EXP, 2, HC, C], F16),
            "wpow": keep("w_pow", [P, 2 * EXP], F32),
            "rank": keep("rank", [P, EXP, NT], F32),
            "ident": keep("ident", [P, P], F32),
            "ones": keep("ones", [P, P], F32),
            "nhalf": keep("nhalf", [P, TB], F32),
            "rows_stored": [all_.enter_context(nc.semaphore(f"rows_stored{h}")) for h in range(HALVES)],
            "acc_stored": [all_.enter_context(nc.semaphore(f"acc_stored{h}")) for h in range(HALVES)],
        }
        attention(nc, k, rows, acc, x, ctx, mask, Wq, bq, Wk, bk, Wv, bv, Wo, bo, ln_g, ln_b, xb, router, up, down)
        with ExitStack() as plan:
            def tab(name, shape, dt):
                return plan.enter_context(nc.sbuf_tensor(name, shape, dt))

            k["slot_row"] = tab("slot_row", [P, EBLOCKS], I32)
            k["tile_expert"] = tab("tile_expert", [P, ETILES], I32)
            k["pick"] = tab("pick", [P, ETILES, EXP], F32)
            k["up_scale"] = tab("up_scale", [P, ETILES], F32)
            k["h_scale"] = tab("h_scale", [P, ETILES], F32)
            k["ident16"] = tab("ident16", [P, P], F16)
            routing(nc, k)
            experts(nc, k, rows, acc)
        last_norm(nc, k, acc, out)


def attention(nc, k, rows, acc, x, ctx, mask, Wq, bq, Wk, bk, Wv, bv, Wo, bo, ln_g, ln_b, xb, router, up, down):
    st = ExitStack()
    with st:
        def sb(name, shape, dt=F32):
            return st.enter_context(nc.sbuf_tensor(name, shape, dt))

        def ps(name, shape, dt=F32):
            return st.enter_context(nc.psum_tensor(name, shape, dt))

        def sem(name):
            return st.enter_context(nc.semaphore(name))

        ident, ones, nhalf = k["ident"], k["ones"], k["nhalf"]
        X = sb("X", [P, TB, C])
        Q = sb("Q", [P, TB, C])
        KZ = sb("KZ", [P, TB * (ROW // 2)])
        V = sb("V", [P, TB, CC, P + 1])
        K = KZ[:, 0:TB * C].rearrange("p (t c) -> p t c", c=C)
        XR = KZ[:, :].bitcast(F16).rearrange("p (t r) -> p t r", r=ROW)
        W8 = sb("W8", [P, 2048])
        wqkv = sb("wqkv", [P, CC, 3 * C])
        woT = sb("woT", [P, CC, C])
        bias = sb("bias", [P, 3 * C])
        cvec = sb("cvec", [P, C])
        tT = sb("tT", [P, 2, CC, P])
        kbd = sb("kbd", [P, CC, XPC, KEYS])
        hsel = sb("hsel", [P, XPC])
        bsel = sb("bsel", [P, HPC])
        state = sb("state", [P, CC, P + HPC])
        ctx_sb = sb("ctx_sb", [KEYS, C])
        vx = sb("vx", [P, FCH, SPAN_MAX, XD + 1])
        mint = sb("mint", [1, KEYS], I32)
        mrow = sb("mrow", [1, KEYS])
        mbf = sb("mbf", [1, XPC, KEYS], BF16)
        one16 = sb("one16", [1, P], BF16)
        pr = sb("pr", [P, 2, XH, KEYS])
        pT = sb("pT", [P, 2, FCH, P])
        rw = sb("rw", [P, CC, EXP])
        gb = sb("gb", [P, 2, CC])
        bcol = sb("bcol", [P, 1])
        kmx = pT[:, 1, 0:CC, :].rearrange("p c t -> p (c t)")
        kdiag = pT[:, 0, 0:CC, :]
        km2 = sb("km2", [P, CC])
        qm = sb("qm", [P, 2, LH])
        rden = sb("rden", [P, 2, LH])
        rst = sb("rst", [P, CC])
        stat = sb("stat", [P, 2, 6])
        mv = sb("mv", [P, 3, TB, 2])
        ve = sb("ve", [P, 3, TB])
        rstd = sb("rstd", [P, 3, TB])
        xm = sb("xm", [P, 2, XH])
        xmb = sb("xmb", [P, 2, XH])
        xr8 = sb("xr8", [P, 2, XH])
        L = sb("L", [P, TB, EXP])
        lm = sb("lm", [P, TB])
        le = sb("le", [P, TB, EXP])
        both = pr[:, :, :, :].rearrange("p r h k -> p (r h k)")[:, 0:2 * HT * EXP * EXP].rearrange(
            "p (r t e j) -> p r t e j", r=2, t=HT, e=EXP)
        cmpa, cmpb = both[:, 0], both[:, 1]
        lower = sb("lower", [P, EXP, EXP])
        rk = sb("rk", [P, TB, EXP])
        gsum = sb("gsum", [P, 2, TB])
        wsq = sb("wsq", [P, 1])
        wnorm = sb("wnorm", [P, 1])
        phalf = sb("phalf", [P, 1])
        wall = sb("wall", [P, 1])
        wcl = sb("wcl", [P, 1])
        wrp = sb("wrp", [P, 1])
        wsc = sb("wsc", [P, 1])

        trans = [ps(f"trans{i}", [P, 4, P]) for i in range(2)]
        small = [ps(f"small{i}", [P, 512]) for i in range(2)]
        big = [ps(f"big{i}", [P, 1024]) for i in range(2)]

        w_nat = Q[:, :, :].rearrange("p (w o) c -> p w o c", w=4)
        zero16 = KZ[:, 0:ROW // 2]
        zero32 = K[:, 2, :]

        setup_loaded, setup_loaded2 = sem("setup_loaded"), sem("setup_loaded2")
        consts, zeros_ready = sem("consts"), sem("zeros_ready")
        x_loaded, ctx_loaded, mask_loaded, w_loaded = sem("x_loaded"), sem("ctx_loaded"), sem("mask_loaded"), sem("w_loaded")
        rows_stored, acc_stored = k["rows_stored"], k["acc_stored"]
        trans_ready, trans_copied = sem("trans_ready"), sem("trans_copied")
        small_ready, small_free = sem("small_ready"), sem("small_free")
        lnbb_ready, woT_ready = sem("lnbb_ready"), sem("woT_ready")
        vx_loaded, mask_ready, pool_step = sem("vx_loaded"), sem("mask_ready"), sem("pool_step")
        qkv_ready, qk_ready, v_ready = sem("qkv_ready"), sem("qk_ready"), sem("v_ready")
        qm_ready, qs_ready, qe_ready, kmx_ready = sem("qm_ready"), sem("qs_ready"), sem("qe_ready"), sem("kmx_ready")
        km2_ready, kdiag_ready, ks_ready, ke_ready = sem("km2_ready"), sem("kdiag_ready"), sem("ks_ready"), sem("ke_ready")
        rst_ready = sem("rst_ready")
        rden_ready, o_ready = sem("rden_ready"), sem("o_ready")
        xc_ready = sem("xc_ready")
        stat_ready, mv_ready, ve_ready, rstd_ready = sem("stat_ready"), sem("mv_ready"), sem("ve_ready"), sem("rstd_ready")
        z_ready, x1_ready = sem("z_ready"), sem("x1_ready")
        lg_ready, xm_ready, xmb_ready, s_ready, p_ready = sem("lg_ready"), sem("xm_ready"), sem("xmb_ready"), sem("s_ready"), sem("p_ready")
        xr8_ready, r2_ready, x2_ready = sem("xr8_ready"), sem("r2_ready"), sem("x2_ready")
        hi_ready, lo_ready = sem("hi_ready"), sem("lo_ready")
        L_ready, route_step, le_shift, le_ready, gates_ready = sem("L_ready"), sem("route_step"), sem("le_shift"), sem("le_ready"), sem("gates_ready")
        wsq_ready, wall_ready, wnorm_ready, wstep, wsc_ready, whi_ready, w_split = (
            sem("wsq_ready"), sem("wall_ready"), sem("wnorm_ready"), sem("wstep"), sem("wsc_ready"), sem("whi_ready"), sem("w_split"))

        passed = {e: sem(f"passed_{i}") for i, e in enumerate((nc.gpsimd, nc.scalar, nc.vector, nc.sync))}

        x_in = x.rearrange("b (t p) c -> b p t c", p=P)
        rows_out = rows[0:B * N, :].rearrange("(b t p) r -> b p t r", p=P, t=TB)
        acc_out = acc[0:B * N, :].rearrange("(b t p) c -> b p t c", p=P, t=TB)
        up_in = up.rearrange("e (c p) h -> e p c h", p=P)
        down_in = down.rearrange("e (c p) d -> e p c d", p=P)

        def lone(eng):
            eng.sem_inc(passed[eng], 1)

        def one(ap, b):
            a = ap[bass.ds(b, 1)]
            return a.squeeze(0)

        def trans_use(stage, i):
            return stage * TB + i if stage < 3 else 3 * TB + CROSS["x1", i] if stage == 3 else 6 * TB + i

        block = st.enter_context(nc.Block())

        @block.sync
        def _(sp):
            for w, mat in enumerate((Wq, Wk, Wv, Wo)):
                sp.dma_start(w_nat[:, w, :, :], mat.rearrange("(o p) c -> p o c", p=P)).then_inc(setup_loaded, 16)
            sp.dma_start(X[:, :, :], x_in[0]).then_inc(x_loaded, 16)
            for w, vec in enumerate((bq, bk, bv)):
                sp.dma_start(bias[:, w * C:(w + 1) * C], vec.partition_broadcast(P)).then_inc(setup_loaded2, 16)
            sp.dma_start(cvec[:, :], bo.partition_broadcast(P)).then_inc(setup_loaded2, 16)
            sp.dma_start(bcol[:, :], xb.partition_broadcast(P)).then_inc(setup_loaded2, 16)
            sp.dma_start(gb[:, 0, :], ln_g.rearrange("(c p) -> p c", p=P), allow_slow_non_contiguous=True).then_inc(setup_loaded2, 16)
            sp.dma_start(gb[:, 1, :], ln_b.rearrange("(c p) -> p c", p=P), allow_slow_non_contiguous=True).then_inc(setup_loaded2, 16)
            sp.dma_start(rw[:, :, :], router.rearrange("(c p) e -> p c e", p=P)).then_inc(setup_loaded2, 16)
            sp.dma_start(ctx_sb[:, :], ctx[0, :, 0:C]).then_inc(ctx_loaded, 16)
            sp.dma_start(mint[:, :], mask[0:1, :]).then_inc(mask_loaded, 16)
            sp.dma_start(W8[:, :].rearrange("p (c h) -> p c h", c=CC), up_in[0]).then_inc(w_loaded, 16)
            def load_values(of_batch):
                for c, p, h, key, n in SEGMENTS:
                    sp.dma_start(vx[p:p + n, c, h - SPAN[c][0], 0:XD], of_batch[key:key + n, C + h * XD:C + (h + 1) * XD]).then_inc(vx_loaded, 16)

            sp.wait_ge(consts, CONST_STEPS)
            load_values(ctx[0])
            sp.wait_ge(zeros_ready, 2)
            for j in range(SB):
                sp.dma_start(rows[B * N + j * P:B * N + (j + 1) * P, :], zero16).then_inc(rows_stored[j], 16)
                sp.dma_start(acc[B * N + j * P:B * N + (j + 1) * P, :], zero32).then_inc(acc_stored[j], 16)

            def next_piece(b, q):
                sp.wait_ge(w_split, PIECES * b + (q + 1))
                lone(sp)
                e, src = 2 * b + (q + 1) // 2, (up_in, down_in)[(q + 1) % 2]
                piece = one(src, e) if not isinstance(e, int) else src[e]
                sp.dma_start(W8[:, :].rearrange("p (c h) -> p c h", c=piece.shape[1]), piece).then_inc(w_loaded, 16)

            def store_x2(b, half):
                sp.wait_ge(x2_ready, TB * b + HT * (half + 1))
                lone(sp)
                at = slice(HT * half, HT * (half + 1))
                dst = acc_out[b] if isinstance(b, int) else one(acc_out, b)
                sp.dma_start(dst[:, at, :], Q[:, at, :]).then_inc(acc_stored[half], 16)

            def store_rows(b, half):
                sp.wait_ge(hi_ready, TB * b + HT * (half + 1))
                lone(sp)
                sp.wait_ge(lo_ready, TB * b + HT * (half + 1))
                lone(sp)
                sp.wait_ge(gates_ready, HALVES * b + half + 1)
                lone(sp)
                at = slice(HT * half, HT * (half + 1))
                dst = rows_out[b] if isinstance(b, int) else one(rows_out, b)
                sp.dma_start(dst[:, at, :], KZ[:, :].rearrange("p (t r) -> p t r", t=TB)[:, at, :]).then_inc(rows_stored[half], 16)

            with sp.Fori(0, B - 1) as b:
                for q in range(PIECES):
                    next_piece(b, q)
                sp.wait_ge(small_free, SMALL_SETUP + SMALL_BATCH * b + 2 * CC + 2 + 2 * TB)
                lone(sp)
                sp.dma_start(X[:, :, :], one(x_in, b + 1)).then_inc(x_loaded, 16)
                sp.dma_start(ctx_sb[:, :], one(ctx, b + 1)[:, 0:C]).then_inc(ctx_loaded, 16)
                sp.wait_ge(mask_ready, b + 1)
                lone(sp)
                sp.dma_start(mint[:, :], mask[bass.ds(b + 1, 1), :]).then_inc(mask_loaded, 16)
                store_x2(b, 0)
                store_x2(b, 1)
                load_values(one(ctx, b + 1))
                store_rows(b, 0)
                store_rows(b, 1)
            for q in range(PIECES - 1):
                next_piece(B - 1, q)
            for half in range(HALVES):
                store_x2(B - 1, half)
            for half in range(HALVES):
                store_rows(B - 1, half)

        @block.gpsimd
        def _(pool):
            steps = [0]

            def done(ins):
                steps[0] += 1
                ins.then_inc(consts, 1)
                pool.wait_ge(consts, steps[0])

            done(pool.memset(ident[:, :], 0.0))
            done(pool.affine_select(out=ident[:, :], in_=ident[:, :], compare_op=ALU.not_equal, fill=1.0,
                                    base=0, pattern=[[-1, P]], channel_multiplier=1))
            done(pool.memset(ones[:, :], 1.0))
            pool.memset(zero16, 0.0).then_inc(zeros_ready, 1)
            pool.memset(zero32, 0.0).then_inc(zeros_ready, 1)
            done(pool.memset(nhalf[:, :], -0.5))
            done(pool.memset(phalf[:, :], 0.5))
            done(pool.memset(one16[:, :], 1.0))
            done(pool.memset(V[:, :, :, P:P + 1], 1.0))
            done(pool.memset(vx[:, :, :, :], 0.0))
            for c, (h0, h1) in enumerate(SPAN):
                col = vx[:, c, 0:h1 - h0, XD]
                done(pool.memset(col, 1.0))
                done(pool.affine_select(out=col, in_=col, compare_op=ALU.is_ge, fill=0.0, base=c * P - h0 * KEYS,
                                        pattern=[[-KEYS, h1 - h0]], channel_multiplier=1))
                done(pool.affine_select(out=col, in_=col, compare_op=ALU.is_ge, fill=0.0, base=h0 * KEYS + KEYS - 1 - c * P,
                                        pattern=[[KEYS, h1 - h0]], channel_multiplier=-1))
            for tile, heads, d in ((hsel, XPC, XD), (bsel, HPC, LD)):
                done(pool.memset(tile[:, :], 1.0))
                done(pool.affine_select(out=tile[:, :], in_=tile[:, :], compare_op=ALU.is_ge, fill=0.0,
                                        base=0, pattern=[[-d, heads]], channel_multiplier=1))
                done(pool.affine_select(out=tile[:, :], in_=tile[:, :], compare_op=ALU.is_ge, fill=0.0,
                                        base=d - 1, pattern=[[d, heads]], channel_multiplier=-1))
            for c in range(CC):
                done(pool.tensor_copy(state[:, c, P:P + HPC], bsel[:, :]))
            done(pool.memset(lower[:, :, :], 1.0))
            done(pool.affine_select(out=lower[:, :, :], in_=lower[:, :, :], compare_op=ALU.is_gt, fill=0.0,
                                    base=0, pattern=[[1, EXP], [-1, EXP]], channel_multiplier=0))

            assert steps[0] == CONST_STEPS

            def piece_norm(b, q):
                pool.wait_ge(wsq_ready, PIECES * b + (q + 1))
                lone(pool)
                pool.partition_all_reduce(wall[:, :], wsq[:, :], P, SUM).then_inc(wall_ready, 1)
                pool.wait_ge(wall_ready, PIECES * b + (q + 1))
                pool.tensor_tensor(wnorm[:, :], wall[:, :], phalf[:, :], ALU.pow).then_inc(wnorm_ready, 1)

            def inverse_deviation(b, kind, i):
                n = 3 * TB * b + TB * kind + i + 1
                pool.wait_ge(mv_ready, n)
                lone(pool)
                pool.tensor_scalar(ve[:, kind, i:i + 1], mv[:, kind, i, 1:2], LN_EPS, None, ALU.add).then_inc(ve_ready, 1)
                pool.wait_ge(ve_ready, n)
                pool.tensor_tensor(rstd[:, kind, i:i + 1], ve[:, kind, i:i + 1], nhalf[:, 0:1], ALU.pow).then_inc(rstd_ready, 1)

            with pool.Fori(0, B) as b:
                pool.wait_ge(mask_loaded, 16 * b + 16)
                lone(pool)
                pool.tensor_scalar(mrow[:, :], mint[:, :], -1.0, 1.0, ALU.mult, ALU.add).then_inc(pool_step, 1)
                pool.wait_ge(pool_step, 1 + b)
                lone(pool)
                for h in range(XPC):
                    ins = pool.tensor_scalar(mbf[:, h, :], mrow[:, :], MASKED, None, ALU.mult)
                ins.then_inc(mask_ready, 1)
                for i in range(TB):
                    if i == 0:
                        pool.wait_ge(small_free, SMALL_SETUP)
                    pool.wait_ge(trans_ready, TRANS_SETUP + TRANS_BATCH * b + i + 1)
                    pool.tensor_tensor(X[:, i, :], X[:, i, :], cvec[:, :], ALU.add).then_inc(xc_ready, 1)
                    if i in (0, 6):
                        piece_norm(b, i // 6)
                for kind in (0, 1):
                    for i in range(TB):
                        if kind == 1 and i == 0:
                            piece_norm(b, 2)
                        inverse_deviation(b, kind, i)
                piece_norm(b, 3)
                for i in range(TB + 1):
                    if i < TB:
                        pool.wait_ge(small_free, SMALL_SETUP + SMALL_BATCH * b + 2 * CC + 2 + 2 * TB + i + 1)
                        pool.tensor_tensor(Q[:, i, :].rearrange("p (c d) -> p c d", c=CC), Q[:, i, :].rearrange("p (c d) -> p c d", c=CC),
                                           V[:, i, :, 0:P], ALU.add).then_inc(r2_ready, 1)
                    if i >= 1:
                        inverse_deviation(b, 2, i - 1)

        @block.scalar
        def _(act):
            for w in range(4):
                for o in range(CC):
                    use = w * CC + o
                    act.wait_ge(trans_ready, use + 1)
                    dst = wqkv[:, :, w * C + o * P:w * C + (o + 1) * P] if w < 3 else woT[:, :, o * P:(o + 1) * P]
                    act.activation(dst, trans[use % 2][:, 0:CC, :], ACT.Copy).then_inc(trans_copied, 1)

            def copy_stage(b, stage, i, scale=1.0):
                s = trans_use(stage, i)
                act.wait_ge(trans_ready, TRANS_SETUP + TRANS_BATCH * b + s + 1)
                act.activation(tT[:, i % 2, :, :], trans[s % 2][:, 0:CC, :], ACT.Copy, scale=scale).then_inc(trans_copied, 1)

            def copy_probs(b, part, j):
                s = 3 * TB + CROSS[part, j]
                act.wait_ge(trans_ready, TRANS_SETUP + TRANS_BATCH * b + s + 1)
                rows_, at, n = (P, 0, 4) if part == "pa" else (FLAT - 4 * P, 4, 1)
                act.activation(pT[0:rows_, j % 2, at:at + n, :], trans[s % 2][0:rows_, 0:n, :], ACT.Copy).then_inc(trans_copied, 1)

            def high_place(b, q):
                wt = (k["wu"], k["wd"])[q % 2]
                return wt[:, bass.ds(2 * b + q // 2, 1), 0, :, :].rearrange("p e c h -> p (e c h)")

            def square_sum(b, q):
                act.wait_ge(w_loaded, 16 * (PIECES * b + q + 1))
                lone(act)
                act.activation(high_place(b, q).bitcast(BF16), W8[:, :], ACT.Square, accum_out=wsq[:, 0:1]).then_inc(wsq_ready, 1)

            def split_high(b, q):
                act.wait_ge(wsc_ready, PIECES * b + (q + 1))
                lone(act)
                act.activation(high_place(b, q), W8[:, :], ACT.Copy, scale=wsc[:, 0:1]).then_inc(whi_ready, 1)

            def shares(b, half):
                act.wait_ge(le_shift, HALVES * b + half + 1)
                at = slice(HT * half, HT * (half + 1))
                act.activation(le[:, at, :], le[:, at, :], ACT.Exp).then_inc(le_ready, 1)

            with act.Fori(0, B) as b:
                for i in range(TB + 2):
                    if i < TB:
                        copy_stage(b, 0, i)
                    if i >= 2:
                        act.wait_ge(qs_ready, TB * b + i - 1)
                        act.activation(Q[:, i - 2, :], Q[:, i - 2, :], ACT.Exp).then_inc(qe_ready, 1)
                    if i == 0 or i == 6:
                        square_sum(b, i // 6)
                    if i == 3:
                        split_high(b, 0)
                for g in range(KG):
                    if g < KG - 1:
                        act.wait_ge(ks_ready, (KG - 1) * b + g + 1)
                    else:
                        act.wait_ge(small_free, SMALL_SETUP + SMALL_BATCH * b + CC + 2)
                    at = slice(g * TB // KG, (g + 1) * TB // KG)
                    act.activation(K[:, at, :], K[:, at, :], ACT.Exp).then_inc(ke_ready, 1)
                split_high(b, 1)
                for i in range(TB):
                    copy_stage(b, 1, i)
                square_sum(b, 2)
                for i in range(TB):
                    copy_stage(b, 2, i)
                    if i == 4:
                        split_high(b, 2)
                for i in range(TB + 4):
                    if i < TB:
                        copy_stage(b, 3, i, XD ** -0.5)
                    if i == 1:
                        square_sum(b, 3)
                    if i == 5:
                        split_high(b, 3)
                    if 0 <= i - 3 < TB:
                        copy_probs(b, "pa", i - 3)
                        copy_probs(b, "pb", i - 3)
                    if 2 <= i < TB + 2:
                        act.wait_ge(s_ready, TB * b + i - 1)
                        act.activation(pr[:, (i - 2) % 2, :, :], pr[:, (i - 2) % 2, :, :], ACT.Exp).then_inc(p_ready, 1)
                for i in range(TB):
                    copy_stage(b, 4, i)
                    act.activation(XR[:, i, 0:C], Q[:, i, :], ACT.Copy, scale=XSCALE).then_inc(hi_ready, 1)
                    if i == HT:
                        shares(b, 0)
                shares(b, 1)

        @block.vector
        def _(dve):
            def small_wait(b, s):
                dve.wait_ge(small_ready, SMALL_SETUP + SMALL_BATCH * b + s + 1)
                return small[(SMALL_SETUP + s) % 2]

            dve.wait_ge(setup_loaded2, 16 * 8)
            dve.wait_ge(consts, ONES_MADE)
            for c in range(CC):
                dve.tensor_scalar(kdiag[:, c, :], ones[:, :], gb[:, 1, c:c + 1], None, ALU.mult).then_inc(lnbb_ready, 1)
            for c in range(CC):
                dve.wait_ge(small_ready, c + 1)
                dve.tensor_tensor(cvec[:, c * P:(c + 1) * P], small[c][:, 0:P], cvec[:, c * P:(c + 1) * P], ALU.add).then_inc(small_free, 1)
            for c in range(CC):
                dve.tensor_scalar(woT[:, c, :], woT[:, c, :], gb[:, 0, c:c + 1], None, ALU.mult).then_inc(woT_ready, 1)

            def scale(b, q):
                n = PIECES * b + q
                at = k["wpow"][:, bass.ds(n, 1)]
                dve.wait_ge(wnorm_ready, n + 1)
                dve.tensor_scalar(wcl[:, :], wnorm[:, :], 1e-18, None, ALU.max).then_inc(wstep, 1)
                dve.wait_ge(wstep, 3 * n + 1)
                dve.tensor_scalar(wcl[:, :].bitcast(I32), wcl[:, :].bitcast(I32), EXPONENT, None, ALU.bitwise_and).then_inc(wstep, 1)
                dve.wait_ge(wstep, 3 * n + 2)
                dve.tensor_copy(at, wcl[:, :])
                dve.reciprocal(wrp[:, :], wcl[:, :]).then_inc(wstep, 1)
                dve.wait_ge(wstep, 3 * n + 3)
                dve.tensor_scalar(wsc[:, :], wrp[:, :], WTARGET, None, ALU.mult).then_inc(wsc_ready, 1)

            def split_low(b, q):
                wt = (k["wu"], k["wd"])[q % 2]
                at = wt[:, bass.ds(2 * b + q // 2, 1), :, :, :].rearrange("p e s c h -> p s (e c h)")
                dve.wait_ge(whi_ready, PIECES * b + q + 1)
                dve.scalar_tensor_tensor(out=at[:, 1, :], in0=W8[:, :], scalar=wsc[:, 0:1], in1=at[:, 0, :],
                                         op0=ALU.mult, op1=ALU.subtract).then_inc(w_split, 1)

            def sums(i, src):
                dve.bn_stats(stat[:, i % 2, :], src).then_inc(stat_ready, 1)

            def moments(b, kind, i):
                dve.wait_ge(stat_ready, 3 * TB * b + TB * kind + i + 1)
                lone(dve)
                dve.bn_aggr(mv[:, kind, i, :], stat[:, i % 2, :]).then_inc(mv_ready, 1)

            def norm(b, kind, i, tile, ready):
                dve.wait_ge(rstd_ready, 3 * TB * b + TB * kind + i + 1)
                dve.tensor_scalar(tile, tile, mv[:, kind, i, 0:1], rstd[:, kind, i:i + 1], ALU.subtract, ALU.mult).then_inc(ready, 1)

            def take_router(b, i):
                dve.wait_ge(hi_ready, TB * b + i + 1)
                dve.scalar_tensor_tensor(out=XR[:, i, C:2 * C], in0=Q[:, i, :], scalar=XSCALE, in1=XR[:, i, 0:C],
                                         op0=ALU.mult, op1=ALU.subtract).then_inc(lo_ready, 1)
                lg8 = small_wait(b, 2 * CC + 2 + 3 * TB + i)
                dve.tensor_copy(L[:, i, :], lg8[:, 0:EXP]).then_inc(small_free, 1)

            def choose(b, half):
                at = slice(HT * half, HT * (half + 1))
                dve.wait_ge(small_free, SMALL_SETUP + SMALL_BATCH * b + 2 * CC + 2 + 3 * TB + HT * (half + 1))
                Lh, lmh = L[:, at, :], lm[:, at]
                lj = Lh.unsqueeze(2).to_broadcast([P, HT, EXP, EXP])
                le_ = Lh.unsqueeze(3).to_broadcast([P, HT, EXP, EXP])
                r0 = 9 * (HALVES * b + half)
                dve.tensor_reduce(lmh, Lh, AX_X, ALU.max).then_inc(route_step, 1)
                dve.tensor_tensor(cmpa[:, :, :, :], lj, le_, ALU.is_gt).then_inc(route_step, 1)
                dve.tensor_tensor(cmpb[:, :, :, :], lj, le_, ALU.is_equal).then_inc(route_step, 1)
                dve.wait_ge(route_step, r0 + 1)
                dve.tensor_tensor(le[:, at, :], Lh, lmh.unsqueeze(2).to_broadcast([P, HT, EXP]), ALU.subtract).then_inc(le_shift, 1)
                dve.wait_ge(route_step, r0 + 3)
                dve.tensor_tensor(cmpb[:, :, :, :], cmpb[:, :, :, :], lower[:, :, :].unsqueeze(1).to_broadcast([P, HT, EXP, EXP]), ALU.mult).then_inc(route_step, 1)
                dve.wait_ge(route_step, r0 + 4)
                dve.tensor_tensor(cmpa[:, :, :, :], cmpa[:, :, :, :], cmpb[:, :, :, :], ALU.add).then_inc(route_step, 1)
                dve.wait_ge(route_step, r0 + 5)
                dve.tensor_reduce(rk[:, at, :], cmpa[:, :, :, :], AX_X, ALU.add).then_inc(route_step, 1)
                dve.wait_ge(route_step, r0 + 6)
                dve.tensor_copy(k["rank"][:, :, bass.ds(TB * b + HT * half, HT)].rearrange("p e t -> p t e"), rk[:, at, :])

            def gates(b, half):
                at = slice(HT * half, HT * (half + 1))
                r0 = 9 * (HALVES * b + half)
                dve.wait_ge(le_ready, HALVES * b + half + 1)
                dve.scalar_tensor_tensor(out=le[:, at, :], in0=rk[:, at, :], scalar=float(TOPK), in1=le[:, at, :],
                                         op0=ALU.is_lt, op1=ALU.mult).then_inc(route_step, 1)
                dve.wait_ge(route_step, r0 + 7)
                dve.tensor_reduce(gsum[:, 0, at], le[:, at, :], AX_X, ALU.add).then_inc(route_step, 1)
                dve.wait_ge(route_step, r0 + 8)
                dve.reciprocal(gsum[:, 1, at], gsum[:, 0, at]).then_inc(route_step, 1)
                dve.wait_ge(route_step, r0 + 9)
                dve.tensor_tensor(XR[:, at, 2 * C:ROW].bitcast(F32), le[:, at, :],
                                  gsum[:, 1, at].unsqueeze(2).to_broadcast([P, HT, EXP]), ALU.mult).then_inc(gates_ready, 1)

            for half in range(HALVES):
                dve.wait_ge(rows_stored[half], 16)
                dve.wait_ge(acc_stored[half], 16)
            dve.wait_ge(consts, CONST_STEPS)

            with dve.Fori(0, B) as b:
                for c in range(CC):
                    kt = small_wait(b, c)
                    dve.tensor_tensor(kbd[:, c, :, :], kt[:, 0:KEYS].unsqueeze(1).to_broadcast([P, XPC, KEYS]),
                                      hsel[:, :].unsqueeze(2).to_broadcast([P, XPC, KEYS]), ALU.mult).then_inc(small_free, 1)
                for i in range(TB):
                    n = TB * b + i
                    if i % HT == 0:
                        dve.wait_ge(rows_stored[i // HT], 16 * (b + 1))
                        dve.wait_ge(acc_stored[i // HT], 16 * (b + 1))
                    if i == 3:
                        split_low(b, 0)
                    src = big[i % 2]
                    dve.wait_ge(qkv_ready, n + 1)
                    dve.tensor_tensor(Q[:, i, :], src[:, 0:C], bias[:, 0:C], ALU.add).then_inc(qk_ready, 1)
                    dve.tensor_tensor(K[:, i, :], src[:, C:2 * C], bias[:, C:2 * C], ALU.add).then_inc(qk_ready, 1)
                    dve.tensor_tensor(V[:, i, :, 0:P], src[:, 2 * C:3 * C].rearrange("p (c d) -> p c d", c=CC),
                                      bias[:, 2 * C:3 * C].rearrange("p (c d) -> p c d", c=CC), ALU.add).then_inc(v_ready, 1)
                    q3 = Q[:, i, :].rearrange("p (h d) -> p h d", h=LH)
                    dve.wait_ge(qk_ready, 2 * n + 2)
                    dve.tensor_reduce(qm[:, i % 2, :], q3, AX_X, ALU.max).then_inc(qm_ready, 1)
                    if i == 0:
                        dve.tensor_copy(kmx[:, :], K[:, 0, :]).then_inc(kmx_ready, 1)
                    else:
                        dve.wait_ge(kmx_ready, n)
                        dve.tensor_tensor(kmx[:, :], kmx[:, :], K[:, i, :], ALU.max).then_inc(kmx_ready, 1)
                    dve.wait_ge(qm_ready, n + 1)
                    dve.tensor_tensor(q3, q3, qm[:, i % 2, :].unsqueeze(2).to_broadcast([P, LH, LD]), ALU.subtract).then_inc(qs_ready, 1)
                    if i in (1, 7):
                        scale(b, i // 6)
                km = small_wait(b, CC)
                dve.tensor_reduce(km2[:, :], km[:, 0:C].rearrange("p (c t) -> p c t", c=CC), AX_X, ALU.max).then_inc(small_free, 1)
                dve.wait_ge(small_free, SMALL_SETUP + SMALL_BATCH * b + CC + 1)
                for c in range(CC):
                    dve.tensor_scalar(kdiag[:, c, :], ident[:, :], km2[:, c:c + 1], None, ALU.mult).then_inc(kdiag_ready, 1)
                kb = small_wait(b, CC + 1)
                for g in range(KG):
                    at = slice(g * TB // KG, (g + 1) * TB // KG)
                    dve.tensor_tensor(K[:, at, :], K[:, at, :], kb[:, 0:C].unsqueeze(1).to_broadcast([P, TB // KG, C]), ALU.subtract
                                      ).then_inc(ks_ready if g < KG - 1 else small_free, 1)
                split_low(b, 1)
                for c in range(CC):
                    sp_ = small_wait(b, CC + 2 + c)
                    dve.reciprocal(rst[:, c:c + 1], sp_[:, P:P + 1]).then_inc(rst_ready, 1)
                    dve.wait_ge(rst_ready, CC * b + c + 1)
                    dve.scalar_tensor_tensor(out=state[:, c, 0:P].rearrange("p (h d) -> p h d", h=HPC),
                                             in0=sp_[:, 0:P].rearrange("p (h d) -> p h d", h=HPC), scalar=rst[:, c:c + 1],
                                             in1=bsel[:, :].unsqueeze(2).to_broadcast([P, HPC, LD]),
                                             op0=ALU.mult, op1=ALU.mult).then_inc(small_free, 1)
                for i in range(TB):
                    n = TB * b + i
                    s = 2 * CC + 2 + i
                    o = small_wait(b, s)[:, 0:CC * (P + HPC)].rearrange("p (c m) -> p c m", c=CC)
                    rd = rden[:, i % 2, :].rearrange("p (c h) -> p c h", c=CC)
                    dve.reciprocal(rd, o[:, :, P:P + HPC]).then_inc(rden_ready, 1)
                    if i >= 1:
                        moments(b, 0, i - 1)
                    dve.wait_ge(rden_ready, n + 1)
                    dve.tensor_tensor(K[:, i, :].rearrange("p (c h d) -> p c h d", c=CC, h=HPC),
                                      o[:, :, 0:P].rearrange("p c (h d) -> p c h d", h=HPC),
                                      rd.unsqueeze(3).to_broadcast([P, CC, HPC, LD]), ALU.mult).then_inc(small_free, 1)
                    if i >= 2:
                        norm(b, 0, i - 2, K[:, i - 2, :], z_ready)
                    dve.wait_ge(small_free, SMALL_SETUP + SMALL_BATCH * b + s + 1)
                    sums(i, K[:, i, :])
                norm(b, 0, TB - 2, K[:, TB - 2, :], z_ready)
                moments(b, 0, TB - 1)
                for i in range(TB):
                    if i == 2:
                        scale(b, 2)
                    if i == 5:
                        split_low(b, 2)
                    y = small_wait(b, 2 * CC + 2 + TB + i)
                    dve.wait_ge(xc_ready, TB * b + i + 1)
                    dve.tensor_tensor(V[:, i, :, 0:P], y[:, 0:C].rearrange("p (c d) -> p c d", c=CC),
                                      X[:, i, :].rearrange("p (c d) -> p c d", c=CC), ALU.add).then_inc(small_free, 1)
                    if i == 0:
                        norm(b, 0, TB - 1, K[:, TB - 1, :], z_ready)
                    else:
                        moments(b, 1, i - 1)
                    if i >= 2:
                        norm(b, 1, i - 2, V[:, i - 2, :, 0:P], x1_ready)
                    dve.wait_ge(small_free, SMALL_SETUP + SMALL_BATCH * b + 2 * CC + 2 + TB + i + 1)
                    sums(i, V[:, i, :, 0:P])
                norm(b, 1, TB - 2, V[:, TB - 2, :, 0:P], x1_ready)
                moments(b, 1, TB - 1)
                for i in range(TB + 3):
                    j = i - 3
                    if i == 3:
                        scale(b, 3)
                    if i == 6:
                        split_low(b, 3)
                    if i < TB:
                        n = TB * b + i
                        lg = big[i % 2][:, LOGIT0:LOGIT0 + XH * KEYS].rearrange("p (h k) -> p h k", h=XH)
                        dve.wait_ge(lg_ready, n + 1)
                        dve.tensor_reduce(xm[:, i % 2, :], lg, AX_X, ALU.max).then_inc(xm_ready, 1)
                    if i == 0:
                        norm(b, 1, TB - 1, V[:, TB - 1, :, 0:P], x1_ready)
                    if j >= 0:
                        o = small_wait(b, 2 * CC + 2 + 2 * TB + j)[:, 0:XH * (XD + 1)].rearrange("p (h m) -> p h m", h=XH)
                        dve.reciprocal(xr8[:, j % 2, :].unsqueeze(2), o[:, :, XD:XD + 1]).then_inc(xr8_ready, 1)
                    if i < TB:
                        dve.wait_ge(xm_ready, n + 1)
                        dve.tensor_scalar(xmb[:, i % 2, :], xm[:, i % 2, :], bcol[:, 0:1], None, ALU.add).then_inc(xmb_ready, 1)
                    if j >= 0:
                        dve.wait_ge(xr8_ready, TB * b + j + 1)
                        dve.tensor_tensor(Q[:, j, :].rearrange("p (h d) -> p h d", h=XH), o[:, :, 0:XD],
                                          xr8[:, j % 2, :].unsqueeze(2).to_broadcast([P, XH, XD]), ALU.mult).then_inc(small_free, 1)
                    if i < TB:
                        dve.wait_ge(xmb_ready, n + 1)
                        dve.scalar_tensor_tensor(out=pr[:, i % 2, :, :], in0=lg, scalar=bcol[:, 0:1],
                                                 in1=xmb[:, i % 2, :].unsqueeze(2).to_broadcast([P, XH, KEYS]),
                                                 op0=ALU.add, op1=ALU.subtract).then_inc(s_ready, 1)
                    if j >= 1:
                        dve.wait_ge(r2_ready, TB * b + j)
                        sums(j - 1, Q[:, j - 1, :])
                    if j >= 2:
                        norm(b, 2, j - 2, Q[:, j - 2, :], x2_ready)
                    if j >= 1:
                        moments(b, 2, j - 1)
                dve.wait_ge(r2_ready, TB * b + TB)
                sums(TB - 1, Q[:, TB - 1, :])
                norm(b, 2, TB - 2, Q[:, TB - 2, :], x2_ready)
                moments(b, 2, TB - 1)
                take_router(b, 0)
                norm(b, 2, TB - 1, Q[:, TB - 1, :], x2_ready)
                take_router(b, 1)
                for i in range(2, TB):
                    take_router(b, i)
                    if i == HT - 1:
                        choose(b, 0)
                    if i == HT + 1:
                        gates(b, 0)
                choose(b, 1)
                gates(b, 1)

        @block.tensor
        def _(pe):
            pe.wait_ge(consts, IDENT_MADE)
            pe.wait_ge(setup_loaded, 16 * 4)
            for w in range(4):
                for o in range(CC):
                    use = w * CC + o
                    if use >= 2:
                        pe.wait_ge(trans_copied, use - 1)
                    for c in range(CC):
                        ins = pe.transpose(trans[use % 2][:, c, :], w_nat[:, w, o, c * P:(c + 1) * P], ident[:, :])
                    ins.then_inc(trans_ready, 1)
            pe.wait_ge(trans_copied, TRANS_SETUP)
            pe.wait_ge(lnbb_ready, CC)
            for half in range(CC):
                for c in range(CC):
                    ins = pe.matmul(small[half][:, 0:P], kdiag[:, c, :], woT[:, c, half * P:(half + 1) * P],
                                    start=(c == 0), stop=(c == CC - 1))
                ins.then_inc(small_ready, 1)
            pe.wait_ge(consts, CONST_STEPS)

            with pe.Fori(0, B) as b:
                def trans_stage(stage, i, src):
                    s = trans_use(stage, i)
                    pe.wait_ge(trans_copied, TRANS_SETUP + TRANS_BATCH * b + s - 1)
                    for c in range(CC):
                        ins = pe.transpose(trans[s % 2][:, c, :], src(c), ident[:, :])
                    ins.then_inc(trans_ready, 1)

                def copied(stage, i):
                    pe.wait_ge(trans_copied, TRANS_SETUP + TRANS_BATCH * b + trans_use(stage, i) + 1)
                    return tT[:, i % 2, :, :]

                def small_slot(s):
                    pe.wait_ge(small_free, SMALL_SETUP + SMALL_BATCH * b + s - 1)
                    return small[(SMALL_SETUP + s) % 2]

                pe.wait_ge(ctx_loaded, 16 * b + 16)
                for c in range(CC):
                    pe.transpose(small_slot(c)[:, 0:KEYS], ctx_sb[:, c * P:(c + 1) * P], ident[0:KEYS, 0:KEYS]).then_inc(small_ready, 1)
                pe.wait_ge(x_loaded, 16 * b + 16)
                for i in range(TB + 1):
                    if i < TB:
                        trans_stage(0, i, lambda c: X[:, i, c * P:(c + 1) * P])
                    if i >= 1:
                        j = i - 1
                        xT = copied(0, j)
                        if j >= 2:
                            pe.wait_ge(v_ready, TB * b + j - 1)
                        for c in range(CC):
                            pe.matmul(big[j % 2][:, 0:2 * C], xT[:, c, :], wqkv[:, c, 0:2 * C], start=(c == 0), stop=(c == CC - 1))
                        for c in range(CC):
                            ins = pe.matmul(big[j % 2][:, 2 * C:3 * C], xT[:, c, :], wqkv[:, c, 2 * C:3 * C], start=(c == 0), stop=(c == CC - 1))
                        ins.then_inc(qkv_ready, 1)
                pe.wait_ge(kmx_ready, TB * b + TB)
                km = small_slot(CC)
                for c in range(CC):
                    ins = pe.transpose(km[:, c * P:(c + 1) * P], kmx[:, c * P:(c + 1) * P], ident[:, :])
                ins.then_inc(small_ready, 1)
                pe.wait_ge(kdiag_ready, CC * b + CC)
                pe.matmul(small_slot(CC + 1)[:, 0:C], ones[:, :], kdiag[:, :, :].rearrange("p c t -> p (c t)"),
                          start=True, stop=True).then_inc(small_ready, 1)
                pe.wait_ge(v_ready, TB * b + TB)
                for c in range(CC):
                    dst = small_slot(CC + 2 + c)
                    for i in range(TB):
                        if c == 0 and i % (TB // KG) == 0:
                            pe.wait_ge(ke_ready, KG * b + i * KG // TB + 1)
                        ins = pe.matmul(dst[:, 0:P + 1], K[:, i, c * P:(c + 1) * P], V[:, i, c, :], start=(i == 0), stop=(i == TB - 1))
                    ins.then_inc(small_ready, 1)
                for i in range(TB + 1):
                    if i < TB:
                        pe.wait_ge(qe_ready, TB * b + i + 1)
                        trans_stage(1, i, lambda c: Q[:, i, c * P:(c + 1) * P])
                    if i >= 1:
                        j = i - 1
                        qT = copied(1, j)
                        if j == 0:
                            pe.wait_ge(small_free, SMALL_SETUP + SMALL_BATCH * b + 2 * CC + 2)
                        dst = small_slot(2 * CC + 2 + j)
                        for c in range(CC):
                            ins = pe.matmul(dst[:, c * (P + HPC):(c + 1) * (P + HPC)], qT[:, c, :], state[:, c, :], start=True, stop=True)
                        ins.then_inc(small_ready, 1)
                for i in range(TB + 1):
                    if i < TB:
                        pe.wait_ge(z_ready, TB * b + i + 1)
                        trans_stage(2, i, lambda c: K[:, i, c * P:(c + 1) * P])
                    if i >= 1:
                        j = i - 1
                        zT = copied(2, j)
                        if j == 0:
                            pe.wait_ge(woT_ready, CC)
                        dst = small_slot(2 * CC + 2 + TB + j)
                        for c in range(CC):
                            ins = pe.matmul(dst[:, 0:C], zT[:, c, :], woT[:, c, :], start=(c == 0), stop=(c == CC - 1))
                        ins.then_inc(small_ready, 1)
                pe.wait_ge(small_free, SMALL_SETUP + SMALL_BATCH * b + CC)
                pe.wait_ge(mask_ready, b + 1)
                pe.wait_ge(vx_loaded, 16 * len(SEGMENTS) * (b + 1))
                for i in range(TB + 4):
                    if i < TB:
                        pe.wait_ge(x1_ready, TB * b + i + 1)
                        trans_stage(3, i, lambda c: V[:, i, c, 0:P])
                    j = i - 3
                    if 0 <= j < TB:
                        pe.wait_ge(p_ready, TB * b + j + 1)
                        flat = pr[:, j % 2, :, :].rearrange("p h k -> p (h k)")
                        for part, chunks in (("pa", range(4)), ("pb", range(4, FCH))):
                            s = 3 * TB + CROSS[part, j]
                            pe.wait_ge(trans_copied, TRANS_SETUP + TRANS_BATCH * b + s - 1)
                            for c in chunks:
                                n = min(P, FLAT - c * P)
                                ins = pe.transpose(trans[s % 2][0:n, c % 4, :], flat[:, c * P:c * P + n], ident[:, :])
                            ins.then_inc(trans_ready, 1)
                    j = i - 1
                    if 0 <= j < TB:
                        x1T = copied(3, j)
                        if j >= 2:
                            pe.wait_ge(s_ready, TB * b + j - 1)
                        for c in range(CC):
                            dst = big[j % 2][:, LOGIT0 + c * XPC * KEYS:LOGIT0 + (c + 1) * XPC * KEYS]
                            pe.matmul(dst, x1T[:, c, :], kbd[:, c, :, :].rearrange("p h k -> p (h k)"), start=True, stop=False)
                            ins = pe.matmul(dst, one16[:, :], mbf[:, :, :].rearrange("p h k -> p (h k)"), start=False, stop=True)
                        ins.then_inc(lg_ready, 1)
                    j = i - 4
                    if 0 <= j < TB:
                        pe.wait_ge(trans_copied, TRANS_SETUP + TRANS_BATCH * b + 3 * TB + CROSS["pb", j] + 1)
                        dst = small_slot(2 * CC + 2 + 2 * TB + j)
                        for c, (h0, h1) in enumerate(SPAN):
                            n = min(P, FLAT - c * P)
                            ins = pe.matmul(dst[:, h0 * (XD + 1):h1 * (XD + 1)], pT[0:n, j % 2, c, :],
                                            vx[0:n, c, 0:h1 - h0, :].rearrange("p h d -> p (h d)"),
                                            start=(c == 0), stop=(c == FCH - 1), skip_group_check=True)
                        ins.then_inc(small_ready, 1)
                for i in range(TB + 1):
                    if i < TB:
                        pe.wait_ge(x2_ready, TB * b + i + 1)
                        trans_stage(4, i, lambda c: Q[:, i, c * P:(c + 1) * P])
                    if i >= 1:
                        j = i - 1
                        x2T = copied(4, j)
                        dst = small_slot(2 * CC + 2 + 3 * TB + j)
                        for c in range(CC):
                            ins = pe.matmul(dst[:, 0:EXP], x2T[:, c, :], rw[:, c, :], start=(c == 0), stop=(c == CC - 1))
                        ins.then_inc(small_ready, 1)


def routing(nc, k):
    st = ExitStack()
    with st:
        def sb(name, shape, dt=F32):
            return st.enter_context(nc.sbuf_tensor(name, shape, dt))

        def sem(name):
            return st.enter_context(nc.semaphore(name))

        PER = N * B // SLOTS
        HALF = NT // 2
        rank, ones, ident = k["rank"], k["ones"], k["ident"]
        values = sb("values", [P, EBLOCKS, NT], F16)
        lo_is = sb("lo_is", [P, P, NT], F16)
        lo_hot = sb("lo_hot", [P, 2, P, NT], F16)
        hi_hot = sb("hi_hot", [P, 2, EBLOCKS, NT], F16)
        chosen = sb("chosen", [P, EXP, NT])
        before = sb("before", [P, P])
        reset = sb("reset", [P, EXP, NT])
        incl = sb("incl", [P, EXP, NT])
        pos = sb("pos", [P, EXP, NT])
        picked = sb("picked", [P, NT, EXP])
        steps256 = sb("steps256", [P, PER])
        cmpt = sb("cmpt", [P, EXP, PER])
        tiles = sb("tiles", [P, EXP])
        endt = sb("endt", [P, EXP])
        start = sb("start", [P, EXP])
        posk = sb("posk", [P, TOPK, NT])
        posi = sb("posi", [P, TOPK, NT], I32)
        hii = sb("hii", [P, TOPK, NT], I32)
        loi = sb("loi", [P, TOPK, NT], I32)
        hif = sb("hif", [P, TOPK, NT], F16)
        lof = sb("lof", [P, TOPK, NT], F16)
        io = sb("io", [P, EBLOCKS], I32)
        iof = sb("iof", [P, EBLOCKS])
        vali = sb("vali", [P, 2, HALF], I32)
        val = sb("val", [P, NT], F16)
        padi = sb("padi", [P, EBLOCKS], I32)
        pad = sb("pad", [P, EBLOCKS])
        late = sb("late", [P, EBLOCKS])
        token = sb("token", [P, EBLOCKS])
        empty = sb("empty", [P, EBLOCKS])
        te = sb("te", [P, ETILES])
        past = sb("past", [P, ETILES, EXP + 1])
        hot = sb("hot", [P, ETILES, EXP])
        inv = sb("inv", [P, 2 * EXP])
        fac = sb("fac", [P, 3, EXP])
        tmp = sb("tmp", [P, ETILES, EXP])
        sum4 = sb("sum4", [P, ETILES, EXP // 2])
        sum2 = sb("sum2", [P, ETILES, EXP // 4])
        counts = st.enter_context(nc.psum_tensor("counts", [P, 512], F32))
        table = [st.enter_context(nc.psum_tensor(f"table{i}", [P, 512], F32)) for i in range(2)]

        made, dve_step, chosen_ready, counts_ready = sem("made"), sem("dve_step"), sem("chosen_ready"), sem("counts_ready")
        is_ready, hot_ready, table_step = sem("is_ready"), sem("hot_ready"), sem("table_step")
        values_ready, past_ready, fac_ready, pool_step = sem("values_ready"), sem("past_ready"), sem("fac_ready"), sem("by_tile_step")
        block = st.enter_context(nc.Block())
        MADE_FIRST, MADE = 6, 12

        @block.gpsimd
        def _(pool):
            n = [0]

            def done(ins):
                n[0] += 1
                ins.then_inc(made, 1)
                pool.wait_ge(made, n[0])

            done(pool.memset(before[:, :], 1.0))
            done(pool.affine_select(out=before[:, :], in_=before[:, :], compare_op=ALU.is_gt, fill=0.0,
                                    base=0, pattern=[[1, P]], channel_multiplier=-1))
            done(pool.iota(io[:, :], pattern=[[1, EBLOCKS]], base=0, channel_multiplier=0))
            done(pool.tensor_copy(iof[:, :], io[:, :]))
            done(pool.memset(reset[:, :, :], 1.0))
            done(pool.memset(reset[:, :, 0:1], 0.0))
            assert n[0] == MADE_FIRST
            done(pool.iota(vali[:, :, :], pattern=[[0, 2], [P, HALF]], base=1, channel_multiplier=1))
            done(pool.tensor_copy(val[:, :], vali[:, :, :].rearrange("p h t -> p (h t)")))
            done(pool.memset(past[:, :, 0:1], 1.0))
            done(pool.memset(past[:, :, EXP:EXP + 1], 0.0))
            done(pool.iota(padi[:, :].rearrange("p (t j) -> p t j", j=SB), pattern=[[0, ETILES], [P, SB]],
                           base=B * N + 1, channel_multiplier=1))
            done(pool.tensor_copy(pad[:, :], padi[:, :]))
            assert n[0] == MADE

            m = [0]

            def then(ins):
                m[0] += 1
                ins.then_inc(pool_step, 1)
                pool.wait_ge(pool_step, m[0])

            def sum_experts(dst, of):
                then(pool.tensor_tensor(sum4[:, :, :], of[:, :, 0:4], of[:, :, 4:8], ALU.add))
                then(pool.tensor_tensor(sum2[:, :, :], sum4[:, :, 0:2], sum4[:, :, 2:4], ALU.add))
                then(pool.tensor_tensor(dst, sum2[:, :, 0], sum2[:, :, 1], ALU.add))

            pool.wait_ge(past_ready, 1)
            sum_experts(te[:, :], past[:, :, 1:EXP + 1])
            then(pool.tensor_copy(k["tile_expert"][:, :], te[:, :]))
            then(pool.tensor_tensor(hot[:, :, :], past[:, :, 0:EXP], past[:, :, 1:EXP + 1], ALU.subtract))
            pool.wait_ge(fac_ready, 1)
            for f, dst in ((0, k["up_scale"]), (1, k["h_scale"])):
                then(pool.tensor_tensor(tmp[:, :, :], hot[:, :, :], fac[:, f, :].unsqueeze(1).to_broadcast([P, ETILES, EXP]), ALU.mult))
                sum_experts(dst[:, :], tmp)
            then(pool.tensor_tensor(k["pick"][:, :, :], hot[:, :, :], fac[:, 2, :].unsqueeze(1).to_broadcast([P, ETILES, EXP]), ALU.mult))

        @block.scalar
        def _(act):
            for half in range(HALVES):
                act.wait_ge(k["acc_stored"][half], 16 * (B + 1))
                act.wait_ge(k["rows_stored"][half], 16 * (B + 1))
            act.wait_ge(made, MADE_FIRST)
            act.activation(values[:, :, :], iof[:, :].unsqueeze(2).to_broadcast([P, EBLOCKS, NT]), ACT.Copy).then_inc(values_ready, 1)

        @block.vector
        def _(dve):
            n = [0]

            def done(ins):
                n[0] += 1
                ins.then_inc(dve_step, 1)
                dve.wait_ge(dve_step, n[0])

            dve.tensor_scalar(chosen[:, :, :], rank[:, :, :], float(TOPK), None, ALU.is_lt).then_inc(chosen_ready, 1)
            dve.wait_ge(made, MADE_FIRST)
            dve.tensor_copy(k["ident16"][:, :], ident[:, :])
            done(dve.tensor_scalar(steps256[:, :], iof[:, 0:PER], float(SLOTS), None, ALU.mult))
            done(dve.reciprocal(inv[:, :], k["wpow"][:, :]))
            wp = k["wpow"][:, :].rearrange("p (e m) -> p e m", m=2)
            iv = inv[:, :].rearrange("p (e m) -> p e m", m=2)
            done(dve.tensor_scalar(fac[:, 0, :], wp[:, :, 0], 1.0 / (XSCALE * WTARGET), None, ALU.mult))
            done(dve.tensor_scalar(fac[:, 1, :], iv[:, :, 0], HTARGET, None, ALU.mult))
            dve.scalar_tensor_tensor(out=fac[:, 2, :], in0=wp[:, :, 0], scalar=1.0 / (HTARGET * WTARGET),
                                     in1=wp[:, :, 1], op0=ALU.mult, op1=ALU.mult).then_inc(fac_ready, 1)
            dve.wait_ge(counts_ready, 1)
            prefix = counts[:, 0:EXP * NT]
            total = counts[:, EXP * NT:2 * EXP * NT]
            flat = lambda t: t[:, :, :].rearrange("p e t -> p (e t)")
            done(dve.tensor_tensor_scan(flat(incl), flat(reset), total, 0.0, ALU.mult, ALU.add))
            done(dve.tensor_tensor(cmpt[:, :, :], incl[:, :, NT - 1:NT].to_broadcast([P, EXP, PER]),
                                   steps256[:, :].unsqueeze(1).to_broadcast([P, EXP, PER]), ALU.is_gt))
            done(dve.tensor_reduce(tiles[:, :], cmpt[:, :, :], AX_X, ALU.add))
            done(dve.tensor_tensor_scan(endt[:, :], ones[:, 0:EXP], tiles[:, :], 0.0, ALU.mult, ALU.add))
            dve.tensor_tensor(past[:, :, 1:EXP], iof[:, 0:ETILES].unsqueeze(2).to_broadcast([P, ETILES, EXP - 1]),
                              endt[:, 0:EXP - 1].unsqueeze(1).to_broadcast([P, ETILES, EXP - 1]), ALU.is_ge).then_inc(past_ready, 1)
            done(dve.tensor_tensor(start[:, :], endt[:, :], tiles[:, :], ALU.subtract))
            done(dve.tensor_tensor(flat(pos), flat(incl), total, ALU.subtract))
            done(dve.tensor_tensor(flat(pos), flat(pos), prefix, ALU.add))
            done(dve.tensor_scalar(start[:, :], start[:, :], float(SLOTS), None, ALU.mult))
            done(dve.tensor_tensor(pos[:, :, :], pos[:, :, :], start[:, :].unsqueeze(2).to_broadcast([P, EXP, NT]), ALU.add))
            for j in range(TOPK):
                done(dve.scalar_tensor_tensor(out=picked[:, :, :].rearrange("p t e -> p e t"), in0=rank[:, :, :], scalar=float(j),
                                              in1=pos[:, :, :], op0=ALU.is_equal, op1=ALU.mult))
                done(dve.tensor_reduce(posk[:, j, :], picked[:, :, :], AX_X, ALU.add))
            done(dve.tensor_copy(posi[:, :, :], posk[:, :, :]))
            done(dve.tensor_scalar(hii[:, :, :], posi[:, :, :], 7, None, ALU.logical_shift_right))
            done(dve.tensor_scalar(loi[:, :, :], posi[:, :, :], P - 1, None, ALU.bitwise_and))
            done(dve.tensor_copy(hif[:, :, :], hii[:, :, :]))
            done(dve.tensor_copy(lof[:, :, :], loi[:, :, :]))
            dve.wait_ge(values_ready, 1)
            dve.wait_ge(made, MADE)
            for j in range(TOPK):
                if j >= 1:
                    dve.wait_ge(hot_ready, 2 * j)
                if j >= 2:
                    dve.wait_ge(table_step, j - 1)
                dve.tensor_tensor(lo_is[:, :, :], values[:, 0:P, :], lof[:, j, :].unsqueeze(1).to_broadcast([P, P, NT]),
                                  ALU.is_equal).then_inc(is_ready, 1)
                dve.tensor_tensor(hi_hot[:, j % 2, :, :], values[:, :, :], hif[:, j, :].unsqueeze(1).to_broadcast([P, EBLOCKS, NT]),
                                  ALU.is_equal).then_inc(hot_ready, 1)
                dve.wait_ge(is_ready, j + 1)
                dve.tensor_tensor(lo_hot[:, j % 2, :, :], lo_is[:, :, :], val[:, :].unsqueeze(1).to_broadcast([P, P, NT]),
                                  ALU.mult).then_inc(hot_ready, 1)
            dve.wait_ge(table_step, TOPK)
            done(dve.tensor_scalar(late[:, :], table[1][:, 0:EBLOCKS], 0.0, float(HALF * P), ALU.is_gt, ALU.mult))
            done(dve.tensor_tensor(late[:, :], table[1][:, 0:EBLOCKS], late[:, :], ALU.add))
            done(dve.tensor_tensor(token[:, :], table[0][:, 0:EBLOCKS], late[:, :], ALU.add))
            done(dve.scalar_tensor_tensor(out=empty[:, :], in0=token[:, :], scalar=0.0, in1=pad[:, :], op0=ALU.is_equal, op1=ALU.mult))
            done(dve.scalar_tensor_tensor(out=k["slot_row"][:, :], in0=token[:, :], scalar=-1.0, in1=empty[:, :], op0=ALU.add, op1=ALU.add))

        @block.tensor
        def _(pe):
            pe.wait_ge(made, MADE_FIRST)
            pe.wait_ge(chosen_ready, 1)
            flat = chosen[:, :, :].rearrange("p e t -> p (e t)")
            pe.matmul(counts[:, 0:EXP * NT], before[:, :], flat, start=True, stop=True)
            pe.matmul(counts[:, EXP * NT:2 * EXP * NT], ones[:, :], flat, start=True, stop=True).then_inc(counts_ready, 1)
            for j in range(TOPK):
                pe.wait_ge(hot_ready, 2 * j + 2)
                for t in range(NT):
                    ins = pe.matmul(table[t // HALF][:, 0:EBLOCKS], lo_hot[:, j % 2, :, t], hi_hot[:, j % 2, :, t],
                                    start=(j == 0 and t % HALF == 0), stop=(j == TOPK - 1 and t % HALF == HALF - 1))
                ins.then_inc(table_step, 1)


def experts(nc, k, rows, acc):
    st = ExitStack()
    with st:
        def sb(name, shape, dt=F32):
            return st.enter_context(nc.sbuf_tensor(name, shape, dt))

        def ps(name, shape, dt=F32):
            return st.enter_context(nc.psum_tensor(name, shape, dt))

        def sem(name):
            return st.enter_context(nc.semaphore(name))

        xg = sb("xg", [P, 2, SB, ROW // 2])
        xT = sb("xT", [P, 2, 2 * CC, SLOTS], F16)
        h = sb("h", [P, PAIRS, 2 * SLOTS])
        hh = sb("hh", [P, 2, HC, SLOTS], F16)
        hl = sb("hl", [P, 2, HC, SLOTS], F16)
        y = sb("y", [P, 2, SB, C])
        gp = sb("gp", [P, 2, SB, EXP])
        gate = sb("gate", [P, ETILES * SB])
        psx = [ps(f"psx{i}", [P, 2 * CC, SLOTS], F16) for i in range(2)]
        psu = [ps(f"psu{i}", [P, 512]) for i in range(PAIRS)]
        psy = [ps(f"psy{i}", [P, SB, C]) for i in range(2)]
        warm = sb("warm", [P, 1])
        gather_rows = sb("gather_rows", [P, 2, SB], I32)
        add_rows = sb("add_rows", [P, 2, SB], I32)

        xg_loaded = [sem(f"xg_loaded{i}") for i in range(2)]
        y_added = [sem(f"y_added{i}") for i in range(2)]
        xt_ready, xt_copied, up_ready, gelu_ready = sem("xt_ready"), sem("xt_copied"), sem("up_ready"), sem("gelu_ready")
        hh_ready, hl_ready, down_ready, y_ready = sem("hh_ready"), sem("hl_ready"), sem("down_ready"), sem("y_ready")
        gather_rows_ready, add_rows_ready = sem("gather_rows_ready"), sem("add_rows_ready")
        gp_ready, gate_ready, table_loaded = sem("gp_ready"), sem("gate_ready"), sem("warm_ready")
        passed = {e: sem(f"tiles_passed_{i}") for i, e in enumerate((nc.gpsimd, nc.scalar))}
        block = st.enter_context(nc.Block())

        def lone(eng):
            eng.sem_inc(passed[eng], 1)

        @block.gpsimd
        def _(pool):
            def slot_rows(dst, t, ready):
                at = t * SB
                src = k["slot_row"][:, bass.ds(at, SB)] if not isinstance(at, int) else k["slot_row"][:, at:at + SB]
                lone(pool)
                pool.tensor_copy(dst, src).then_inc(ready, 1)
                pool.wait_ge(ready, t + 1)
                lone(pool)

            def gather(t, par):
                slot_rows(gather_rows[:, par, :], t, gather_rows_ready)
                for j in range(SB):
                    pool.indirect_dma_start(xg[:, par, j, :], None, rows,
                                            bass.IndirectOffsetOnAxis(ap=gather_rows[:, par, j:j + 1], axis=0)
                                            ).then_inc(xg_loaded[par], 16)

            def add(t, par):
                for j in range(SB):
                    pool.indirect_dma_start(acc, bass.IndirectOffsetOnAxis(ap=add_rows[:, par, j:j + 1], axis=0),
                                            y[:, par, j, :], None, compute_op=ALU.add).then_inc(y_added[par], 16)

            def step(t, par, half, prior):
                if prior:
                    pool.wait_ge(xt_ready, t - 1)
                    pool.wait_ge(gate_ready, t - 1)
                gather(t, par)

            def result(t, par, half, prior):
                pool.wait_ge(y_ready, SB * (t + 1))
                slot_rows(add_rows[:, par, :], t, add_rows_ready)
                if prior:
                    pool.wait_ge(y_added[1 - par], 16 * SB * (half + par))
                lone(pool)
                add(t, par)

            gather(0, 0)
            gather(1, 1)
            step(2, 0, 1, True)
            step(3, 1, 1, True)
            result(0, 0, 0, False)
            with pool.Fori(2, ETILES // 2) as u:
                for par in range(2):
                    step(2 * u + par, par, u, True)
                    result(2 * u + par - 3, 1 - par, u - 2 + par, True)
            for t in range(ETILES - ETILES % 2, ETILES):
                step(t, t % 2, t // 2, True)
            for t in range(2 * (ETILES // 2) - 3, ETILES):
                result(t, t % 2, t // 2, True)
            pool.wait_ge(y_added[0], 16 * SB * ((ETILES + 1) // 2))
            pool.wait_ge(y_added[1], 16 * SB * (ETILES // 2))

        @block.tensor
        def _(pe):
            def row_transposes(t, par, half, prior=True):
                pe.wait_ge(xg_loaded[par], 16 * SB * (half + 1))
                if prior:
                    pe.wait_ge(xt_copied, t - 1)
                for q in range(2 * CC):
                    for j in range(SB):
                        ins = pe.transpose(psx[par][:, q, j * P:(j + 1) * P], xg[:, par, j, q * P // 2:(q + 1) * P // 2].bitcast(F16), k["ident16"][:, :])
                ins.then_inc(xt_ready, 1)

            def up_products(t, par, half, e, prior=True):
                pe.wait_ge(xt_copied, t + 1)
                w = k["wu"][:, bass.ds(e, 1), :, :, :].rearrange("p e s c h -> p (e s) c h")
                for p in range(PAIRS):
                    if prior:
                        pe.wait_ge(gelu_ready, PAIRS * (t - 1) + (p + 1))
                    for i in range(2):
                        m = (2 * p + i) * P
                        n = 0
                        for c in range(CC):
                            for ws, xs in ((0, 0), (0, 1), (1, 0)):
                                ins = pe.matmul(psu[p][:, i * SLOTS:(i + 1) * SLOTS], w[:, ws, c, m:m + P], xT[:, par, xs * CC + c, :],
                                                start=(n == 0), stop=(n == 3 * CC - 1))
                                n += 1
                    ins.then_inc(up_ready, 1)

            def down_products(t, par, half, e, prior=True):
                pe.wait_ge(hl_ready, PAIRS * (t + 1))
                w = k["wd"][:, bass.ds(e, 1), :, :, :].rearrange("p e s c d -> p (e s) c d")
                for j in range(SB):
                    if prior and j == 0:
                        pe.wait_ge(y_ready, SB * (t - 1))
                    n = 0
                    for c in range(HC):
                        for hs, ws in ((0, 0), (0, 1), (1, 0)):
                            ins = pe.matmul(psy[par][:, j, :], (hh, hl)[hs][:, par, c, j * P:(j + 1) * P], w[:, ws, c, :],
                                            start=(n == 0), stop=(n == 3 * HC - 1))
                            n += 1
                    ins.then_inc(down_ready, 1)

            def expert_of(t):
                at = k["tile_expert"][0:1, bass.ds(t, 1)] if not isinstance(t, int) else k["tile_expert"][0:1, t:t + 1]
                return pe.value_load(at, min_val=0, max_val=EXP - 1)

            def turn(t, par, half, more=True, prior=True):
                up_products(t, par, half, expert_of(t))
                if more:
                    row_transposes(t + 1, 1 - par, half + par)
                down_products(t - 1, 1 - par, half, expert_of(t - 1), prior)

            row_transposes(0, 0, 0, False)
            up_products(0, 0, 0, expert_of(0), False)
            row_transposes(1, 1, 0, False)
            turn(1, 1, 0, prior=False)
            turn(2, 0, 1, prior=False)
            turn(3, 1, 1)
            with pe.Fori(2, (ETILES - 1) // 2) as u:
                for par in range(2):
                    turn(2 * u + par, par, u)
            last = ETILES - 1
            for t in range(2 * (last // 2), ETILES):
                turn(t, t % 2, t // 2, more=t + 1 < ETILES)
            down_products(last, last % 2, last // 2, expert_of(last))

        @block.scalar
        def _(act):
            act.activation(warm[:, :], k["nhalf"][:, 0:1], ACT.Gelu_apprx_tanh).then_inc(table_loaded, 1)

            def gelus(t, par, half, prior=True):
                sc = k["up_scale"][:, bass.ds(t, 1)] if not isinstance(t, int) else k["up_scale"][:, t:t + 1]
                for p in range(PAIRS):
                    act.wait_ge(up_ready, PAIRS * t + (p + 1))
                    if prior:
                        act.wait_ge(hl_ready, PAIRS * (t - 1) + (p + 1))
                    lone(act)
                    act.activation(h[:, p, :], psu[p][:, :], ACT.Gelu_apprx_tanh, scale=sc).then_inc(gelu_ready, 1)

            def results(t, par, half, prior=True):
                if prior:
                    act.wait_ge(y_added[par], 16 * SB * half)
                act.wait_ge(gate_ready, t + 1)
                act.wait_ge(down_ready, SB * (t + 1))
                lone(act)
                for j in range(SB):
                    g = t * SB + j
                    scale = gate[:, bass.ds(g, 1)] if not isinstance(g, int) else gate[:, g:g + 1]
                    act.activation(y[:, par, j, :], psy[par][:, j, :], ACT.Copy, scale=scale).then_inc(y_ready, 1)

            gelus(0, 0, 0, False)
            gelus(1, 1, 0)
            results(0, 0, 0, False)
            gelus(2, 0, 1)
            results(1, 1, 0, False)
            gelus(3, 1, 1)
            results(2, 0, 1)
            with act.Fori(2, ETILES // 2) as u:
                for par in range(2):
                    gelus(2 * u + par, par, u)
                    results(2 * u + par - 1, 1 - par, u - 1 + par)
            for t in range(2 * (ETILES // 2), ETILES):
                gelus(t, t % 2, t // 2)
                results(t - 1, 1 - t % 2, (t - 1) // 2)
            results(ETILES - 1, (ETILES - 1) % 2, (ETILES - 1) // 2)

        @block.vector
        def _(dve):
            def take_rows(t, par, prior=True):
                dve.wait_ge(xt_ready, t + 1)
                if prior:
                    dve.wait_ge(up_ready, PAIRS * (t - 1))
                dve.tensor_copy(xT[:, par, :, :], psx[par][:, :, :]).then_inc(xt_copied, 1)
                pick = k["pick"][:, bass.ds(t, 1), :] if not isinstance(t, int) else k["pick"][:, t:t + 1, :]
                dve.tensor_tensor(gp[:, par, :, :], xg[:, par, :, C:ROW // 2], pick.to_broadcast([P, SB, EXP]),
                                  ALU.mult).then_inc(gp_ready, 1)
                dve.wait_ge(gp_ready, t + 1)
                at = t * SB
                dst = gate[:, bass.ds(at, SB)] if not isinstance(at, int) else gate[:, at:at + SB]
                dve.tensor_reduce(dst, gp[:, par, :, :], AX_X, ALU.add).then_inc(gate_ready, 1)

            def halves(t, par, prior=True):
                sc = k["h_scale"][:, bass.ds(t, 1)] if not isinstance(t, int) else k["h_scale"][:, t:t + 1]
                if prior:
                    dve.wait_ge(down_ready, SB * (t - 1))
                for p in range(PAIRS):
                    hi = hh[:, par, 2 * p:2 * p + 2, :].rearrange("p c s -> p (c s)")
                    lo = hl[:, par, 2 * p:2 * p + 2, :].rearrange("p c s -> p (c s)")
                    dve.wait_ge(gelu_ready, PAIRS * t + (p + 1))
                    dve.tensor_scalar(hi, h[:, p, :], sc, None, ALU.mult).then_inc(hh_ready, 1)
                    dve.wait_ge(hh_ready, PAIRS * t + (p + 1))
                    dve.scalar_tensor_tensor(out=lo, in0=h[:, p, :], scalar=sc, in1=hi, op0=ALU.mult, op1=ALU.subtract).then_inc(hl_ready, 1)

            take_rows(0, 0, False)
            halves(0, 0, False)
            take_rows(1, 1, False)
            halves(1, 1, False)
            take_rows(2, 0)
            with dve.Fori(1, (ETILES - 1) // 2) as u:
                for par in range(2):
                    halves(2 * u + par, par)
                    take_rows(2 * u + par + 1, 1 - par)
            for t in range(2 * ((ETILES - 1) // 2), ETILES):
                halves(t, t % 2)
                if t + 1 < ETILES:
                    take_rows(t + 1, 1 - t % 2)


def last_norm(nc, k, acc, out):
    st = ExitStack()
    with st:
        def sem(name):
            return st.enter_context(nc.semaphore(name))

        G = 4
        GROUPS = NT // G
        s = st.enter_context(nc.sbuf_tensor("sums", [P, NT, C], F32))
        stat = st.enter_context(nc.sbuf_tensor("fstat", [P, 2, 6], F32))
        mv = st.enter_context(nc.sbuf_tensor("fmv", [P, NT, 2], F32))
        var = st.enter_context(nc.sbuf_tensor("fvar", [P, NT], F32))
        rstd = st.enter_context(nc.sbuf_tensor("frstd", [P, NT], F32))
        prod = st.enter_context(nc.sbuf_tensor("fprod", [P, NT], F32))
        shift = st.enter_context(nc.sbuf_tensor("fshift", [P, NT], F32))
        loaded = [sem(f"loaded{g}") for g in range(GROUPS)]
        stats_ready, mv_ready, var_ready, rstd_ready, prod_ready, shift_ready = (
            sem("fstats_ready"), sem("fmv_ready"), sem("fvar_ready"), sem("frstd_ready"), sem("fprod_ready"), sem("fshift_ready"))
        normed_v, normed_s, stored = sem("normed_by_vector"), sem("normed_by_scalar"), sem("stored")
        a = acc[0:B * N, :].rearrange("(t p) c -> p t c", p=P)
        o = out.rearrange("b (t p) c -> b p t c", p=P)
        block = st.enter_context(nc.Block())

        @block.sync
        def _(sp):
            for g in range(GROUPS):
                sp.dma_start(s[:, g * G:(g + 1) * G, :], a[:, g * G:(g + 1) * G, :]).then_inc(loaded[g], 16)
            for g in range(GROUPS):
                sp.wait_ge(normed_v, (g + 1) * G // 2)
                sp.wait_ge(normed_s, (g + 1) * G // 2)
                t = g * G % TB
                sp.dma_start(o[g * G // TB][:, t:t + G, :], s[:, g * G:(g + 1) * G, :]).then_inc(stored, 16)
            sp.wait_ge(stored, 16 * GROUPS)

        @block.vector
        def _(dve):
            def norm_group(g):
                dve.wait_ge(rstd_ready, g + 1)
                for i in range(g * G, g * G + G // 2):
                    dve.tensor_scalar(s[:, i, :], s[:, i, :], mv[:, i, 0:1], rstd[:, i:i + 1], ALU.subtract, ALU.mult).then_inc(normed_v, 1)

            for t in range(NT + 1):
                if t < NT:
                    if t % G == 0:
                        dve.wait_ge(loaded[t // G], 16)
                    if t >= 2:
                        dve.wait_ge(mv_ready, t - 1)
                    dve.bn_stats(stat[:, t % 2, :], s[:, t, :]).then_inc(stats_ready, 1)
                if t >= 1:
                    dve.wait_ge(stats_ready, t)
                    dve.bn_aggr(mv[:, t - 1, :], stat[:, (t - 1) % 2, :]).then_inc(mv_ready, 1)
                if t >= G + 2 and t % G == 2:
                    norm_group(t // G - 1)
            norm_group(GROUPS - 1)

        @block.gpsimd
        def _(pool):
            for g in range(GROUPS):
                at = slice(g * G, (g + 1) * G)
                pool.wait_ge(mv_ready, (g + 1) * G)
                pool.tensor_scalar(var[:, at], mv[:, at, 1], LN_EPS, None, ALU.add).then_inc(var_ready, 1)
                pool.wait_ge(var_ready, g + 1)
                pool.tensor_tensor(rstd[:, at], var[:, at], k["nhalf"][:, 0:G], ALU.pow).then_inc(rstd_ready, 1)
                pool.wait_ge(rstd_ready, g + 1)
                pool.tensor_tensor(prod[:, at], mv[:, at, 0], rstd[:, at], ALU.mult).then_inc(prod_ready, 1)
                pool.wait_ge(prod_ready, g + 1)
                pool.tensor_scalar(shift[:, at], prod[:, at], -1.0, None, ALU.mult).then_inc(shift_ready, 1)

        @block.scalar
        def _(act):
            for g in range(GROUPS):
                act.wait_ge(shift_ready, g + 1)
                for i in range(g * G + G // 2, (g + 1) * G):
                    act.activation(s[:, i, :], s[:, i, :], ACT.Identity, scale=rstd[:, i:i + 1], bias=shift[:, i:i + 1]).then_inc(normed_s, 1)


_INS = ["x", "ctx_2048", "mask_BxS2_ik0", "L0_attn_Wq", "L0_attn_bq", "L0_attn_Wk", "L0_attn_bk", "L0_attn_Wv",
        "L0_attn_bv", "L0_attn_Wo", "L0_attn_bo", "L0_attn_ln_g", "L0_attn_ln_b", "L0_xattn_b", "L0_ffn_router_w",
        "L0_ffn_up_w", "L0_ffn_down_w"]
_OUTS = [((B, N, C), "float32")]


def kernel(**inputs):
    import numpy as _np
    import concourse.bacc as _bacc
    from concourse import mybir as _mybir
    from concourse.bass_utils import run_bass_kernel_spmd as _run

    nc = _bacc.Bacc("TRN2", target_bir_lowering=False, num_devices=1)
    arrays, args = {}, []
    for name in _INS:
        a = _np.ascontiguousarray(inputs[name])
        arrays[f"in_{name}_dram"] = a
        args.append(nc.dram_tensor(f"in_{name}_dram", a.shape, _mybir.dt.from_np(a.dtype), kind="ExternalInput").ap())
    for i, (shape, dtype) in enumerate(_OUTS):
        dt = _mybir.dt.from_np(_np.dtype(dtype))
        args.append(nc.dram_tensor(f"out_{i}_dram", shape, dt, kind="ExternalOutput").ap())
    layer_kernel(nc, *args)
    r = _run(nc, [arrays], core_ids=[0])
    return r.results[0]["out_0_dram"]
```
